# Optimizing a Trainium2 kernel written in Bass

```python
import numpy as np
import jax
import jax.numpy as jnp

def _softmax(x, axis=-1):
    return jax.nn.softmax(x, axis=axis)

def _gelu(x):
    return jax.nn.gelu(x, approximate=True)

def _silu(x):
    return jax.nn.silu(x)

def _sigmoid(x):
    return jax.nn.sigmoid(x)

def _layernorm(x, axis=-1, eps=1e-05):
    m = jnp.mean(x, axis=axis, keepdims=True)
    v = jnp.var(x, axis=axis, keepdims=True)
    return (x - m) / jnp.sqrt(v + eps)

def _scatter_add(tgt, idx, src, axis=0):
    return tgt.at[idx].add(src)

def _segment_sum(src, seg, n):
    return jax.ops.segment_sum(src, seg, n)
kernel_name = 'mk_decoder_preln_d1_seqx_r8_f1b4e3'

def setup_inputs(seed: int=0):
    np.random.seed(seed)
    _w = jnp.asarray

    def _rec_inputs():
        import jax
        import jax.numpy as jnp
        _rk = jax.random.key(seed)
        x = 7.22e-05 + 1 * jax.random.normal(jax.random.fold_in(_rk, 1), (32, 128, 128), jnp.float32)
        _lenS = 128 - jax.random.randint(jax.random.fold_in(_rk, 7), (32,), 0, max(1, 128 // 4) + 1, jnp.int32)
        _lenS2 = 128 - jax.random.randint(jax.random.fold_in(_rk, 8), (32,), 0, max(1, 128 // 4) + 1, jnp.int32)
        _ctx_1024P = jax.random.normal(jax.random.fold_in(_rk, 11), (32, 16, 128), jnp.float32)
        _ctx_1024c = jax.random.dirichlet(jax.random.fold_in(_rk, 511), 0.3 * jnp.ones((16,), jnp.float32), (32, 128))
        _ctx_1024t = jnp.einsum('bsk,bkd->bsd', _ctx_1024c, _ctx_1024P)
        _ctx_1024t = _ctx_1024t * jax.lax.rsqrt(jnp.mean(jnp.square(_ctx_1024t)) + 1e-12) * 0.953939
        ctx_1024 = 4.13588e-05 + 0.999923 * (_ctx_1024t + 0.3 * jax.random.normal(jax.random.fold_in(_rk, 611), (32, 128, 128), jnp.float32))
        return (x, ctx_1024)
    x, ctx_1024 = _rec_inputs()

    def _L0_attn_setup():
        import jax, jax.numpy as jnp
        import numpy as np
        EMBED_DIM = 128
        SEQ_LEN = 256
        BATCH = 4
        TOPK = 32
        key = jax.random.key(seed)
        ks = jax.random.split(key, 9)
        E = EMBED_DIM
        w = lambda k: jax.random.normal(k, (E, E), dtype=jnp.float32) * 0.02
        return {'x': jax.random.normal(ks[0], (BATCH, SEQ_LEN, E), dtype=jnp.float32), 'Wq': w(ks[1]), 'bq': jnp.zeros((E,), jnp.float32), 'Wk': w(ks[2]), 'bk': jnp.zeros((E,), jnp.float32), 'Wv': w(ks[3]), 'bv': jnp.zeros((E,), jnp.float32), 'Wo': w(ks[4]), 'bo': jnp.zeros((E,), jnp.float32)}
    _L0_attn_all = _L0_attn_setup()
    _L0_attn_in = {k: v for k, v in _L0_attn_all.items() if k in ('Wq', 'bq', 'Wk', 'bk', 'Wv', 'bv', 'Wo', 'bo')}
    del _L0_attn_all

    def _L0_xattn_setup():
        import jax, jax.numpy as jnp
        import numpy as np
        D = 128
        H = 16
        HD = D // H
        key = jax.random.key(seed)
        ks = jax.random.split(key, 9)
        B, S = (4, 256)
        s = 1.0 / np.sqrt(D)
        return {'query': jax.random.normal(ks[0], (B, S, D), jnp.float32), 'key': jax.random.normal(ks[1], (B, S, D), jnp.float32), 'value': jax.random.normal(ks[2], (B, S, D), jnp.float32), 'Wq': jax.random.normal(ks[3], (D, D), jnp.float32) * s, 'bq': jax.random.normal(ks[4], (D,), jnp.float32) * s, 'Wk': jax.random.normal(ks[5], (D, D), jnp.float32) * s, 'bk': jax.random.normal(ks[6], (D,), jnp.float32) * s, 'Wv': jax.random.normal(ks[7], (D, D), jnp.float32) * s, 'bv': jax.random.normal(ks[8], (D,), jnp.float32) * s}
    _L0_xattn_all = _L0_xattn_setup()
    _L0_xattn_in = {k: v for k, v in _L0_xattn_all.items() if k in ('Wq', 'bq', 'Wk', 'bk', 'Wv', 'bv')}
    del _L0_xattn_all

    def _L0_ffn_setup():
        import jax, jax.numpy as jnp
        import numpy as np
        E = 8
        EPS = 1e-05
        key = jax.random.key(seed)
        ks = jax.random.split(key, 6)
        d, f = (128, 512)
        B, S = (2, 128)
        x = jax.random.normal(ks[0], (B, S, d), dtype=jnp.float32)
        c = jax.random.normal(ks[1], (d, E), dtype=jnp.float32)
        q, _ = jnp.linalg.qr(c)
        centroids = (0.1 * q.T).astype(jnp.float32)
        w1 = jax.random.normal(ks[2], (E, d, f), dtype=jnp.float32) / np.sqrt(d).astype(np.float32)
        b1 = jnp.zeros((E, f), dtype=jnp.float32)
        w2 = jax.random.normal(ks[3], (E, f, d), dtype=jnp.float32) * 0.02
        b2 = jnp.zeros((E, d), dtype=jnp.float32)
        gamma = jnp.ones((E, d), dtype=jnp.float32)
        beta = jnp.zeros((E, d), dtype=jnp.float32)
        return dict(x=x, centroids=centroids, w1=w1, b1=b1, w2=w2, b2=b2, gamma=gamma, beta=beta)
    _L0_ffn_all = _L0_ffn_setup()
    _L0_ffn_in = {k: v for k, v in _L0_ffn_all.items() if k in ('centroids', 'w1', 'b1', 'w2', 'b2', 'gamma', 'beta')}
    del _L0_ffn_all
    return {'x': x, 'ctx_1024': ctx_1024, 'L0_attn_Wq': _L0_attn_in['Wq'], 'L0_attn_bq': _L0_attn_in['bq'], 'L0_attn_Wk': _L0_attn_in['Wk'], 'L0_attn_bk': _L0_attn_in['bk'], 'L0_attn_Wv': _L0_attn_in['Wv'], 'L0_attn_bv': _L0_attn_in['bv'], 'L0_attn_Wo': _L0_attn_in['Wo'], 'L0_attn_bo': _L0_attn_in['bo'], 'L0_xattn_Wq': _L0_xattn_in['Wq'], 'L0_xattn_bq': _L0_xattn_in['bq'], 'L0_xattn_Wk': _L0_xattn_in['Wk'], 'L0_xattn_bk': _L0_xattn_in['bk'], 'L0_xattn_Wv': _L0_xattn_in['Wv'], 'L0_xattn_bv': _L0_xattn_in['bv'], 'L0_ffn_centroids': _L0_ffn_in['centroids'], 'L0_ffn_w1': _L0_ffn_in['w1'], 'L0_ffn_b1': _L0_ffn_in['b1'], 'L0_ffn_w2': _L0_ffn_in['w2'], 'L0_ffn_b2': _L0_ffn_in['b2'], 'L0_ffn_gamma': _L0_ffn_in['gamma'], 'L0_ffn_beta': _L0_ffn_in['beta']}

def reference(x, ctx_1024, L0_attn_Wq, L0_attn_bq, L0_attn_Wk, L0_attn_bk, L0_attn_Wv, L0_attn_bv, L0_attn_Wo, L0_attn_bo, L0_xattn_Wq, L0_xattn_bq, L0_xattn_Wk, L0_xattn_bk, L0_xattn_Wv, L0_xattn_bv, L0_ffn_centroids, L0_ffn_w1, L0_ffn_b1, L0_ffn_w2, L0_ffn_b2, L0_ffn_gamma, L0_ffn_beta):
    import jax
    import jax.numpy as jnp

    def _L0_attn_ref(x, Wq, bq, Wk, bk, Wv, bv, Wo, bo):
        import jax, jax.numpy as jnp
        import numpy as np
        EMBED_DIM = 128
        SEQ_LEN = 256
        BATCH = 4
        TOPK = 32
        B, S, E = x.shape
        lin = lambda t, W, b: jnp.einsum('bse,oe->bso', t, W) + b
        q = lin(x, Wq, bq)
        k = lin(x, Wk, bk)
        v = lin(x, Wv, bv)
        scale = jnp.sqrt(jnp.asarray(E, x.dtype))
        scores = jnp.einsum('bqe,bke->bqk', q, k) / scale
        kk = min(TOPK, S)
        top_vals, top_idx = jax.lax.top_k(scores, kk)
        bi = jnp.arange(B)[:, None, None]
        si = jnp.arange(S)[None, :, None]
        sparse = jnp.full_like(scores, -jnp.inf).at[bi, si, top_idx].set(top_vals)
        attn = jax.nn.softmax(sparse, axis=-1)
        attn = jnp.nan_to_num(attn, nan=0.0)
        out = jnp.einsum('bqk,bke->bqe', attn, v)
        return lin(out, Wo, bo)

    def _L0_xattn_ref(query, key, value, Wq, bq, Wk, bk, Wv, bv):
        import jax, jax.numpy as jnp
        import numpy as np
        D = 128
        H = 16
        HD = D // H
        B, S, _ = query.shape
        Q = (query @ Wq.T + bq).reshape(B, S, H, HD).transpose(0, 2, 1, 3)
        K = (key @ Wk.T + bk).reshape(B, S, H, HD).transpose(0, 2, 1, 3)
        V = (value @ Wv.T + bv).reshape(B, S, H, HD).transpose(0, 2, 1, 3)
        scores = jnp.einsum('bhqd,bhkd->bhqk', Q, K) / jnp.sqrt(jnp.asarray(HD, Q.dtype))
        weights = jax.nn.softmax(scores, axis=-1)
        out = jnp.einsum('bhqk,bhkd->bhqd', weights, V)
        return out.transpose(0, 2, 1, 3).reshape(B, S, H * HD)

    def _L0_ffn_ref(x, centroids, w1, b1, w2, b2, gamma, beta):
        import jax, jax.numpy as jnp
        import numpy as np
        E = 8
        EPS = 1e-05
        B, S, d = x.shape
        feats = x.reshape(-1, d)
        aff = feats @ centroids.T
        eid = jnp.argmax(aff, axis=1)
        mu = jnp.mean(feats, axis=-1, keepdims=True)
        var = jnp.var(feats, axis=-1, keepdims=True)
        xhat = (feats - mu) * jax.lax.rsqrt(var + EPS)
        out = jnp.zeros_like(feats)
        for e in range(E):
            mask = (eid == e).astype(feats.dtype)[:, None]
            h = xhat * gamma[e] + beta[e]
            y = feats + jax.nn.relu(h @ w1[e] + b1[e]) @ w2[e] + b2[e]
            alpha = jax.nn.sigmoid(feats @ centroids[e])[:, None]
            out = out + mask * (alpha * y + (1.0 - alpha) * feats)
        return out.reshape(B, S, d)
    x = x + _L0_attn_ref(_layernorm(x, axis=-1), L0_attn_Wq, L0_attn_bq, L0_attn_Wk, L0_attn_bk, L0_attn_Wv, L0_attn_bv, L0_attn_Wo, L0_attn_bo)
    x = x + _L0_xattn_ref(_layernorm(x, axis=-1), ctx_1024, ctx_1024, L0_xattn_Wq, L0_xattn_bq, L0_xattn_Wk, L0_xattn_bk, L0_xattn_Wv, L0_xattn_bv)
    x = x + _L0_ffn_ref(_layernorm(x, axis=-1), L0_ffn_centroids, L0_ffn_w1, L0_ffn_b1, L0_ffn_w2, L0_ffn_b2, L0_ffn_gamma, L0_ffn_beta)
    return x

_drawn_inputs = setup_inputs


def setup_inputs(seed=0):
    import zlib

    import numpy as np

    out = dict(_drawn_inputs(seed))
    spreads = {'L0_attn_bq': (0.0, 0.73),
     'L0_attn_bk': (0.0, 0.8),
     'L0_attn_bv': (0.0, 0.371),
     'L0_attn_bo': (0.0, 0.1),
     'L0_ffn_b1': (0.0, 0.8),
     'L0_ffn_b2': (0.0, 0.326),
     'L0_ffn_gamma': (1.0, 0.6),
     'L0_ffn_beta': (0.0, 0.8)}
    factors = {'L0_attn_Wq': 4.627, 'L0_attn_Wk': 4.409, 'L0_attn_Wv': 4.329, 'L0_xattn_bk': 8.0}
    for name, (base, spread) in spreads.items():
        noise = np.random.default_rng([zlib.crc32(name.encode()), seed]).standard_normal(out[name].shape)
        drawn = base * np.exp(spread * noise) if base else spread * noise
        out[name] = jnp.asarray(drawn.astype(out[name].dtype))
    for name, factor in factors.items():
        out[name] = (out[name] * factor).astype(out[name].dtype)
    return out
```

```python
import numpy as np
import concourse.bass as bass
from concourse import mybir
from contextlib import ExitStack


def preln_decoder_kernel(nc, T, out):
    F32 = mybir.dt.float32
    BF16 = mybir.dt.bfloat16
    I32 = mybir.dt.int32
    U32 = mybir.dt.uint32
    ALU = mybir.AluOpType
    ACT = mybir.ActivationFunctionType
    AX = mybir.AxisListType
    ds = bass.ds

    B, S, D = T["x"].shape
    E, _, F = T["w1"].shape
    H, HD = 16, 8
    G = 4
    NG = B // G
    GS = G * S
    TOPK = 32
    NPART = 3
    STK = NPART * NPART * HD
    HC = HD + 1
    FC = F // 128
    NTILE = B * S // 128 + E - 1
    NTC = NTILE + 1
    PAY = 2 * D + 4
    TAKEN = -3.0e38
    EPS = 1e-5
    SELF_SCALE = 1.0 / float(np.sqrt(D))
    HEAD_SCALE = 1.0 / float(np.sqrt(HD))
    RING = 6

    q_scratch = [nc.dram_tensor(f"q_parts_{i}", [128, NPART, GS], BF16, kind="Internal").ap() for i in range(2)]
    k_scratch = [nc.dram_tensor(f"k_parts_{i}", [128, NPART, GS], BF16, kind="Internal").ap() for i in range(2)]
    rows = nc.dram_tensor("routed_rows", [B * S, PAY], F32, kind="Internal").ap()
    out_rows = out.rearrange("b s d -> (b s) d")

    with ExitStack() as stack:
        def sb(name, shape, dt=F32):
            return stack.enter_context(nc.sbuf_tensor(name, shape, dt))

        def ps(name, shape, dt=F32):
            return stack.enter_context(nc.psum_tensor(name, shape, dt))

        def sem(name):
            return stack.enter_context(nc.semaphore(name))

        ident = sb("ident", [128, 128])
        ident_bf = sb("ident_bf", [128, 128], BF16)
        head_sel = sb("head_sel", [128, H, 128], BF16)
        minus_half = sb("minus_half", [128, G])
        wq_t, wk_t, wv, wo_t, wvo_t = (sb(n, [128, D]) for n in ("wq_t", "wk_t", "wv", "wo_t", "wvo_t"))
        xwq_t, xwk_t, xwv_t = (sb(n, [128, D]) for n in ("xwq_t", "xwk_t", "xwv_t"))
        cent_t = sb("cent_t", [128, E])
        gamma_t = sb("gamma_t", [128, E])
        beta_t = sb("beta_t", [128, E])
        bias_cols = sb("bias_cols", [128, 4])
        bv_col = sb("bv_col", [128, 1])
        bv_cols = sb("bv_cols", [128, 128])
        bo_rows = sb("bo_rows", [128, D])
        xbv_rows = sb("xbv_rows", [128, D])
        bvo_rows = sb("bvo_rows", [128, D])
        w1 = sb("w1", [128, E * F])
        w2 = sb("w2", [128, E * FC * D])
        x_in = sb("x_in", [128, 4 * GS])
        ctx_in = sb("ctx_in", [128, GS])
        stats = [sb(f"stats_{i}", [128, G, 6]) for i in range(3)]
        moments = [sb(f"moments_{i}", [128, G, 2]) for i in range(3)]
        var_eps = [sb(f"var_eps_{i}", [128, G]) for i in range(3)]
        rstd = [sb(f"rstd_{i}", [128, G]) for i in range(3)]
        centred = sb("centred", [128, GS])
        xn = sb("xn", [128, GS])
        xn_t = sb("xn_t", [128, GS])
        q_t = sb("q_t", [128, GS])
        k_t = sb("k_t", [128, GS])
        v = sb("v", [128, 2 * GS])
        scores = sb("scores", [128, GS])
        left = sb("left", [128, GS])
        best8 = sb("best8", [128, G, TOPK // 8, 8])
        neg_max = sb("neg_max", [128, G])
        expd = sb("expd", [128, GS])
        probs = sb("probs", [128, GS])
        probs_n = sb("probs_n", [128, GS])
        prob_sum = sb("prob_sum", [128, G])
        prob_inv = sb("prob_inv", [128, G])
        probs_t = sb("probs_t", [128, GS])
        x_bo = sb("x_bo", [128, GS])
        x1 = sb("x1", [128, GS])
        x1_bv = sb("x1_bv", [128, 2 * GS])
        xn2 = sb("xn2", [128, GS])
        xn2_t = sb("xn2_t", [128, GS])
        xq = sb("xq", [128, GS])
        xq_rest = sb("xq_rest", [128, GS])
        xq_parts = sb("xq_parts", [128, NPART, GS], BF16)
        ctx_t = sb("ctx_t", [128, GS])
        xk = sb("xk", [128, GS])
        xk_rest = sb("xk_rest", [128, GS])
        xk_parts = sb("xk_parts", [128, NPART, GS], BF16)
        xv = sb("xv", [128, 2 * G * H * HC])
        q_stack = sb("q_stack", [128, 2 * H * GS], BF16)
        k_stack = sb("k_stack", [128, 2 * H * GS], BF16)
        neg_hmax = sb("neg_hmax", [128, 2, H])
        hmax_rest = sb("hmax_rest", [128, 2, H])
        hmax_parts = sb("hmax_parts", [128, 2, 128], BF16)
        hmax_t = sb("hmax_t", [128, 2, 128], BF16)
        weights = sb("weights", [128, 2, H // 2 * 128])
        wsum_inv = sb("wsum_inv", [128, H])
        attended = sb("attended", [128, 2, H * HD])
        x2 = sb("x2", [128, 2 * GS])
        feats_c = sb("feats_c", [128, GS])
        feats = sb("feats", [128, GS])
        feats_t = sb("feats_t", [128, GS])
        var2 = sb("var2", [128, G])
        rstd2 = sb("rstd2", [128, G])
        pay = sb("pay", [128, G, PAY])
        aff = sb("aff", [128, B, E])
        aff_max = sb("aff_max", [128, G])
        aff_exp = sb("aff_exp", [128, G])
        aff_den = sb("aff_den", [128, G])

        iota_i = sb("iota_i", [128, 128], I32)
        iota_f = sb("iota_f", [128, 128])
        place_i = sb("place_i", [128, 1], I32)
        place_f = sb("place_f", [128, 1])
        earlier = sb("earlier", [128, 128], BF16)
        ones_row = sb("ones_row", [1, 128])
        all_ones = sb("all_ones", [128, 128], BF16)
        tile_expert = sb("tile_expert", [128, NTC], I32)
        gather_idx = sb("gather_idx", [128, NTC], I32)
        scatter_idx = sb("scatter_idx", [128, NTC], I32)
        index_now = sb("index_now", [128, RING, 2], I32)

        room = {"q": [q_stack[:, :].bitcast(F32), 0], "k": [k_stack[:, :].bitcast(F32), 0]}

        def carve(which, n, dt=F32):
            words = n if dt == F32 or dt == I32 else n // 2
            ap, at0 = room[which]
            room[which][1] = at0 + words
            assert at0 + words <= H * GS
            piece = ap[:, at0:at0 + words]
            return piece if dt == F32 else piece.bitcast(dt)

        ffn_row = [carve("q", PAY) for _ in range(RING)]
        ffn_row_t = [carve("k", D) for _ in range(2)]
        ffn_hid = [carve("q", F) for _ in range(2)]
        ffn_relu = [carve("q", F) for _ in range(2)]
        ffn_y = [carve("q", D) for _ in range(2)]
        ffn_out = [x_in[:, (E + n) * D:(E + n + 1) * D] for n in range(RING)]
        b1_rows = carve("q", E * F)
        b2_rows = x_in[:, 0:E * D]
        beta_cols = carve("k", 128)
        lo_hot = carve("k", B * 128, BF16)
        hi_hot = carve("k", B * 2 * NTC, BF16)
        onehot = carve("k", E * B, BF16)

        s1_bank = ps("s1_bank", [128, 1024])
        s2_bank = ps("s2_bank", [128, 1024])
        pv_bank = ps("pv_bank", [128, 512])
        self_bank = ps("self_bank", [128, 512])
        cross_bank = ps("cross_bank", [128, 512])
        small_bank = ps("small_bank", [128, 512])
        small_bf = small_bank[:, :].bitcast(BF16)

        names = """x_loaded ctx_loaded weights_loaded ffn_loaded consts_made sel_made
            ln0_stats ln0_moments ln0_var ln0_rstd ln0_centred xn_ready
            ln1_stats ln1_moments ln1_var ln1_rstd ln1_centred xn2_ready
            ln2_stats ln2_moments ln2_var ln2_rstd ln2_centred feats_ready
            xn_transposed xn_t_ready q_done q_ready k_done k_ready v_done v_ready scores_done scores_ready
            topk_step neg_max_ready self_exp probs_ready inv_ready probs_n_ready probs_transposed probs_t_ready
            attn_done x_bo_ready x1_ready x1_bv_ready
            xn2_transposed xn2_t_ready xq_done xq_ready xq_step xq_split xq_stored xq_stacked
            ctx_transposed ctx_t_ready xk_done xk_ready xk_step xk_split xk_stored xk_stacked xv_done xv_ready ones_made
            s1_done s1_max hmax_step hmax_split hmax_transposed hmax_t_ready s2_done s2_exp pv_half
            wsum_inv_ready attended_ready x2_ready
            feats_transposed feats_t_ready aff_done aff_ready aff_max_ready aff_exp_ready aff_den_ready alpha_ready
            rstd2_step rstd2_ready base_ready pay_ready pay_stored bv_made wvo_done wvo_ready
            beta_made b1_done b1_ready w1_scaled iota_made
            route_step onehot_ready counts_done slots_ready tok_done tok_ready experts_ready
            row_transposed row_t_ready hid_done hid_ready hid_transposed relu_ready
            y_done y_biased result_ready
            """.split()
        s = {n: sem(n) for n in names}
        s["index_copied"] = [sem("gather_index_copied"), sem("scatter_index_copied")]
        row_gathered = [sem(f"row_gathered_{r}") for r in range(RING)]
        row_scattered = [sem(f"row_scattered_{r}") for r in range(RING)]
        block = stack.enter_context(nc.Block())

        N_WEIGHTS = 16 * 17
        N_FFN = 16 * (2 * E + 2)

        def wait_alone(eng, semaphore, n):
            eng.wait_ge(semaphore, n)
            if not isinstance(n, int):
                eng.nop(nofuse=True)

        def at(t, start, n, p=128):
            return t[0:p, ds(start, n)]

        def grouped(ap):
            return ap.rearrange("p (g n) -> p g n", g=G)

        def spread(ap, shape):
            return ap.to_broadcast(shape)

        def passes(eng, run):
            run(-2)
            run(-1)
            run(0)
            run(1)
            with eng.Fori(2, NG - 2) as g:
                run(g)
            run(NG - 2)
            run(NG - 1)
            run(NG)

        def stages(g):
            if not isinstance(g, int):
                return True, True, True, True
            return 0 <= g - 1, 0 <= g < NG, 0 <= g + 1 < NG, g + 2 < NG

        def half(g):
            return g % 2

        be = lambda ap: ap.rearrange("p (b e) -> p b e", e=E)
        eb = lambda ap: ap.rearrange("p (e b) -> p e b", b=B)
        chosen = carve("k", B * E)
        most = carve("k", B)
        counts = carve("k", 2 * E * B)
        running = carve("k", E * B)
        per_expert = carve("k", E)
        passed = carve("k", E * B)
        tiles_of = carve("k", E)
        tiles_end = carve("k", E)
        shift_of = carve("k", E)
        ones_f = carve("k", E * B)
        slot = carve("k", B)
        slot_i = carve("k", B, I32)
        hi_i = carve("k", B, I32)
        lo_i = carve("k", B, I32)
        hi_f = carve("k", B)
        lo_f = carve("k", B)
        hi_eq = carve("k", B * NTC, BF16)
        after = carve("k", NTC * E)
        expert_f = carve("k", NTC)
        token_f = carve("k", NTC)
        empty_f = carve("k", NTC)
        index_f = carve("k", NTC)

        def route_vector(dve):
            step = [0]

            def link(ins):
                step[0] += 1
                ins.then_inc(s["route_step"], 1)
                dve.wait_ge(s["route_step"], step[0])

            dve.wait_ge(s["aff_ready"], NG)
            dve.wait_ge(s["iota_made"], 4)
            dve.wait_ge(s["attended_ready"], B)
            dve.wait_ge(s["s2_done"], 2 * B)
            link(dve.tensor_reduce(most, aff[:, :, :], AX.X, ALU.max))
            link(dve.tensor_tensor(be(chosen), aff[:, :, :], spread(most.rearrange("p (b a) -> p b a", a=1), [128, B, E]),
                                   ALU.is_equal))
            link(dve.tensor_scalar(per_expert, iota_f[:, 0:E], -1.0, float(E), ALU.mult, ALU.add))
            link(dve.tensor_tensor(be(chosen), be(chosen), spread(per_expert.rearrange("p (a e) -> p a e", a=1), [128, B, E]),
                                   ALU.mult))
            link(dve.tensor_reduce(most, be(chosen), AX.X, ALU.max))
            link(dve.tensor_tensor(onehot.rearrange("p (e b) -> p b e", b=B), be(chosen),
                                   spread(most.rearrange("p (b a) -> p b a", a=1), [128, B, E]), ALU.is_equal))
            dve.memset(ones_f, 1.0).then_inc(s["onehot_ready"], 1)
            dve.wait_ge(s["counts_done"], 1)
            link(dve.tensor_copy(counts, s1_bank[:, 0:2 * E * B]))
            total = counts[:, E * B:2 * E * B]
            dve.wait_ge(s["onehot_ready"], 1)
            link(dve.tensor_tensor_scan(running, ones_f, total, 0.0, ALU.mult, ALU.add))
            link(dve.tensor_reduce(per_expert, eb(total), AX.X, ALU.add))
            link(dve.tensor_scalar(chosen[:, 0:B], iota_f[:, 0:B], 128.0, None, ALU.mult))
            link(dve.tensor_tensor(eb(passed), spread(per_expert.rearrange("p (e a) -> p e a", a=1), [128, E, B]),
                                   spread(chosen[:, 0:B].rearrange("p (a b) -> p a b", a=1), [128, E, B]), ALU.is_gt))
            link(dve.tensor_reduce(tiles_of, eb(passed), AX.X, ALU.add))
            link(dve.tensor_tensor_scan(tiles_end, ones_f[:, 0:E], tiles_of, 0.0, ALU.mult, ALU.add))
            link(dve.tensor_tensor(shift_of, tiles_end, tiles_of, ALU.subtract))
            link(dve.scalar_tensor_tensor(shift_of, shift_of, 128.0, per_expert, ALU.mult, ALU.add))
            link(dve.tensor_tensor(shift_of, shift_of, eb(running)[:, :, B - 1], ALU.subtract))
            link(dve.tensor_tensor(running, running, total, ALU.subtract))
            link(dve.tensor_tensor(running, running, counts[:, 0:E * B], ALU.add))
            link(dve.tensor_tensor(eb(running), eb(running), spread(shift_of.rearrange("p (e a) -> p e a", a=1), [128, E, B]),
                                   ALU.add))
            link(dve.tensor_tensor(running, running, onehot, ALU.mult))
            link(dve.tensor_reduce(slot, running.rearrange("p (e b) -> p b e", b=B), AX.X, ALU.add))
            link(dve.tensor_copy(slot_i, slot))
            link(dve.tensor_scalar(hi_i, slot_i, 7, None, ALU.logical_shift_right))
            link(dve.tensor_scalar(lo_i, slot_i, 127, None, ALU.bitwise_and))
            link(dve.tensor_copy(hi_f, hi_i))
            link(dve.tensor_copy(lo_f, lo_i))
            col = lambda ap: ap.rearrange("p (b a) -> p b a", a=1)
            row = lambda ap: ap.rearrange("p (a n) -> p a n", a=1)
            dve.tensor_tensor(lo_hot.rearrange("p (b n) -> p b n", b=B), spread(row(iota_f[:, :]), [128, B, 128]),
                              spread(col(lo_f), [128, B, 128]), ALU.is_equal).then_inc(s["slots_ready"], 1)
            link(dve.tensor_tensor(hi_eq.rearrange("p (b n) -> p b n", b=B), spread(row(iota_f[:, 0:NTC]), [128, B, NTC]),
                                   spread(col(hi_f), [128, B, NTC]), ALU.is_equal))
            parts = hi_hot.rearrange("p (b k n) -> p b k n", b=B, k=2)
            heq = hi_eq.rearrange("p (b n) -> p b n", b=B)
            dve.tensor_scalar(parts[:, :, 0, :], heq, place_f[:, 0:1], None, ALU.mult).then_inc(s["slots_ready"], 1)
            dve.tensor_tensor(parts[:, :, 1, :], heq, spread(col(iota_f[:, 0:B]), [128, B, NTC]), ALU.mult)\
               .then_inc(s["slots_ready"], 1)
            link(dve.tensor_tensor(after.rearrange("p (t e) -> p t e", e=E), spread(col(iota_f[:, 0:NTC]), [128, NTC, E]),
                                   spread(row(tiles_end), [128, NTC, E]), ALU.is_ge))
            link(dve.tensor_reduce(expert_f, after.rearrange("p (t e) -> p t e", e=E), AX.X, ALU.add))
            link(dve.tensor_scalar(expert_f, expert_f, float(E - 1), None, ALU.min))
            dve.tensor_copy(tile_expert[:, :], expert_f).then_inc(s["experts_ready"], 1)
            dve.wait_ge(s["tok_done"], 1)
            link(dve.tensor_copy(token_f, self_bank[:, 0:NTC]))
            link(dve.tensor_scalar(empty_f, token_f, 0.5, float(2 * B * S), ALU.is_lt, ALU.mult))
            link(dve.tensor_scalar(index_f, self_bank[:, NTC:2 * NTC], float(S), -1.0, ALU.mult, ALU.add))
            link(dve.tensor_tensor(token_f, token_f, index_f, ALU.add))
            link(dve.tensor_scalar(index_f, token_f, 0.0, None, ALU.max))
            dve.tensor_copy(gather_idx[:, :], index_f).then_inc(s["tok_ready"], 1)
            link(dve.tensor_tensor(empty_f, empty_f, token_f, ALU.add))
            dve.tensor_copy(scatter_idx[:, :], empty_f).then_inc(s["tok_ready"], 1)
            ffn_vector(dve)

        def tiles(eng, step, first, last):
            for t in range(first, RING):
                step(t // RING, t % RING)
            with eng.Fori(1, NTILE // RING) as i:
                for r in range(RING):
                    step(i, r)
            for t in range(NTILE // RING * RING, last):
                step(t // RING, t % RING)

        def tile(i, r, ahead):
            t = RING * i + r + ahead
            return t, (r + ahead) % RING, not isinstance(i, int) or 0 <= t < NTILE

        def expert_of(eng, t):
            col = tile_expert[0:1, t:t + 1] if isinstance(t, int) else tile_expert[0:1, ds(t, 1)]
            return eng.value_load(col, min_val=0, max_val=E - 1)

        def ffn_tensor(pe):
            pe.wait_ge(s["onehot_ready"], 1)
            pe.wait_ge(s["iota_made"], 4)
            pe.matmul(s1_bank[:, 0:E * B], earlier[:, :], onehot, start=True, stop=True)
            pe.matmul(s1_bank[:, E * B:2 * E * B], all_ones[:, :], onehot, start=True, stop=True)\
              .then_inc(s["counts_done"], 1)
            for e in range(E):
                pe.wait_ge(s["beta_made"], e + 1)
                if e >= 2:
                    pe.wait_ge(s["b1_ready"], e - 1)
                bank = s2_bank[:, (e % 2) * F:(e % 2 + 1) * F]
                pe.matmul(bank, beta_cols, w1[:, e * F:(e + 1) * F], start=True, stop=False)
                pe.matmul(bank, ones_row[0:1, :], b1_rows[0:1, e * F:(e + 1) * F], start=False, stop=True)\
                  .then_inc(s["b1_done"], 1)
            pe.wait_ge(s["slots_ready"], 3)
            for b in range(B):
                m = pe.matmul(self_bank[:, 0:2 * NTC], lo_hot[:, b * 128:(b + 1) * 128],
                              hi_hot[:, b * 2 * NTC:(b + 1) * 2 * NTC], start=b == 0, stop=b == B - 1)
            m.then_inc(s["tok_done"], 1)
            pe.wait_ge(s["experts_ready"], 1)
            pe.wait_ge(s["b1_ready"], E)
            pe.wait_ge(s["w1_scaled"], E)
            pe.wait_ge(s["tok_ready"], 2)

            def step(i, r):
                t, k, there = tile(i, r, 1)
                if there:
                    q = t // RING if isinstance(t, int) else (i + (1 if r + 1 >= RING else 0))
                    pe.wait_ge(row_gathered[k], 16 * (q + 1))
                    if not isinstance(i, int) or t >= 1:
                        pe.wait_ge(s["row_t_ready"], t)
                    pe.transpose(cross_bank[:, 0:128], ffn_row[k][:, 0:D], ident[:, :]).then_inc(s["row_transposed"], 1)
                t, k, there = tile(i, r, 0)
                if there:
                    e = expert_of(pe, t)
                    pe.wait_ge(s["row_t_ready"], t + 1)
                    if not isinstance(i, int) or t >= 2:
                        pe.wait_ge(s["hid_ready"], t - 1)
                    pe.matmul(s1_bank[:, (k % 2) * F:(k % 2 + 1) * F], ffn_row_t[k % 2], at(w1, e * F, F),
                              start=True, stop=True).then_inc(s["hid_done"], 1)
                t, k, there = tile(i, r, -1)
                if there:
                    pe.wait_ge(s["hid_ready"], t + 1)
                    if not isinstance(i, int) or t >= 2:
                        pe.wait_ge(s["relu_ready"], t - 1)
                    for c in range(FC):
                        m = pe.transpose(s2_bank[:, (k % 2) * F + c * 128:(k % 2) * F + (c + 1) * 128],
                                         ffn_hid[k % 2][:, c * 128:(c + 1) * 128], ident[:, :])
                    m.then_inc(s["hid_transposed"], 1)
                t, k, there = tile(i, r, -2)
                if there:
                    e = expert_of(pe, t)
                    pe.wait_ge(s["relu_ready"], t + 1)
                    if not isinstance(i, int) or t >= 2:
                        pe.wait_ge(s["y_biased"], t - 1)
                    bank = (pv_bank, self_bank)[k % 2]
                    for c in range(FC):
                        m = pe.matmul(bank[:, 0:D], ffn_relu[k % 2][:, c * 128:(c + 1) * 128],
                                      at(w2, e * (FC * D) + c * D, D), start=c == 0, stop=c == FC - 1)
                    m.then_inc(s["y_done"], 1)

            tiles(pe, step, -1, NTILE + 2)

        def ffn_vector(dve):
            dve.wait_ge(s["b1_ready"], E)

            def step(i, r):
                t, k, there = tile(i, r, 2)
                if there:
                    e = expert_of(dve, t)
                    dve.wait_ge(s["hid_done"], t + 1)
                    if not isinstance(i, int) or t >= 2:
                        dve.wait_ge(s["hid_transposed"], t - 1)
                    dve.tensor_tensor(ffn_hid[k % 2], s1_bank[:, (k % 2) * F:(k % 2 + 1) * F], at(b1_rows, e * F, F),
                                      ALU.add).then_inc(s["hid_ready"], 1)
                t, k, there = tile(i, r, 0)
                if there:
                    e = expert_of(dve, t)
                    bank = (pv_bank, self_bank)[k % 2]
                    dve.wait_ge(s["y_done"], t + 1)
                    dve.tensor_tensor(ffn_y[k % 2], bank[:, 0:D], at(b2_rows, e * D, D), ALU.add).then_inc(s["y_biased"], 1)
                    dve.wait_ge(s["y_biased"], t + 1)
                    dve.wait_ge(row_gathered[k], 16 * (i + 1))
                    if not isinstance(i, int) or t >= RING:
                        dve.wait_ge(row_scattered[k], 16 * i)
                    dve.scalar_tensor_tensor(ffn_out[k], ffn_y[k % 2], ffn_row[k][:, 2 * D:2 * D + 1], ffn_row[k][:, D:2 * D],
                                             ALU.mult, ALU.add).then_inc(s["result_ready"], 1)

            tiles(dve, step, -2, NTILE)

        def ffn_scalar(act):
            for e in range(E):
                act.wait_ge(s["b1_done"], e + 1)
                act.activation(b1_rows[:, e * F:(e + 1) * F], s2_bank[:, (e % 2) * F:(e % 2 + 1) * F], ACT.Copy)\
                   .then_inc(s["b1_ready"], 1)

            def step(i, r):
                t, k, there = tile(i, r, 1)
                if there:
                    act.wait_ge(s["row_transposed"], t + 1)
                    if not isinstance(i, int) or t >= 2:
                        act.wait_ge(s["hid_done"], t - 1)
                    act.activation(ffn_row_t[k % 2], cross_bank[:, 0:128], ACT.Copy).then_inc(s["row_t_ready"], 1)
                t, k, there = tile(i, r, -1)
                if there:
                    act.wait_ge(s["hid_transposed"], t + 1)
                    if not isinstance(i, int) or t >= 2:
                        act.wait_ge(s["y_done"], t - 1)
                    act.activation(ffn_relu[k % 2], s2_bank[:, (k % 2) * F:(k % 2 + 1) * F], ACT.Relu).then_inc(s["relu_ready"], 1)

            tiles(act, step, -1, NTILE + 2)

        def ffn_pool(pool):
            wait_alone(pool, s["ffn_loaded"], N_FFN)
            wait_alone(pool, s["s2_done"], 2 * B)
            for e in range(E):
                if e >= 1:
                    wait_alone(pool, s["b1_done"], e)
                pool.tensor_copy(beta_cols, spread(beta_t[:, e:e + 1], [128, 128])).then_inc(s["beta_made"], 1)
            for e in range(E):
                wait_alone(pool, s["b1_done"], e + 1)
                pool.tensor_scalar(w1[:, e * F:(e + 1) * F], w1[:, e * F:(e + 1) * F], gamma_t[:, e:e + 1], 1.0,
                                   ALU.mult, ALU.mult).then_inc(s["w1_scaled"], 1)
            wait_alone(pool, s["tok_ready"], 2)
            wait_alone(pool, s["pay_stored"], 16 * NG)

            def index(idx, t, k, n):
                src = idx[:, t:t + 1] if isinstance(t, int) else idx[:, ds(t, 1)]
                pool.tensor_copy(index_now[:, k, n:n + 1], src).then_inc(s["index_copied"][n], 1)
                wait_alone(pool, s["index_copied"][n], t + 1)
                return bass.IndirectOffsetOnAxis(ap=index_now[:, k, n:n + 1].bitcast(U32), axis=0)

            def step(i, r):
                t, k, there = tile(i, r, 0)
                old, _, stored = tile(i, r, -RING)
                if stored:
                    wait_alone(pool, s["result_ready"], old + 1)
                if there:
                    if stored:
                        wait_alone(pool, row_gathered[k], 16 * i)
                    pool.indirect_dma_start(out=ffn_row[k], out_offset=None, in_=rows,
                                            in_offset=index(gather_idx, t, k, 0)).then_inc(row_gathered[k], 16)
                if stored:
                    if not isinstance(i, int) or old >= RING:
                        wait_alone(pool, row_scattered[k], 16 * (i - 1))
                    pool.indirect_dma_start(out=out_rows, out_offset=index(scatter_idx, old, k, 1),
                                            in_=ffn_out[k], in_offset=None, bounds_check=B * S - 1,
                                            oob_is_err=False).then_inc(row_scattered[k], 16)

            tiles(pool, step, 0, NTILE + RING)
            for k in range(RING):
                n = len(range(k, NTILE, RING))
                wait_alone(pool, row_scattered[k], 16 * n)

        @block.sync
        def _(sp):
            def load_x(g):
                sp.dma_start(grouped(at(x_in, (g % 4) * GS, GS)),
                             T["x"][ds(g * G, G), :, :].rearrange("b s d -> s b d")).then_inc(s["x_loaded"], 16)

            def load_ctx(g):
                sp.dma_start(grouped(ctx_in[:, :]),
                             T["ctx_1024"][ds(g * G, G), :, :].rearrange("b s d -> s b d")).then_inc(s["ctx_loaded"], 16)

            load_x(0)
            for dst, src in ((wq_t, "wq_t"), (wk_t, "wk_t"), (wv, "wv"), (wo_t, "wo_t"),
                             (xwq_t, "xwq_t"), (xwk_t, "xwk_t"), (xwv_t, "xwv_t"), (cent_t, "cent_t"),
                             (gamma_t, "gamma_t"), (beta_t, "beta_t")):
                sp.dma_start(dst[:, :], T[src]).then_inc(s["weights_loaded"], 16)
            for n, src in enumerate(("bq", "bk", "xbq", "xbk")):
                sp.dma_start(bias_cols[:, n:n + 1], T[src].rearrange("(p a) -> p a", a=1)).then_inc(s["weights_loaded"], 16)
            sp.dma_start(bv_col[:, :], T["bv"].rearrange("(p a) -> p a", a=1)).then_inc(s["weights_loaded"], 16)
            for dst, src in ((bo_rows, "bo"), (xbv_rows, "xbv")):
                sp.dma_start(dst[:, :], T[src].partition_broadcast(128)).then_inc(s["weights_loaded"], 16)
            load_ctx(0)

            def store_and_stack(g, parts, scratch, stacked, is_q):
                name = "xq" if is_q else "xk"
                wait_alone(sp, s[name + "_split"], g + 1)
                if not isinstance(g, int) or g >= 1:
                    wait_alone(sp, s[name + "_stacked"], 144 * g)
                sp.dma_start(scratch, parts[:, :, :]).then_inc(s[name + "_stored"], 16)
                wait_alone(sp, s[name + "_stored"], 16 * g + 16)
                if not isinstance(g, int) or g >= 2:
                    wait_alone(sp, s["s2_done"], 8 * (g - 1))
                for a in range(NPART):
                    for b in range(NPART):
                        r = (a * NPART + b) * HD
                        src = scratch[:, a if is_q else b, :].rearrange("(h d) t -> d h t", d=HD)
                        dst = stacked[r:r + HD, ds(half(g) * H * GS, H * GS)].rearrange("d (h t) -> d h t", h=H)
                        sp.dma_start(dst, src).then_inc(s[name + "_stacked"], 16)

            def run(g):
                has_f, has_c, has_e, has_s = stages(g)
                if not isinstance(g, int) or g + 3 < NG:
                    if not isinstance(g, int) or g >= 1:
                        wait_alone(sp, s["x_bo_ready"], g)
                    if not isinstance(g, int) or g > -3:
                        wait_alone(sp, s["x_loaded"], 16 * (g + 3))
                    load_x(g + 3)
                if not isinstance(g, int) or (0 <= g + 2 < NG and g + 2 > 0):
                    wait_alone(sp, s["ctx_transposed"], g + 2)
                    wait_alone(sp, s["ctx_loaded"], 16 * (g + 2))
                    load_ctx(g + 2)
                if has_e:
                    store_and_stack(g + 1, xk_parts, k_scratch[0], k_stack, False)
                    store_and_stack(g + 1, xq_parts, q_scratch[0], q_stack, True)
                if has_f:
                    wait_alone(sp, s["pay_ready"], g)
                    wait_alone(sp, s["alpha_ready"], g)
                    sp.dma_start(rows[ds((g - 1) * GS, GS), :].rearrange("(b s) c -> s b c", s=S),
                                 pay[:, :, :]).then_inc(s["pay_stored"], 16)

            run(-2)
            for e in range(E):
                sp.dma_start(at(w1, e * F, F), T["w1"][e, :, :]).then_inc(s["ffn_loaded"], 16)
                sp.dma_start(at(w2, e * FC * D, FC * D).rearrange("p (c d) -> p c d", c=FC),
                             T["w2"][e, :, :].rearrange("(c p) d -> p c d", c=FC)).then_inc(s["ffn_loaded"], 16)
            run(-1)
            run(0)
            run(1)
            with sp.Fori(2, NG - 3) as g:
                run(g)
            run(NG - 3)
            run(NG - 2)
            run(NG - 1)
            wait_alone(sp, s["s2_done"], 2 * B)
            wait_alone(sp, s["x_bo_ready"], NG)
            sp.dma_start(b1_rows[0:1, :], T["b1"].rearrange("(a e) f -> a (e f)", a=1)).then_inc(s["ffn_loaded"], 16)
            sp.dma_start(b2_rows, T["b2"].rearrange("e d -> (e d)").partition_broadcast(128)).then_inc(s["ffn_loaded"], 16)
            run(NG)


        def norm_stats(dve, n, src, base, g, ready, count):
            dve.wait_ge(s[ready], count)
            if not isinstance(g, int) or g >= 1:
                dve.wait_ge(s[f"ln{n}_centred"], g)
            for b in range(G):
                dve.bn_stats(stats[n][:, b, :], at(src, base + b * S, S)).then_inc(s[f"ln{n}_stats"], 1)

        def norm_moments(dve, n, g):
            for b in range(G):
                wait_alone(dve, s[f"ln{n}_stats"], G * g + b + 1)
                dve.bn_aggr(moments[n][:, b, :], stats[n][:, b, :]).then_inc(s[f"ln{n}_moments"], 1)
            dve.wait_ge(s[f"ln{n}_moments"], G * g + G)
            dve.tensor_scalar(var_eps[n][:, :], moments[n][:, :, 1], EPS, None, ALU.add).then_inc(s[f"ln{n}_var"], 1)

        def norm_rstd(pool, n, g):
            wait_alone(pool, s[f"ln{n}_var"], g + 1)
            pool.tensor_tensor(rstd[n][:, :], var_eps[n][:, :], minus_half[:, :], ALU.pow).then_inc(s[f"ln{n}_rstd"], 1)

        def norm_apply(pool, n, g, src, centred_buf, dst, done):
            shape = [128, G, S]
            pool.tensor_tensor(grouped(centred_buf), grouped(src), spread(moments[n][:, :, 0:1], shape),
                               ALU.subtract).then_inc(s[f"ln{n}_centred"], 1)
            wait_alone(pool, s[f"ln{n}_centred"], g + 1)
            wait_alone(pool, s[f"ln{n}_rstd"], g + 1)
            pool.tensor_tensor(grouped(dst), grouped(centred_buf),
                               spread(rstd[n][:, :].rearrange("p (g a) -> p g a", a=1), shape),
                               ALU.mult).then_inc(s[done], 1)

        @block.gpsimd
        def _(pool):
            pool.memset(ident[:, :], 0.0).then_inc(s["consts_made"], 1)
            pool.memset(ident_bf[:, :], 0.0).then_inc(s["consts_made"], 1)
            pool.memset(minus_half[:, :], -0.5).then_inc(s["consts_made"], 1)
            pool.memset(head_sel[:, :, :], 0.0).then_inc(s["consts_made"], 1)
            pool.memset(xv[:, :], 1.0).then_inc(s["ones_made"], 1)
            pool.memset(hmax_parts[:, :, :], 0.0).then_inc(s["ones_made"], 1)
            pool.memset(earlier[:, :], 1.0).then_inc(s["consts_made"], 1)
            pool.memset(all_ones[:, :], 1.0).then_inc(s["consts_made"], 1)
            pool.memset(ones_row[:, :], 1.0).then_inc(s["consts_made"], 1)
            pool.iota(iota_i[:, :], pattern=[[1, 128]], base=0, channel_multiplier=0).then_inc(s["consts_made"], 1)
            pool.iota(place_i[:, :], pattern=[[0, 1]], base=1, channel_multiplier=1).then_inc(s["consts_made"], 1)
            wait_alone(pool, s["consts_made"], 9)
            pool.affine_select(out=earlier[:, :], in_=earlier[:, :], compare_op=ALU.is_gt, fill=0.0, base=0,
                               pattern=[[1, 128]], channel_multiplier=-1).then_inc(s["iota_made"], 1)
            pool.tensor_copy(iota_f[:, :], iota_i[:, :]).then_inc(s["iota_made"], 1)
            pool.tensor_copy(place_f[:, :], place_i[:, :]).then_inc(s["iota_made"], 1)
            pool.memset(pay[:, :, 2 * D:PAY], 0.0).then_inc(s["iota_made"], 1)
            for m in (ident, ident_bf):
                pool.affine_select(out=m[:, :], in_=m[:, :], compare_op=ALU.not_equal, fill=1.0, base=0,
                                   pattern=[[-1, 128]], channel_multiplier=1).then_inc(s["consts_made"], 1)
            for i in range(NPART):
                wait_alone(pool, s["sel_made"], i)
                pool.affine_select(out=head_sel[:, :, :], in_=head_sel[:, :, :], compare_op=ALU.not_equal, fill=1.0,
                                   base=-H * i, pattern=[[-1, H], [0, 128]], channel_multiplier=1).then_inc(s["sel_made"], 1)

            def split(g, name, full, rest, parts):
                if not isinstance(g, int) or g >= 1:
                    wait_alone(pool, s[name + "_stored"], 16 * g)
                wait_alone(pool, s[name + "_ready"], 2 * g + 2)
                pool.tensor_tensor(rest[:, :], full[:, :], parts[:, 0, :], ALU.subtract).then_inc(s[name + "_step"], 1)
                wait_alone(pool, s[name + "_step"], 2 * g + 1)
                pool.tensor_copy(parts[:, 1, :], rest[:, :]).then_inc(s[name + "_step"], 1)
                wait_alone(pool, s[name + "_step"], 2 * g + 2)
                pool.tensor_tensor(parts[:, 2, :], rest[:, :], parts[:, 1, :], ALU.subtract).then_inc(s[name + "_split"], 1)

            def hmax_split(g, j):
                n, i = G * g + j, j % 2
                wait_alone(pool, s["s1_max"], 2 * n + 2)
                if not isinstance(g, int) or n >= 2:
                    wait_alone(pool, s["hmax_transposed"], n - 1)
                parts = [hmax_parts[:, i, H * a:H * (a + 1)] for a in range(NPART)]
                pool.tensor_copy(parts[0], neg_hmax[:, i, :]).then_inc(s["hmax_step"], 1)
                wait_alone(pool, s["hmax_step"], 3 * n + 1)
                pool.tensor_tensor(hmax_rest[:, i, :], neg_hmax[:, i, :], parts[0], ALU.subtract).then_inc(s["hmax_step"], 1)
                wait_alone(pool, s["hmax_step"], 3 * n + 2)
                pool.tensor_copy(parts[1], hmax_rest[:, i, :]).then_inc(s["hmax_step"], 1)
                wait_alone(pool, s["hmax_step"], 3 * n + 3)
                pool.tensor_tensor(parts[2], hmax_rest[:, i, :], parts[1], ALU.subtract).then_inc(s["hmax_split"], 1)

            def add_attended(g, j):
                n = G * g + j
                wait_alone(pool, s["attended_ready"], n + 1)
                if j == 0 and (not isinstance(g, int) or g >= 2):
                    wait_alone(pool, s["pay_ready"], g - 1)
                pool.tensor_tensor(at(x2, half(g) * GS + j * S, S), at(x1_bv, half(g) * GS + j * S, S),
                                   attended[:, j % 2, :], ALU.add).then_inc(s["x2_ready"], 1)

            def run(g):
                has_f, has_c, has_e, has_s = stages(g)
                if has_s:
                    h = g + 2
                    norm_rstd(pool, 0, h)
                    if not isinstance(h, int) or h >= 1:
                        wait_alone(pool, s["xn_transposed"], h)
                    norm_apply(pool, 0, h, at(x_in, (h % 4) * GS, GS), centred[:, :], xn[:, :], "xn_ready")
                if has_e:
                    h = g + 1
                    if not isinstance(h, int) or h >= 1:
                        wait_alone(pool, s["x1_ready"], h)
                    pool.tensor_tensor(grouped(x_bo[:, :]), grouped(at(x_in, (h % 4) * GS, GS)),
                                       spread(bo_rows[:, :].rearrange("p (a n) -> p a n", a=1), [128, G, S]),
                                       ALU.add).then_inc(s["x_bo_ready"], 1)
                if has_c:
                    hmax_split(g, 0)
                if has_e:
                    split(g + 1, "xk", xk, xk_rest, xk_parts)
                if has_f:
                    h = g - 1
                    norm_rstd(pool, 2, h)
                    if not isinstance(h, int) or h >= 1:
                        wait_alone(pool, s["feats_transposed"], h)
                    norm_apply(pool, 2, h, at(x2, half(h) * GS, GS), feats_c[:, :], feats[:, :], "feats_ready")
                if has_c:
                    hmax_split(g, 1)
                    add_attended(g, 0)
                if has_e:
                    h = g + 1
                    norm_rstd(pool, 1, h)
                    if not isinstance(h, int) or h >= 1:
                        wait_alone(pool, s["xn2_transposed"], h)
                    norm_apply(pool, 1, h, x1[:, :], centred[:, :], xn2[:, :], "xn2_ready")
                    if not isinstance(h, int) or h >= 2:
                        wait_alone(pool, s["x2_ready"], G * (h - 1))
                    pool.tensor_tensor(grouped(at(x1_bv, half(h) * GS, GS)), grouped(x1[:, :]),
                                       spread(xbv_rows[:, :].rearrange("p (a n) -> p a n", a=1), [128, G, S]),
                                       ALU.add).then_inc(s["x1_bv_ready"], 1)
                if has_c:
                    hmax_split(g, 2)
                    add_attended(g, 1)
                if has_e:
                    split(g + 1, "xq", xq, xq_rest, xq_parts)
                if has_c:
                    hmax_split(g, 3)
                    add_attended(g, 2)
                if has_f:
                    h = g - 1
                    k = 3 * h
                    pool.tensor_tensor(var2[:, :], rstd[2][:, :], rstd[2][:, :], ALU.mult).then_inc(s["rstd2_step"], 1)
                    wait_alone(pool, s["rstd2_step"], k + 1)
                    pool.tensor_tensor(rstd2[:, :], var2[:, :], moments[2][:, :, 1], ALU.mult).then_inc(s["rstd2_step"], 1)
                    wait_alone(pool, s["rstd2_step"], k + 2)
                    pool.tensor_scalar(var2[:, :], rstd2[:, :], 1.0, EPS, ALU.mult, ALU.add).then_inc(s["rstd2_step"], 1)
                    wait_alone(pool, s["rstd2_step"], k + 3)
                    pool.tensor_tensor(rstd2[:, :], var2[:, :], minus_half[:, :], ALU.pow).then_inc(s["rstd2_ready"], 1)
                    if not isinstance(h, int) or h >= 1:
                        wait_alone(pool, s["pay_stored"], 16 * h)
                    wait_alone(pool, s["feats_ready"], h + 1)
                    pool.tensor_tensor(pay[:, :, D:2 * D], grouped(at(x2, half(h) * GS, GS)), grouped(feats[:, :]),
                                       ALU.add).then_inc(s["base_ready"], 1)
                    wait_alone(pool, s["rstd2_ready"], h + 1)
                    pool.tensor_tensor(pay[:, :, 0:D], grouped(feats[:, :]),
                                       spread(rstd2[:, :].rearrange("p (g a) -> p g a", a=1), [128, G, S]),
                                       ALU.mult).then_inc(s["pay_ready"], 1)
                if has_c:
                    add_attended(g, 3)

            wait_alone(pool, s["weights_loaded"], N_WEIGHTS)
            passes(pool, run)
            ffn_pool(pool)

        @block.vector
        def _(dve):
            dve.wait_ge(s["weights_loaded"], N_WEIGHTS)
            dve.tensor_copy(bv_cols[:, :], spread(bv_col[:, 0:1], [128, 128])).then_inc(s["bv_made"], 1)
            dve.wait_ge(s["wvo_done"], 1)
            dve.tensor_copy(wvo_t[:, :], self_bank[:, 0:D]).then_inc(s["wvo_ready"], 1)
            dve.tensor_copy(bvo_rows[:, :], self_bank[:, D:2 * D]).then_inc(s["wvo_ready"], 1)

            def topk(g, r):
                for b in range(G):
                    src = scores if r == 0 else left
                    if r == 0 and b == 0:
                        wait_alone(dve, s["scores_ready"], g + 1)
                    elif r > 0:
                        wait_alone(dve, s["topk_step"], 32 * g + 8 * (r - 1) + 4 + b + 1)
                    dve.max(best8[:, b, r, :], at(src, b * S, S)).then_inc(s["topk_step"], 1)
                for b in range(G):
                    src = scores if r == 0 else left
                    wait_alone(dve, s["topk_step"], 32 * g + 8 * r + b + 1)
                    dve.match_replace(at(left, b * S, S), best8[:, b, r, :], at(src, b * S, S), TAKEN)\
                       .then_inc(s["topk_step"], 1)

            def head_max(g, j, u):
                n = 2 * (G * g + j) + u
                dve.wait_ge(s["s1_done"], n + 1)
                if u == 0 and (not isinstance(g, int) or G * g + j >= 2):
                    dve.wait_ge(s["hmax_split"], G * g + j - 1)
                dve.tensor_reduce(neg_hmax[:, j % 2, u * 8:u * 8 + 8],
                                  s1_bank[:, :].rearrange("p (h k) -> p h k", k=S), AX.X, ALU.max,
                                  negate=True).then_inc(s["s1_max"], 1)

            def normalise(g, j):
                n = G * g + j
                pv = pv_bank[:, 0:H * HC].rearrange("p (h c) -> p h c", c=HC)
                dve.wait_ge(s["pv_half"], 2 * n + 2)
                dve.reciprocal(wsum_inv[:, :], pv[:, :, HD]).then_inc(s["wsum_inv_ready"], 1)
                dve.wait_ge(s["wsum_inv_ready"], n + 1)
                if not isinstance(g, int) or n >= 2:
                    dve.wait_ge(s["x2_ready"], n - 1)
                dve.tensor_tensor(attended[:, j % 2, :].rearrange("p (h d) -> p h d", d=HD), pv[:, :, 0:HD],
                                  spread(wsum_inv[:, :].rearrange("p (h a) -> p h a", a=1), [128, H, HD]),
                                  ALU.mult).then_inc(s["attended_ready"], 1)

            def run(g):
                has_f, has_c, has_e, has_s = stages(g)
                if has_e:
                    h = g + 1
                    wait_alone(dve, s["topk_step"], 32 * h + 29)
                    dve.tensor_scalar(neg_max[:, :], best8[:, :, 0, 0], -SELF_SCALE, None, ALU.mult)\
                       .then_inc(s["neg_max_ready"], 1)
                if has_s:
                    norm_stats(dve, 0, x_in, ((g + 2) % 4) * GS, g + 2, "x_loaded", 16 * (g + 3))
                    norm_moments(dve, 0, g + 2)
                if has_c:
                    head_max(g, 0, 0)
                if has_f:
                    norm_stats(dve, 2, x2, half(g - 1) * GS, g - 1, "x2_ready", G * g)
                    if not isinstance(g, int) or g >= 2:
                        dve.wait_ge(s["rstd2_ready"], g - 1)
                    norm_moments(dve, 2, g - 1)
                if has_c:
                    head_max(g, 0, 1)
                if has_e:
                    h = g + 1
                    wait_alone(dve, s["topk_step"], 32 * h + 32)
                    if not isinstance(h, int) or h >= 1:
                        dve.wait_ge(s["probs_n_ready"], G * h)
                    for b in range(G):
                        dve.wait_ge(s["self_exp"], G * h + b + 1)
                        dve.scalar_tensor_tensor(at(probs, b * S, S), at(left, b * S, S), TAKEN, at(expd, b * S, S),
                                                 ALU.is_equal, ALU.mult, accum_out=prob_sum[:, b:b + 1])\
                           .then_inc(s["probs_ready"], 1)
                    dve.wait_ge(s["probs_ready"], G * h + G)
                    dve.reciprocal(prob_inv[:, :], prob_sum[:, :]).then_inc(s["inv_ready"], 1)
                    dve.wait_ge(s["inv_ready"], h + 1)
                    if not isinstance(h, int) or h >= 1:
                        dve.wait_ge(s["probs_transposed"], h)
                    for b in range(G):
                        dve.tensor_scalar(at(probs_n, b * S, S), at(probs, b * S, S), prob_inv[:, b:b + 1], 0.0,
                                          ALU.mult, ALU.max).then_inc(s["probs_n_ready"], 1)
                if has_c:
                    head_max(g, 1, 0)
                    head_max(g, 1, 1)
                if has_e:
                    h = g + 1
                    dve.wait_ge(s["attn_done"], h + 1)
                    dve.wait_ge(s["x_bo_ready"], h + 1)
                    if not isinstance(h, int) or h >= 1:
                        dve.wait_ge(s["x1_bv_ready"], h)
                    dve.tensor_tensor(x1[:, :], cross_bank[:, :], x_bo[:, :], ALU.add).then_inc(s["x1_ready"], 1)
                    norm_stats(dve, 1, x1, 0, h, "x1_ready", h + 1)
                    norm_moments(dve, 1, h)
                if has_c:
                    normalise(g, 0)
                if has_s:
                    topk(g + 2, 0)
                if has_c:
                    head_max(g, 2, 0)
                if has_s:
                    topk(g + 2, 1)
                if has_c:
                    head_max(g, 2, 1)
                    normalise(g, 1)
                if has_s:
                    h = g + 2
                    dve.wait_ge(s["v_done"], h + 1)
                    if not isinstance(h, int) or h >= 2:
                        dve.wait_ge(s["attn_done"], h - 1)
                    if isinstance(h, int) and h == 0:
                        dve.wait_ge(s["wvo_ready"], 2)
                    dve.tensor_tensor(grouped(at(v, half(h) * GS, GS)), grouped(self_bank[:, :]),
                                      spread(bvo_rows[:, :].rearrange("p (a n) -> p a n", a=1), [128, G, S]),
                                      ALU.add).then_inc(s["v_ready"], 1)
                if has_c:
                    head_max(g, 3, 0)
                if has_s:
                    topk(g + 2, 2)
                if has_c:
                    head_max(g, 3, 1)
                    normalise(g, 2)
                if has_s:
                    topk(g + 2, 3)
                if has_f:
                    h = g - 1
                    dve.wait_ge(s["aff_done"], h + 1)
                    dve.tensor_copy(aff[:, ds(h * G, G), :],
                                    small_bank[:, 256:256 + G * E].rearrange("p (b e) -> p b e", e=E))\
                       .then_inc(s["aff_ready"], 1)
                    wait_alone(dve, s["aff_ready"], h + 1)
                    if not isinstance(h, int) or h >= 1:
                        wait_alone(dve, s["aff_exp_ready"], h)
                    dve.tensor_reduce(aff_max[:, :], aff[:, ds(h * G, G), :], AX.X, ALU.max).then_inc(s["aff_max_ready"], 1)
                    dve.wait_ge(s["aff_exp_ready"], h + 1)
                    dve.tensor_scalar(aff_den[:, :], aff_exp[:, :], 1.0, None, ALU.add).then_inc(s["aff_den_ready"], 1)
                    dve.wait_ge(s["aff_den_ready"], h + 1)
                    if not isinstance(h, int) or h >= 1:
                        dve.wait_ge(s["pay_stored"], 16 * h)
                    dve.reciprocal(pay[:, :, 2 * D], aff_den[:, :]).then_inc(s["alpha_ready"], 1)
                if has_c:
                    normalise(g, 3)

            passes(dve, run)
            route_vector(dve)

        @block.scalar
        def _(act):
            act.wait_ge(s["weights_loaded"], N_WEIGHTS)

            def evacuate(dst, bank, done, count, ready, bias=None):
                act.wait_ge(s[done], count)
                if bias is None:
                    act.activation(dst, bank, ACT.Copy).then_inc(s[ready], 1)
                else:
                    act.activation(dst, bank, ACT.Identity, bias=bias_cols[:, bias:bias + 1]).then_inc(s[ready], 1)

            def exps(g, j, u):
                n = 2 * (G * g + j) + u
                act.wait_ge(s["s2_done"], n + 1)
                if not isinstance(g, int) or n >= 2:
                    act.wait_ge(s["pv_half"], n - 1)
                act.activation(weights[:, u, :], s2_bank[:, :], ACT.Exp, scale=HEAD_SCALE).then_inc(s["s2_exp"], 1)

            def hmax_out(g, j):
                n = G * g + j
                if not isinstance(g, int) or n >= 2:
                    act.wait_ge(s["s2_done"], 2 * (n - 1))
                evacuate(hmax_t[:, j % 2, :], small_bf[:, 0:128], "hmax_transposed", n + 1, "hmax_t_ready")

            def run(g):
                has_f, has_c, has_e, has_s = stages(g)
                if has_e:
                    h = g + 1
                    act.wait_ge(s["neg_max_ready"], h + 1)
                    if not isinstance(h, int) or h >= 1:
                        act.wait_ge(s["probs_ready"], G * h)
                    for b in range(G):
                        act.activation(at(expd, b * S, S), at(scores, b * S, S), ACT.Exp, bias=neg_max[:, b:b + 1],
                                       scale=SELF_SCALE).then_inc(s["self_exp"], 1)
                    evacuate(ctx_t[:, :], cross_bank[:, :], "ctx_transposed", h + 1, "ctx_t_ready")
                    if not isinstance(h, int) or h >= 1:
                        act.wait_ge(s["xk_split"], h)
                        act.wait_ge(s["xk_stored"], 16 * h)
                    evacuate(xk[:, :], cross_bank[:, :], "xk_done", h + 1, "xk_ready", 3)
                    act.activation(xk_parts[:, 0, :], cross_bank[:, :], ACT.Identity, bias=bias_cols[:, 3:4])\
                       .then_inc(s["xk_ready"], 1)
                if has_c:
                    hmax_out(g, 0)
                if has_e:
                    if not isinstance(g, int) or g >= 1:
                        act.wait_ge(s["pv_half"], 2 * G * g)
                    act.wait_ge(s["xv_done"], g + 2)
                    act.activation(at(xv, half(g + 1) * G * H * HC, G * H * HC)
                                   .rearrange("p (n c) -> p n c", c=HC)[:, :, 0:HD],
                                   cross_bank[:, :].rearrange("p (n c) -> p n c", c=HD), ACT.Copy)\
                       .then_inc(s["xv_ready"], 1)
                if has_s:
                    evacuate(xn_t[:, :], self_bank[:, :], "xn_transposed", g + 3, "xn_t_ready")
                if has_c:
                    exps(g, 0, 0)
                if has_s:
                    evacuate(q_t[:, :], self_bank[:, :], "q_done", g + 3, "q_ready", 0)
                if has_e:
                    evacuate(probs_t[:, :], cross_bank[:, :], "probs_transposed", g + 2, "probs_t_ready")
                if has_c:
                    exps(g, 0, 1)
                if has_s:
                    evacuate(k_t[:, :], self_bank[:, :], "k_done", g + 3, "k_ready", 1)
                if has_c:
                    hmax_out(g, 1)
                    exps(g, 1, 0)
                if has_s:
                    act.wait_ge(s["topk_step"], 32 * (g + 2))
                    evacuate(scores[:, :], self_bank[:, :], "scores_done", g + 3, "scores_ready")
                if has_c:
                    exps(g, 1, 1)
                if has_e:
                    evacuate(xn2_t[:, :], cross_bank[:, :], "xn2_transposed", g + 2, "xn2_t_ready")
                if has_c:
                    hmax_out(g, 2)
                if has_e:
                    h = g + 1
                    if not isinstance(h, int) or h >= 1:
                        act.wait_ge(s["xq_split"], h)
                        act.wait_ge(s["xq_stored"], 16 * h)
                    evacuate(xq[:, :], cross_bank[:, :], "xq_done", h + 1, "xq_ready", 2)
                    act.activation(xq_parts[:, 0, :], cross_bank[:, :], ACT.Identity, bias=bias_cols[:, 2:3])\
                       .then_inc(s["xq_ready"], 1)
                if has_c:
                    exps(g, 2, 0)
                    exps(g, 2, 1)
                    hmax_out(g, 3)
                if has_f:
                    evacuate(feats_t[:, :], cross_bank[:, :], "feats_transposed", g, "feats_t_ready")
                if has_c:
                    exps(g, 3, 0)
                    exps(g, 3, 1)
                if has_f:
                    act.wait_ge(s["aff_max_ready"], g)
                    act.activation(aff_exp[:, :], aff_max[:, :], ACT.Exp, scale=-1.0).then_inc(s["aff_exp_ready"], 1)

            passes(act, run)
            ffn_scalar(act)

        @block.tensor
        def _(pe):
            def transposed(src, bank, g, ready, count, done):
                pe.wait_ge(s[ready], count)
                for b in range(G):
                    m = pe.transpose(bank[:, b * S:(b + 1) * S], src(b), ident[:, :])
                m.then_inc(s[done], 1)

            def project(bank, w, src, ready, count, done):
                pe.wait_ge(s[ready], count)
                pe.matmul(bank[:, :], w[:, :], src[:, :], start=True, stop=True).then_inc(s[done], 1)

            def s1(g, j, u):
                n = 2 * (G * g + j) + u
                if not isinstance(g, int) or n >= 1:
                    pe.wait_ge(s["s1_max"], n)
                if j == 0 and u == 0:
                    pe.wait_ge(s["xq_stacked"], 144 * (g + 1))
                    pe.wait_ge(s["xk_stacked"], 144 * (g + 1))
                for i in range(8):
                    o = half(g) * H * GS + (u * 8 + i) * GS + j * S
                    m = pe.matmul(s1_bank[:, i * S:(i + 1) * S], at(q_stack, o, S, STK), at(k_stack, o, S, STK),
                                  start=True, stop=True)
                m.then_inc(s["s1_done"], 1)

            def s2(g, j, u):
                n = 2 * (G * g + j) + u
                if not isinstance(g, int) or n >= 1:
                    pe.wait_ge(s["s2_exp"], n)
                if u == 0:
                    pe.wait_ge(s["hmax_t_ready"], G * g + j + 1)
                for i in range(8):
                    o = half(g) * H * GS + (u * 8 + i) * GS + j * S
                    pe.matmul(s2_bank[:, i * S:(i + 1) * S], at(k_stack, o, S, STK), at(q_stack, o, S, STK),
                              start=True, stop=False)
                    m = pe.matmul(s2_bank[:, i * S:(i + 1) * S], head_sel[:, u * 8 + i, :], hmax_t[:, j % 2, :],
                                  start=False, stop=True)
                m.then_inc(s["s2_done"], 1)

            def hmax_rows(g, j):
                n = G * g + j
                pe.wait_ge(s["hmax_split"], n + 1)
                if not isinstance(g, int) or n >= 1:
                    pe.wait_ge(s["hmax_t_ready"], n)
                if j == 0 and (not isinstance(g, int) or g >= 2):
                    pe.wait_ge(s["aff_ready"], g - 1)
                pe.transpose(small_bf[:, 0:128], hmax_parts[:, j % 2, :], ident_bf[:, :]).then_inc(s["hmax_transposed"], 1)

            def pv(g, j, u):
                n = G * g + j
                pe.wait_ge(s["s2_exp"], 2 * n + u + 1)
                if u == 0 and (not isinstance(g, int) or n >= 1):
                    pe.wait_ge(s["attended_ready"], n)
                if u == 0 and j == 0:
                    pe.wait_ge(s["xv_ready"], g + 1)
                for i in range(8):
                    h = u * 8 + i
                    m = pe.matmul(pv_bank[:, h * HC:(h + 1) * HC], weights[:, u, i * S:(i + 1) * S],
                                  at(xv, half(g) * G * H * HC + (j * H + h) * HC, HC), start=True, stop=True)
                m.then_inc(s["pv_half"], 1)

            def run(g):
                has_f, has_c, has_e, has_s = stages(g)
                if has_c:
                    s1(g, 0, 0)
                if has_e:
                    h = g + 1
                    pe.wait_ge(s["ctx_loaded"], 16 * (h + 1))
                    if not isinstance(h, int) or h >= 1:
                        pe.wait_ge(s["xq_ready"], 2 * h)
                    if not isinstance(h, int) or h >= 3:
                        pe.wait_ge(s["feats_t_ready"], h - 2)
                    transposed(lambda b: ctx_in[:, b * S:(b + 1) * S], cross_bank, h, "consts_made", 11, "ctx_transposed")
                    project(cross_bank, xwk_t, ctx_t, "ctx_t_ready", h + 1, "xk_done")
                if has_c:
                    s1(g, 0, 1)
                if has_e:
                    pe.wait_ge(s["xk_ready"], 2 * h + 2)
                    for b in range(G):
                        m = pe.matmul(cross_bank[:, b * D:(b + 1) * D], ctx_t[:, b * S:(b + 1) * S], xwv_t[:, :],
                                      start=True, stop=True)
                    m.then_inc(s["xv_done"], 1)
                if has_c:
                    hmax_rows(g, 0)
                if has_s:
                    h = g + 2
                    if not isinstance(h, int) or h >= 1:
                        pe.wait_ge(s["v_ready"], h)
                    transposed(lambda b: xn[:, b * S:(b + 1) * S], self_bank, h, "xn_ready", h + 1, "xn_transposed")
                if has_c:
                    s2(g, 0, 0)
                    s1(g, 1, 0)
                if has_s:
                    project(self_bank, wq_t, xn_t, "xn_t_ready", h + 1, "q_done")
                if has_c:
                    pv(g, 0, 0)
                if has_e:
                    h = g + 1
                    pe.wait_ge(s["xv_ready"], h + 1)
                    transposed(lambda b: probs_n[:, b * S:(b + 1) * S], cross_bank, h, "probs_n_ready", G * h + G,
                               "probs_transposed")
                if has_c:
                    s2(g, 0, 1)
                    s1(g, 1, 1)
                if has_s:
                    h = g + 2
                    pe.wait_ge(s["q_ready"], h + 1)
                    project(self_bank, wk_t, xn_t, "xn_t_ready", h + 1, "k_done")
                if has_c:
                    pv(g, 0, 1)
                if has_e:
                    h = g + 1
                    pe.wait_ge(s["probs_t_ready"], h + 1)
                    pe.wait_ge(s["v_ready"], h + 1)
                    for b in range(G):
                        m = pe.matmul(cross_bank[:, b * D:(b + 1) * D], probs_t[:, b * S:(b + 1) * S],
                                      at(v, half(h) * GS + b * D, D), start=True, stop=True)
                    m.then_inc(s["attn_done"], 1)
                if has_c:
                    hmax_rows(g, 1)
                    s2(g, 1, 0)
                if has_s:
                    h = g + 2
                    pe.wait_ge(s["k_ready"], h + 1)
                    for b in range(G):
                        m = pe.matmul(self_bank[:, b * S:(b + 1) * S], q_t[:, b * S:(b + 1) * S],
                                      k_t[:, b * S:(b + 1) * S], start=True, stop=True)
                    m.then_inc(s["scores_done"], 1)
                if has_c:
                    s1(g, 2, 0)
                    pv(g, 1, 0)
                    s2(g, 1, 1)
                    s1(g, 2, 1)
                if has_e:
                    h = g + 1
                    pe.wait_ge(s["x1_ready"], h + 1)
                    transposed(lambda b: xn2[:, b * S:(b + 1) * S], cross_bank, h, "xn2_ready", h + 1, "xn2_transposed")
                if has_c:
                    pv(g, 1, 1)
                    hmax_rows(g, 2)
                if has_e:
                    project(cross_bank, xwq_t, xn2_t, "xn2_t_ready", g + 2, "xq_done")
                if has_c:
                    s2(g, 2, 0)
                if has_s:
                    h = g + 2
                    pe.wait_ge(s["scores_ready"], h + 1)
                    if isinstance(h, int) and h == 0:
                        pe.wait_ge(s["wvo_ready"], 2)
                    for b in range(G):
                        m = pe.matmul(self_bank[:, b * D:(b + 1) * D], xn_t[:, b * S:(b + 1) * S], wvo_t[:, :],
                                      start=True, stop=True)
                    m.then_inc(s["v_done"], 1)
                if has_c:
                    s1(g, 3, 0)
                    pv(g, 2, 0)
                    s2(g, 2, 1)
                    s1(g, 3, 1)
                    pv(g, 2, 1)
                    hmax_rows(g, 3)
                    s2(g, 3, 0)
                if has_f:
                    h = g - 1
                    if has_e:
                        pe.wait_ge(s["xq_ready"], 2 * (g + 2))
                    transposed(lambda b: feats[:, b * S:(b + 1) * S], cross_bank, h, "feats_ready", h + 1, "feats_transposed")
                if has_c:
                    pv(g, 3, 0)
                    s2(g, 3, 1)
                if has_f:
                    h = g - 1
                    pe.wait_ge(s["feats_t_ready"], h + 1)
                    if has_c:
                        pe.wait_ge(s["hmax_t_ready"], G * g + G)
                    if not isinstance(h, int) or h >= 1:
                        pe.wait_ge(s["aff_ready"], h)
                    for b in range(G):
                        m = pe.matmul(small_bank[:, 256 + b * E:256 + (b + 1) * E], feats_t[:, b * S:(b + 1) * S],
                                      cent_t[:, :], start=True, stop=True)
                    m.then_inc(s["aff_done"], 1)
                if has_c:
                    pv(g, 3, 1)

            pe.wait_ge(s["weights_loaded"], N_WEIGHTS)
            pe.matmul(self_bank[:, 0:D], wv[:, :], wo_t[:, :], start=True, stop=True)
            pe.wait_ge(s["bv_made"], 1)
            pe.matmul(self_bank[:, D:2 * D], bv_cols[:, :], wo_t[:, :], start=True, stop=True).then_inc(s["wvo_done"], 1)
            pe.wait_ge(s["wvo_ready"], 2)
            pe.wait_ge(s["sel_made"], NPART)
            pe.wait_ge(s["ones_made"], 2)
            passes(pe, run)
            ffn_tensor(pe)



_TRANSPOSED = {"wq_t": "L0_attn_Wq", "wk_t": "L0_attn_Wk", "wo_t": "L0_attn_Wo",
               "xwq_t": "L0_xattn_Wq", "xwk_t": "L0_xattn_Wk", "xwv_t": "L0_xattn_Wv",
               "cent_t": "L0_ffn_centroids", "gamma_t": "L0_ffn_gamma", "beta_t": "L0_ffn_beta"}
_PLAIN = {"x": "x", "ctx_1024": "ctx_1024", "wv": "L0_attn_Wv", "bq": "L0_attn_bq", "bk": "L0_attn_bk",
          "bv": "L0_attn_bv", "bo": "L0_attn_bo", "xbq": "L0_xattn_bq", "xbk": "L0_xattn_bk", "xbv": "L0_xattn_bv",
          "w1": "L0_ffn_w1", "b1": "L0_ffn_b1", "w2": "L0_ffn_w2", "b2": "L0_ffn_b2"}


def kernel(**inputs):
    import concourse.bacc as bacc
    from concourse.bass_utils import run_bass_kernel_spmd

    nc = bacc.Bacc("TRN2", target_bir_lowering=False, num_devices=1)
    arrays, tensors = {}, {}
    for name, source in list(_PLAIN.items()) + list(_TRANSPOSED.items()):
        a = np.asarray(inputs[source])
        a = np.ascontiguousarray(a.T if name in _TRANSPOSED else a)
        arrays[f"in_{name}"] = a
        tensors[name] = nc.dram_tensor(f"in_{name}", a.shape, mybir.dt.from_np(a.dtype), kind="ExternalInput").ap()
    out = nc.dram_tensor("out", tensors["x"].shape, mybir.dt.float32, kind="ExternalOutput").ap()
    preln_decoder_kernel(nc, tensors, out)
    result = run_bass_kernel_spmd(nc, [arrays], core_ids=[0])
    return result.results[0]["out"]
```

```python
import numpy as np
import concourse.bass as bass
from concourse import mybir
from contextlib import ExitStack


def preln_decoder_kernel(nc, T, out):
    F32 = mybir.dt.float32
    BF16 = mybir.dt.bfloat16
    I32 = mybir.dt.int32
    U32 = mybir.dt.uint32
    ALU = mybir.AluOpType
    ACT = mybir.ActivationFunctionType
    AX = mybir.AxisListType
    ds = bass.ds

    B, S, D = T["x"].shape
    E, _, F = T["w1"].shape
    H, HD = 16, 8
    G = 4
    NG = B // G
    GS = G * S
    TOPK = 32
    NPART = 3
    STK = NPART * NPART * HD
    HC = HD + 1
    FC = F // 128
    NTILE = B * S // 128 + E - 1
    NTC = NTILE + 1
    PAY = 2 * D + 4
    TAKEN = -3.0e38
    EPS = 1e-5
    SELF_SCALE = 1.0 / float(np.sqrt(D))
    HEAD_SCALE = 1.0 / float(np.sqrt(HD))
    Q_PIECES = ((0, 0, 3), (3, 0, 3), (6, 0, 3))
    K_PIECES = ((0, 0, 3), (3, 1, 2), (5, 0, 1), (6, 2, 1), (7, 0, 2))
    RING = 6

    q_scratch = nc.dram_tensor("q_parts", [H, NPART, HD, GS], BF16, kind="Internal").ap()
    k_scratch = nc.dram_tensor("k_parts", [H, NPART, HD, GS], BF16, kind="Internal").ap()
    rows = nc.dram_tensor("routed_rows", [B * S, PAY], F32, kind="Internal").ap()
    out_rows = out.rearrange("b s d -> (b s) d")

    with ExitStack() as stack:
        def sb(name, shape, dt=F32):
            return stack.enter_context(nc.sbuf_tensor(name, shape, dt))

        def ps(name, shape, dt=F32):
            return stack.enter_context(nc.psum_tensor(name, shape, dt))

        def sem(name):
            return stack.enter_context(nc.semaphore(name))

        ident = sb("ident", [128, 128])
        ident_bf = sb("ident_bf", [128, 128], BF16)
        head_sel = sb("head_sel", [128, H, 128], BF16)
        minus_half = sb("minus_half", [128, G])
        wq_t, wk_t, wv, wo_t, wvo_t = (sb(n, [128, D]) for n in ("wq_t", "wk_t", "wv", "wo_t", "wvo_t"))
        xwq_t, xwk_t, xwv_t = (sb(n, [128, D]) for n in ("xwq_t", "xwk_t", "xwv_t"))
        cent_t = sb("cent_t", [128, E])
        gamma_t = sb("gamma_t", [128, E])
        beta_t = sb("beta_t", [128, E])
        bias_cols = sb("bias_cols", [128, 4])
        bv_col = sb("bv_col", [128, 1])
        bv_cols = sb("bv_cols", [128, 128])
        bo_rows = sb("bo_rows", [128, D])
        xbv_rows = sb("xbv_rows", [128, D])
        bvo_rows = sb("bvo_rows", [128, D])
        w1 = sb("w1", [128, E * F])
        w2 = sb("w2", [128, E * FC * D])
        x_in = sb("x_in", [128, 4 * GS])
        ctx_in = sb("ctx_in", [128, GS])
        stats = [sb(f"stats_{i}", [128, G, 6]) for i in range(3)]
        moments = [sb(f"moments_{i}", [128, G, 2]) for i in range(3)]
        var_eps = [sb(f"var_eps_{i}", [128, G]) for i in range(3)]
        rstd = [sb(f"rstd_{i}", [128, G]) for i in range(3)]
        centred = sb("centred", [128, GS])
        self_room = sb("self_room", [128, 10 * GS])
        xn, xn_t, q_t, k_t, scores, left, expd, probs, probs_n, probs_t = (
            self_room[:, n * GS:(n + 1) * GS] for n in range(10))
        v = sb("v", [128, 2 * GS])
        best8 = sb("best8", [128, G, TOPK // 8, 8])
        neg_max = sb("neg_max", [128, G])
        prob_sum = sb("prob_sum", [128, G])
        prob_inv = sb("prob_inv", [128, G])
        x_bo = sb("x_bo", [128, GS])
        x1 = sb("x1", [128, GS])
        x1_bv = sb("x1_bv", [128, 4 * GS])
        xn2 = sb("xn2", [128, GS])
        xq = sb("xq", [128, GS])
        xq_parts = sb("xq_parts", [128, NPART, GS], BF16)
        ctx_t = sb("ctx_t", [128, GS])
        xn2_t = ctx_t
        xk = sb("xk", [128, GS])
        rest = sb("rest", [128, GS])
        xk_parts = sb("xk_parts", [128, NPART, GS], BF16)
        xv = sb("xv", [128, 4 * G * H * HC])
        q_stack = sb("q_stack", [128, 2 * H * GS], BF16)
        k_stack = sb("k_stack", [128, 2 * H * GS], BF16)
        neg_hmax = sb("neg_hmax", [128, 2 * H])
        hmax_parts = sb("hmax_parts", [128, 2 * 128], BF16)
        hmax_t = sb("hmax_t", [128, 2 * 128], BF16)
        weights = sb("weights", [128, 4, GS])
        wsum_inv = sb("wsum_inv", [128, H])
        attended = sb("attended", [128, 2 * H * HD])
        x2 = sb("x2", [128, 2 * GS])
        feats = sb("feats", [128, GS])
        feats_t = sb("feats_t", [128, GS])
        var2 = sb("var2", [128, G])
        rstd2 = sb("rstd2", [128, G])
        pay = sb("pay", [128, G, PAY])
        aff = sb("aff", [128, B, E])
        aff_max = sb("aff_max", [128, G])
        aff_exp = sb("aff_exp", [128, G])
        aff_den = sb("aff_den", [128, G])

        iota_i = sb("iota_i", [128, 128], I32)
        iota_f = sb("iota_f", [128, 128])
        place_i = sb("place_i", [128, 1], I32)
        place_f = sb("place_f", [128, 1])
        earlier = sb("earlier", [128, 128], BF16)
        all_ones = sb("all_ones", [128, 128], BF16)
        tile_expert = sb("tile_expert", [128, NTC], I32)
        gather_idx = sb("gather_idx", [128, NTC], I32)
        scatter_idx = sb("scatter_idx", [128, NTC], I32)
        index_now = sb("index_now", [128, RING, 2], I32)

        room = {"q": [q_stack[:, :].bitcast(F32), 0], "k": [k_stack[:, :].bitcast(F32), 0]}

        def carve(which, n, dt=F32):
            words = n if dt == F32 or dt == I32 else n // 2
            ap, at0 = room[which]
            room[which][1] = at0 + words
            assert at0 + words <= H * GS
            piece = ap[:, at0:at0 + words]
            return piece if dt == F32 else piece.bitcast(dt)

        ffn_row = [carve("q", PAY) for _ in range(RING)]
        ffn_row_t = [carve("k", D) for _ in range(2)]
        ffn_hid = [carve("q", F) for _ in range(2)]
        ffn_relu = [carve("q", F) for _ in range(2)]
        ffn_y = [carve("q", D) for _ in range(2)]
        ffn_out = [x_in[:, (E + n) * D:(E + n + 1) * D] for n in range(RING)]
        b1_rows = self_room[:, 0:E * F]
        beta_cols = self_room[:, E * F:E * F + E * 128]
        b2_rows = x_in[:, 0:E * D]
        lo_hot = carve("k", B * 128, BF16)
        hi_hot = carve("k", B * 2 * NTC, BF16)
        onehot = carve("k", E * B, BF16)

        s1_bank = ps("s1_bank", [128, 1024])
        s2_bank = ps("s2_bank", [128, 1024])
        pv_bank = ps("pv_bank", [128, 1024])
        self_bank = ps("self_bank", [128, 512])
        cross_bank = ps("cross_bank", [128, 512])
        hmax_bank = s1_bank[:, 512:576].bitcast(BF16)
        AFF = 896

        names = """x_loaded ctx_loaded attn_loaded cross_loaded ffn_loaded consts_made sel_made
            ln0_stats ln0_moments ln0_var ln0_rstd ln0_centred xn_ready
            ln1_stats ln1_moments ln1_var ln1_rstd ln1_centred xn2_ready
            ln2_stats ln2_moments ln2_var ln2_rstd ln2_centred feats_ready
            xn_transposed xn_t_ready q_done q_ready k_done k_ready v_done v_ready scores_done scores_ready
            topk_step neg_max_ready self_exp probs_ready inv_ready probs_n_ready probs_transposed probs_t_ready
            attn_done x_bo_ready x1_ready x1_bv_ready
            xn2_transposed xn2_t_ready xq_done xq_ready xq_rest_ready xq_part1 xq_split xq_stored xq_stacked
            ctx_transposed ctx_t_ready xk_done xk_ready xk_rest_ready xk_part1 xk_split xk_stored xk_stacked xv_done xv_ready ones_made
            s1_done s1_max hmax_step hmax_split hmax_transposed hmax_t_ready s2_done s2_exp pv_done
            wsum_inv_ready attended_ready x2_ready
            feats_transposed feats_t_ready aff_done aff_ready aff_max_ready aff_exp_ready aff_den_ready alpha_ready
            rstd2_step rstd2_ready base_ready pay_ready pay_stored bv_made xk_zeroed xq_zeroed wvo_done wvo_ready
            beta_made b1_done b1_ready w1_scaled iota_made
            route_step onehot_ready counts_done slots_ready tok_done tok_ready experts_ready
            row_transposed row_t_ready hid_done hid_ready hid_transposed relu_ready
            y_done y_biased result_ready
            """.split()
        s = {n: sem(n) for n in names}
        s["index_copied"] = [sem("gather_index_copied"), sem("scatter_index_copied")]
        row_gathered = [sem(f"row_gathered_{r}") for r in range(RING)]
        row_scattered = [sem(f"row_scattered_{r}") for r in range(RING)]
        block = stack.enter_context(nc.Block())

        N_ATTN = 16 * 8
        N_CROSS = 16 * 9
        N_FFN = 16 * (2 * E + 2)

        def wait_alone(eng, semaphore, n):
            eng.wait_ge(semaphore, n)
            if not isinstance(n, int):
                eng.nop(nofuse=True)

        def at(t, start, n, p=128):
            return t[0:p, ds(start, n)]

        def grouped(ap):
            return ap.rearrange("p (g n) -> p g n", g=G)

        def spread(ap, shape):
            return ap.to_broadcast(shape)

        def passes(eng, run):
            for g in range(-3, 2):
                run(g)
            with eng.Fori(2, NG - 4) as g:
                run(g)
            for g in range(NG - 4, NG + 1):
                run(g)

        def stages(g):
            if not isinstance(g, int):
                return True, True, True, True
            return 0 <= g - 1, 0 <= g < NG, 0 <= g + 2 < NG, g + 3 < NG

        def half(g):
            return g % 2

        def later(g, first):
            return not isinstance(g, int) or g >= first

        be = lambda ap: ap.rearrange("p (b e) -> p b e", e=E)
        eb = lambda ap: ap.rearrange("p (e b) -> p e b", b=B)
        chosen = carve("k", B * E)
        most = carve("k", B)
        counts = carve("k", 2 * E * B)
        running = carve("k", E * B)
        per_expert = carve("k", E)
        passed = carve("k", E * B)
        tiles_of = carve("k", E)
        tiles_end = carve("k", E)
        shift_of = carve("k", E)
        ones_f = carve("k", E * B)
        slot = carve("k", B)
        slot_i = carve("k", B, I32)
        hi_i = carve("k", B, I32)
        lo_i = carve("k", B, I32)
        hi_f = carve("k", B)
        lo_f = carve("k", B)
        hi_eq = carve("k", B * NTC, BF16)
        after = carve("k", NTC * E)
        expert_f = carve("k", NTC)
        token_f = carve("k", NTC)
        empty_f = carve("k", NTC)
        index_f = carve("k", NTC)

        LO_CHUNK = 8

        def route_vector(dve):
            step = [0]

            def link(ins):
                step[0] += 1
                ins.then_inc(s["route_step"], 1)
                dve.wait_ge(s["route_step"], step[0])

            dve.wait_ge(s["aff_ready"], NG)
            dve.wait_ge(s["iota_made"], 4)
            dve.wait_ge(s["attended_ready"], B)
            dve.wait_ge(s["s2_done"], 4 * B)
            link(dve.tensor_reduce(most, aff[:, :, :], AX.X, ALU.max))
            link(dve.tensor_tensor(be(chosen), aff[:, :, :], spread(most.rearrange("p (b a) -> p b a", a=1), [128, B, E]),
                                   ALU.is_equal))
            link(dve.tensor_scalar(per_expert, iota_f[:, 0:E], -1.0, float(E), ALU.mult, ALU.add))
            link(dve.tensor_tensor(be(chosen), be(chosen), spread(per_expert.rearrange("p (a e) -> p a e", a=1), [128, B, E]),
                                   ALU.mult))
            link(dve.tensor_reduce(most, be(chosen), AX.X, ALU.max))
            link(dve.tensor_tensor(onehot.rearrange("p (e b) -> p b e", b=B), be(chosen),
                                   spread(most.rearrange("p (b a) -> p b a", a=1), [128, B, E]), ALU.is_equal))
            dve.memset(ones_f, 1.0).then_inc(s["onehot_ready"], 1)
            dve.wait_ge(s["counts_done"], 1)
            link(dve.tensor_copy(counts, s1_bank[:, 0:2 * E * B]))
            total = counts[:, E * B:2 * E * B]
            dve.wait_ge(s["onehot_ready"], 1)
            link(dve.tensor_tensor_scan(running, ones_f, total, 0.0, ALU.mult, ALU.add))
            link(dve.tensor_reduce(per_expert, eb(total), AX.X, ALU.add))
            link(dve.tensor_scalar(chosen[:, 0:B], iota_f[:, 0:B], 128.0, None, ALU.mult))
            link(dve.tensor_tensor(eb(passed), spread(per_expert.rearrange("p (e a) -> p e a", a=1), [128, E, B]),
                                   spread(chosen[:, 0:B].rearrange("p (a b) -> p a b", a=1), [128, E, B]), ALU.is_gt))
            link(dve.tensor_reduce(tiles_of, eb(passed), AX.X, ALU.add))
            link(dve.tensor_tensor_scan(tiles_end, ones_f[:, 0:E], tiles_of, 0.0, ALU.mult, ALU.add))
            link(dve.tensor_tensor(shift_of, tiles_end, tiles_of, ALU.subtract))
            link(dve.scalar_tensor_tensor(shift_of, shift_of, 128.0, per_expert, ALU.mult, ALU.add))
            link(dve.tensor_tensor(shift_of, shift_of, eb(running)[:, :, B - 1], ALU.subtract))
            link(dve.tensor_tensor(running, running, total, ALU.subtract))
            link(dve.tensor_tensor(running, running, counts[:, 0:E * B], ALU.add))
            link(dve.tensor_tensor(eb(running), eb(running), spread(shift_of.rearrange("p (e a) -> p e a", a=1), [128, E, B]),
                                   ALU.add))
            link(dve.tensor_tensor(running, running, onehot, ALU.mult))
            link(dve.tensor_reduce(slot, running.rearrange("p (e b) -> p b e", b=B), AX.X, ALU.add))
            link(dve.tensor_copy(slot_i, slot))
            link(dve.tensor_scalar(hi_i, slot_i, 7, None, ALU.logical_shift_right))
            link(dve.tensor_scalar(lo_i, slot_i, 127, None, ALU.bitwise_and))
            link(dve.tensor_copy(hi_f, hi_i))
            link(dve.tensor_copy(lo_f, lo_i))
            col = lambda ap: ap.rearrange("p (b a) -> p b a", a=1)
            row = lambda ap: ap.rearrange("p (a n) -> p a n", a=1)
            link(dve.tensor_tensor(hi_eq.rearrange("p (b n) -> p b n", b=B), spread(row(iota_f[:, 0:NTC]), [128, B, NTC]),
                                   spread(col(hi_f), [128, B, NTC]), ALU.is_equal))
            parts = hi_hot.rearrange("p (b k n) -> p b k n", b=B, k=2)
            heq = hi_eq.rearrange("p (b n) -> p b n", b=B)
            dve.tensor_scalar(parts[:, :, 0, :], heq, place_f[:, 0:1], None, ALU.mult).then_inc(s["slots_ready"], 1)
            dve.tensor_tensor(parts[:, :, 1, :], heq, spread(col(iota_f[:, 0:B]), [128, B, NTC]), ALU.mult)\
               .then_inc(s["slots_ready"], 1)
            for b in range(0, B, LO_CHUNK):
                dve.tensor_tensor(lo_hot[:, b * 128:(b + LO_CHUNK) * 128].rearrange("p (b n) -> p b n", b=LO_CHUNK),
                                  spread(row(iota_f[:, :]), [128, LO_CHUNK, 128]),
                                  spread(col(lo_f[:, b:b + LO_CHUNK]), [128, LO_CHUNK, 128]),
                                  ALU.is_equal).then_inc(s["slots_ready"], 1)
            link(dve.tensor_tensor(after.rearrange("p (t e) -> p t e", e=E), spread(col(iota_f[:, 0:NTC]), [128, NTC, E]),
                                   spread(row(tiles_end), [128, NTC, E]), ALU.is_ge))
            link(dve.tensor_reduce(expert_f, after.rearrange("p (t e) -> p t e", e=E), AX.X, ALU.add))
            link(dve.tensor_scalar(expert_f, expert_f, float(E - 1), None, ALU.min))
            dve.tensor_copy(tile_expert[:, :], expert_f).then_inc(s["experts_ready"], 1)
            dve.wait_ge(s["tok_done"], 1)
            link(dve.tensor_copy(token_f, self_bank[:, 0:NTC]))
            link(dve.tensor_scalar(empty_f, token_f, 0.5, float(2 * B * S), ALU.is_lt, ALU.mult))
            link(dve.tensor_scalar(index_f, self_bank[:, NTC:2 * NTC], float(S), -1.0, ALU.mult, ALU.add))
            link(dve.tensor_tensor(token_f, token_f, index_f, ALU.add))
            link(dve.tensor_scalar(index_f, token_f, 0.0, None, ALU.max))
            dve.tensor_copy(gather_idx[:, :], index_f).then_inc(s["tok_ready"], 1)
            link(dve.tensor_tensor(empty_f, empty_f, token_f, ALU.add))
            dve.tensor_copy(scatter_idx[:, :], empty_f).then_inc(s["tok_ready"], 1)
            ffn_vector(dve)

        def tiles(eng, step, first, last):
            for t in range(first, RING):
                step(t // RING, t % RING)
            with eng.Fori(1, NTILE // RING) as i:
                for r in range(RING):
                    step(i, r)
            for t in range(NTILE // RING * RING, last):
                step(t // RING, t % RING)

        def tile(i, r, ahead):
            t = RING * i + r + ahead
            return t, (r + ahead) % RING, not isinstance(i, int) or 0 <= t < NTILE

        def expert_of(eng, t):
            col = tile_expert[0:1, t:t + 1] if isinstance(t, int) else tile_expert[0:1, ds(t, 1)]
            return eng.value_load(col, min_val=0, max_val=E - 1)

        def ffn_tensor(pe):
            pe.wait_ge(s["onehot_ready"], 1)
            pe.wait_ge(s["iota_made"], 4)
            pe.matmul(s1_bank[:, 0:E * B], earlier[:, :], onehot, start=True, stop=True)
            pe.matmul(s1_bank[:, E * B:2 * E * B], all_ones[:, :], onehot, start=True, stop=True)\
              .then_inc(s["counts_done"], 1)
            for b in range(B):
                if b % LO_CHUNK == 0:
                    pe.wait_ge(s["slots_ready"], 3 + b // LO_CHUNK)
                m = pe.matmul(self_bank[:, 0:2 * NTC], lo_hot[:, b * 128:(b + 1) * 128],
                              hi_hot[:, b * 2 * NTC:(b + 1) * 2 * NTC], start=b == 0, stop=b == B - 1)
            m.then_inc(s["tok_done"], 1)
            pe.wait_ge(s["experts_ready"], 1)
            pe.wait_ge(s["b1_ready"], E)
            pe.wait_ge(s["w1_scaled"], E)

            def step(i, r):
                t, k, there = tile(i, r, 1)
                if there:
                    q = t // RING if isinstance(t, int) else (i + (1 if r + 1 >= RING else 0))
                    pe.wait_ge(row_gathered[k], 16 * (q + 1))
                    if not isinstance(i, int) or t >= 1:
                        pe.wait_ge(s["row_t_ready"], t)
                    pe.transpose(cross_bank[:, 0:128], ffn_row[k][:, 0:D], ident[:, :]).then_inc(s["row_transposed"], 1)
                t, k, there = tile(i, r, 0)
                if there:
                    e = expert_of(pe, t)
                    pe.wait_ge(s["row_t_ready"], t + 1)
                    if not isinstance(i, int) or t >= 2:
                        pe.wait_ge(s["hid_ready"], t - 1)
                    pe.matmul(s1_bank[:, (k % 2) * F:(k % 2 + 1) * F], ffn_row_t[k % 2], at(w1, e * F, F),
                              start=True, stop=True).then_inc(s["hid_done"], 1)
                t, k, there = tile(i, r, -1)
                if there:
                    pe.wait_ge(s["hid_ready"], t + 1)
                    if not isinstance(i, int) or t >= 2:
                        pe.wait_ge(s["relu_ready"], t - 1)
                    for c in range(FC):
                        m = pe.transpose(s2_bank[:, (k % 2) * F + c * 128:(k % 2) * F + (c + 1) * 128],
                                         ffn_hid[k % 2][:, c * 128:(c + 1) * 128], ident[:, :])
                    m.then_inc(s["hid_transposed"], 1)
                t, k, there = tile(i, r, -2)
                if there:
                    e = expert_of(pe, t)
                    pe.wait_ge(s["relu_ready"], t + 1)
                    if not isinstance(i, int) or t >= 2:
                        pe.wait_ge(s["y_biased"], t - 1)
                    bank = (pv_bank, self_bank)[k % 2]
                    for c in range(FC):
                        m = pe.matmul(bank[:, 0:D], ffn_relu[k % 2][:, c * 128:(c + 1) * 128],
                                      at(w2, e * (FC * D) + c * D, D), start=c == 0, stop=c == FC - 1)
                    m.then_inc(s["y_done"], 1)

            tiles(pe, step, -1, NTILE + 2)

        def ffn_vector(dve):
            dve.wait_ge(s["b1_ready"], E)

            def step(i, r):
                t, k, there = tile(i, r, 2)
                if there:
                    e = expert_of(dve, t)
                    dve.wait_ge(s["hid_done"], t + 1)
                    if not isinstance(i, int) or t >= 2:
                        dve.wait_ge(s["hid_transposed"], t - 1)
                    dve.tensor_tensor(ffn_hid[k % 2], s1_bank[:, (k % 2) * F:(k % 2 + 1) * F], at(b1_rows, e * F, F),
                                      ALU.add).then_inc(s["hid_ready"], 1)
                t, k, there = tile(i, r, 0)
                if there:
                    e = expert_of(dve, t)
                    bank = (pv_bank, self_bank)[k % 2]
                    dve.wait_ge(s["y_done"], t + 1)
                    dve.tensor_tensor(ffn_y[k % 2], bank[:, 0:D], at(b2_rows, e * D, D), ALU.add).then_inc(s["y_biased"], 1)
                    dve.wait_ge(s["y_biased"], t + 1)
                    dve.wait_ge(row_gathered[k], 16 * (i + 1))
                    if not isinstance(i, int) or t >= RING:
                        dve.wait_ge(row_scattered[k], 16 * i)
                    dve.scalar_tensor_tensor(ffn_out[k], ffn_y[k % 2], ffn_row[k][:, 2 * D:2 * D + 1], ffn_row[k][:, D:2 * D],
                                             ALU.mult, ALU.add).then_inc(s["result_ready"], 1)

            tiles(dve, step, -2, NTILE)

        def ffn_scalar(act):
            def step(i, r):
                t, k, there = tile(i, r, 1)
                if there:
                    act.wait_ge(s["row_transposed"], t + 1)
                    if not isinstance(i, int) or t >= 2:
                        act.wait_ge(s["hid_done"], t - 1)
                    act.activation(ffn_row_t[k % 2], cross_bank[:, 0:128], ACT.Copy).then_inc(s["row_t_ready"], 1)
                t, k, there = tile(i, r, -1)
                if there:
                    act.wait_ge(s["hid_transposed"], t + 1)
                    if not isinstance(i, int) or t >= 2:
                        act.wait_ge(s["y_done"], t - 1)
                    act.activation(ffn_relu[k % 2], s2_bank[:, (k % 2) * F:(k % 2 + 1) * F], ACT.Relu).then_inc(s["relu_ready"], 1)

            tiles(act, step, -1, NTILE + 2)

        def ffn_pool(pool):
            wait_alone(pool, s["s2_done"], 4 * B)
            wait_alone(pool, s["tok_ready"], 2)
            wait_alone(pool, s["pay_stored"], 16 * NG)

            def index(idx, t, k, n):
                src = idx[:, t:t + 1] if isinstance(t, int) else idx[:, ds(t, 1)]
                pool.tensor_copy(index_now[:, k, n:n + 1], src).then_inc(s["index_copied"][n], 1)
                wait_alone(pool, s["index_copied"][n], t + 1)
                return bass.IndirectOffsetOnAxis(ap=index_now[:, k, n:n + 1].bitcast(U32), axis=0)

            def step(i, r):
                t, k, there = tile(i, r, 0)
                old, _, stored = tile(i, r, -RING)
                if stored:
                    wait_alone(pool, s["result_ready"], old + 1)
                if there:
                    if stored:
                        wait_alone(pool, row_gathered[k], 16 * i)
                    pool.indirect_dma_start(out=ffn_row[k], out_offset=None, in_=rows,
                                            in_offset=index(gather_idx, t, k, 0)).then_inc(row_gathered[k], 16)
                if stored:
                    if not isinstance(i, int) or old >= RING:
                        wait_alone(pool, row_scattered[k], 16 * (i - 1))
                    pool.indirect_dma_start(out=out_rows, out_offset=index(scatter_idx, old, k, 1),
                                            in_=ffn_out[k], in_offset=None, bounds_check=B * S - 1,
                                            oob_is_err=False).then_inc(row_scattered[k], 16)

            tiles(pool, step, 0, NTILE + RING)
            for k in range(RING):
                n = len(range(k, NTILE, RING))
                wait_alone(pool, row_scattered[k], 16 * n)

        @block.sync
        def _(sp):
            def load_x(g):
                sp.dma_start(grouped(at(x_in, (g % 4) * GS, GS)),
                             T["x"][ds(g * G, G), :, :].rearrange("b s d -> s b d")).then_inc(s["x_loaded"], 16)

            def load_ctx(g):
                sp.dma_start(grouped(ctx_in[:, :]),
                             T["ctx_1024"][ds(g * G, G), :, :].rearrange("b s d -> s b d")).then_inc(s["ctx_loaded"], 16)

            load_x(0)
            for dst, src in ((wq_t, "wq_t"), (wk_t, "wk_t"), (wv, "wv"), (wo_t, "wo_t")):
                sp.dma_start(dst[:, :], T[src]).then_inc(s["attn_loaded"], 16)
            for dst, src in ((bv_col[:, :], "bv"), (bias_cols[:, 0:1], "bq"), (bias_cols[:, 1:2], "bk")):
                sp.dma_start(dst, T[src].rearrange("(p a) -> p a", a=1)).then_inc(s["attn_loaded"], 16)
            sp.dma_start(bo_rows[:, :], T["bo"].partition_broadcast(128)).then_inc(s["attn_loaded"], 16)
            wait_alone(sp, s["x_loaded"], 16)
            load_x(1)
            load_ctx(0)

            def store(g, name, parts, scratch, reads):
                for a in range(NPART):
                    if a == 0:
                        wait_alone(sp, s[name + "_split"], g + 1)
                        if later(g, 1):
                            wait_alone(sp, s[name + "_stacked"], 16 * reads * g)
                    sp.dma_start(scratch[:, a, :, :], parts[:, a, :]).then_inc(s[name + "_stored"], 16)

            def stack_parts(g, name, scratch, stacked, pieces):
                wait_alone(sp, s[name + "_stored"], 16 * NPART * (g + 1))
                if not later(g, 1):
                    sp.wait_ge(s[name + "_zeroed"], 1)
                if later(g, 2):
                    wait_alone(sp, s["s2_done"], 16 * (g - 1))
                for row, a, n in pieces:
                    src = scratch[:, a:a + n, :, :].rearrange("h c d t -> (c d) h t")
                    dst = stacked[row * HD:(row + n) * HD, ds(half(g) * H * GS, H * GS)]
                    sp.dma_start(dst.rearrange("p (h t) -> p h t", h=H), src).then_inc(s[name + "_stacked"], 16)

            def load_biases():
                wait_alone(sp, s["attn_done"], NG)
                wait_alone(sp, s["x_bo_ready"], NG)
                for dst, src in ((b1_rows, T["b1"].rearrange("e f -> (e f)")), (b2_rows, T["b2"].rearrange("e d -> (e d)"))):
                    sp.dma_start(dst, src.partition_broadcast(128)).then_inc(s["ffn_loaded"], 16)

            def run(g):
                has_f, has_c, has_e, has_s = stages(g)
                if isinstance(g, int) and g + 5 < NG:
                    if later(g, -1):
                        wait_alone(sp, s["x_bo_ready"], g + 2)
                    wait_alone(sp, s["x_loaded"], 16 * (g + 5))
                    load_x(g + 5)
                if not isinstance(g, int) or 0 <= g + 1 < NG:
                    stack_parts(g + 1, "xk", k_scratch, k_stack, K_PIECES)
                    stack_parts(g + 1, "xq", q_scratch, q_stack, Q_PIECES)
                if not isinstance(g, int) or 0 < g + 3 < NG:
                    wait_alone(sp, s["ctx_transposed"], g + 3)
                    wait_alone(sp, s["ctx_loaded"], 16 * (g + 3))
                    load_ctx(g + 3)
                if has_e:
                    store(g + 2, "xk", xk_parts, k_scratch, len(K_PIECES))
                if isinstance(g, int) and g == NG - 3:
                    load_biases()
                if has_f:
                    wait_alone(sp, s["pay_ready"], g)
                    wait_alone(sp, s["alpha_ready"], g)
                    sp.dma_start(rows[ds((g - 1) * GS, GS), :].rearrange("(b s) c -> s b c", s=S),
                                 pay[:, :, :]).then_inc(s["pay_stored"], 16)
                if has_e:
                    store(g + 2, "xq", xq_parts, q_scratch, len(Q_PIECES))

            def load_ffn():
                for e in range(E):
                    sp.dma_start(at(w1, e * F, F), T["w1"][e, :, :]).then_inc(s["ffn_loaded"], 16)
                    sp.dma_start(at(w2, e * FC * D, FC * D).rearrange("p (c d) -> p c d", c=FC),
                                 T["w2"][e, :, :].rearrange("(c p) d -> p c d", c=FC)).then_inc(s["ffn_loaded"], 16)

            for g in range(-3, NG - 5):
                if g == 1:
                    load_ffn()
                run(g)
            with sp.Fori(NG - 5, NG - 3) as g:
                run(g)
            for g in range(NG - 3, NG):
                run(g)
            run(NG)

        def norm_stats(dve, n, src, base, g, ready, count):
            dve.wait_ge(s[ready], count)
            if not isinstance(g, int) or g >= 1:
                dve.wait_ge(s[f"ln{n}_centred"], g)
            for b in range(G):
                dve.bn_stats(stats[n][:, b, :], at(src, base + b * S, S)).then_inc(s[f"ln{n}_stats"], 1)

        def norm_moments(dve, n, g):
            for b in range(G):
                wait_alone(dve, s[f"ln{n}_stats"], G * g + b + 1)
                dve.bn_aggr(moments[n][:, b, :], stats[n][:, b, :]).then_inc(s[f"ln{n}_moments"], 1)
            dve.wait_ge(s[f"ln{n}_moments"], G * g + G)
            dve.tensor_scalar(var_eps[n][:, :], moments[n][:, :, 1], EPS, None, ALU.add).then_inc(s[f"ln{n}_var"], 1)

        def norm_rstd(pool, n, g):
            wait_alone(pool, s[f"ln{n}_var"], g + 1)
            pool.tensor_tensor(rstd[n][:, :], var_eps[n][:, :], minus_half[:, :], ALU.pow).then_inc(s[f"ln{n}_rstd"], 1)

        def norm_apply(pool, n, g, src, centred_buf, dst, done):
            shape = [128, G, S]
            pool.tensor_tensor(grouped(centred_buf), grouped(src), spread(moments[n][:, :, 0:1], shape),
                               ALU.subtract).then_inc(s[f"ln{n}_centred"], 1)
            wait_alone(pool, s[f"ln{n}_centred"], g + 1)
            wait_alone(pool, s[f"ln{n}_rstd"], g + 1)
            pool.tensor_tensor(grouped(dst), grouped(centred_buf),
                               spread(rstd[n][:, :].rearrange("p (g a) -> p g a", a=1), shape),
                               ALU.mult).then_inc(s[done], 1)

        @block.gpsimd
        def _(pool):
            pool.memset(ident[:, :], 0.0).then_inc(s["consts_made"], 1)
            pool.memset(ident_bf[:, :], 0.0).then_inc(s["consts_made"], 1)
            pool.memset(minus_half[:, :], -0.5).then_inc(s["consts_made"], 1)
            pool.memset(head_sel[:, :, :], 0.0).then_inc(s["consts_made"], 1)
            pool.memset(xv[:, :], 1.0).then_inc(s["ones_made"], 1)
            pool.memset(hmax_parts[:, :], 0.0).then_inc(s["ones_made"], 1)
            pool.memset(earlier[:, :], 1.0).then_inc(s["consts_made"], 1)
            pool.memset(all_ones[:, :], 1.0).then_inc(s["consts_made"], 1)
            pool.iota(iota_i[:, :], pattern=[[1, 128]], base=0, channel_multiplier=0).then_inc(s["consts_made"], 1)
            pool.iota(place_i[:, :], pattern=[[0, 1]], base=1, channel_multiplier=1).then_inc(s["consts_made"], 1)
            wait_alone(pool, s["consts_made"], 8)
            pool.affine_select(out=earlier[:, :], in_=earlier[:, :], compare_op=ALU.is_gt, fill=0.0, base=0,
                               pattern=[[1, 128]], channel_multiplier=-1).then_inc(s["iota_made"], 1)
            pool.tensor_copy(iota_f[:, :], iota_i[:, :]).then_inc(s["iota_made"], 1)
            pool.tensor_copy(place_f[:, :], place_i[:, :]).then_inc(s["iota_made"], 1)
            pool.memset(pay[:, :, 2 * D:PAY], 0.0).then_inc(s["iota_made"], 1)
            for m in (ident, ident_bf):
                pool.affine_select(out=m[:, :], in_=m[:, :], compare_op=ALU.not_equal, fill=1.0, base=0,
                                   pattern=[[-1, 128]], channel_multiplier=1).then_inc(s["consts_made"], 1)
            for i in range(2):
                wait_alone(pool, s["sel_made"], i)
                pool.affine_select(out=head_sel[:, :, :], in_=head_sel[:, :, :], compare_op=ALU.not_equal, fill=1.0,
                                   base=-H * i, pattern=[[-1, H], [0, 128]], channel_multiplier=1).then_inc(s["sel_made"], 1)

            def split_rest(g, name, full, rest, parts):
                wait_alone(pool, s[name + "_ready"], 2 * g + 2)
                if name == "xq":
                    wait_alone(pool, s["xk_split"], g + 1)
                elif later(g, 1):
                    wait_alone(pool, s["xq_split"], g)
                pool.tensor_tensor(rest[:, :], full[:, :], parts[:, 0, :], ALU.subtract).then_inc(s[name + "_rest_ready"], 1)

            def split_last(g, name, rest, parts):
                wait_alone(pool, s[name + "_part1"], g + 1)
                pool.tensor_tensor(parts[:, 2, :], rest[:, :], parts[:, 1, :], ALU.subtract).then_inc(s[name + "_split"], 1)

            def add_attended(g, j):
                n = G * g + j
                wait_alone(pool, s["attended_ready"], n + 1)
                pool.tensor_tensor(at(x2, half(g) * GS + j * S, S), at(x1_bv, (g % 4) * GS + j * S, S),
                                   attended[:, (j % 2) * S:(j % 2 + 1) * S], ALU.add).then_inc(s["x2_ready"], 1)

            def first_norm(h):
                if later(h, 1):
                    wait_alone(pool, s["xn_ready"], h)
                norm_rstd(pool, 0, h)
                if later(h, 1):
                    wait_alone(pool, s["xn_transposed"], h)
                norm_apply(pool, 0, h, at(x_in, (h % 4) * GS, GS), centred[:, :], xn[:, :], "xn_ready")

            def scale_w1(e):
                wait_alone(pool, s["b1_done"], e + 1)
                pool.tensor_scalar(w1[:, e * F:(e + 1) * F], w1[:, e * F:(e + 1) * F], gamma_t[:, e:e + 1], 1.0,
                                   ALU.mult, ALU.mult).then_inc(s["w1_scaled"], 1)

            def run(g):
                has_f, has_c, has_e, has_s = stages(g)
                f, e, h = g - 1, g + 2, g + 3
                if isinstance(g, int) and g == NG - 1:
                    for expert in range(E // 2):
                        scale_w1(expert)
                if isinstance(g, int) and g == -2:
                    pool.wait_ge(s["cross_loaded"], N_CROSS)
                if has_f:
                    add_attended(f, 3)
                if not isinstance(g, int) or 0 <= e - 1 < NG:
                    split_last(e - 1, "xq", rest, xq_parts)
                if has_e:
                    if later(e, 1):
                        wait_alone(pool, s["x1_ready"], e)
                    pool.tensor_tensor(grouped(x_bo[:, :]), grouped(at(x_in, (e % 4) * GS, GS)),
                                       spread(bo_rows[:, :].rearrange("p (a n) -> p a n", a=1), [128, G, S]),
                                       ALU.add).then_inc(s["x_bo_ready"], 1)
                    split_rest(e, "xk", xk, rest, xk_parts)
                if has_c:
                    if later(g, 2):
                        wait_alone(pool, s["pay_ready"], g - 1)
                    add_attended(g, 0)
                if has_e:
                    split_last(e, "xk", rest, xk_parts)
                if has_f:
                    norm_rstd(pool, 2, f)
                    if later(f, 1):
                        wait_alone(pool, s["feats_transposed"], f)
                    norm_apply(pool, 2, f, at(x2, half(f) * GS, GS), centred[:, :], feats[:, :], "feats_ready")
                if has_e:
                    norm_rstd(pool, 1, e)
                    if later(e, 1):
                        wait_alone(pool, s["xn2_transposed"], e)
                    if has_f:
                        wait_alone(pool, s["feats_ready"], f + 1)
                    norm_apply(pool, 1, e, x1[:, :], centred[:, :], xn2[:, :], "xn2_ready")
                if has_c:
                    add_attended(g, 1)
                if has_f:
                    pool.tensor_tensor(var2[:, :], rstd[2][:, :], rstd[2][:, :], ALU.mult).then_inc(s["rstd2_step"], 1)
                    wait_alone(pool, s["rstd2_step"], 3 * f + 1)
                    pool.tensor_tensor(rstd2[:, :], var2[:, :], moments[2][:, :, 1], ALU.mult).then_inc(s["rstd2_step"], 1)
                    wait_alone(pool, s["rstd2_step"], 3 * f + 2)
                    pool.tensor_scalar(var2[:, :], rstd2[:, :], 1.0, EPS, ALU.mult, ALU.add).then_inc(s["rstd2_step"], 1)
                    wait_alone(pool, s["rstd2_step"], 3 * f + 3)
                    pool.tensor_tensor(rstd2[:, :], var2[:, :], minus_half[:, :], ALU.pow).then_inc(s["rstd2_ready"], 1)
                    if later(f, 1):
                        wait_alone(pool, s["pay_stored"], 16 * f)
                    wait_alone(pool, s["feats_ready"], f + 1)
                    pool.tensor_tensor(pay[:, :, D:2 * D], grouped(at(x2, half(f) * GS, GS)), grouped(feats[:, :]),
                                       ALU.add).then_inc(s["base_ready"], 1)
                if has_c:
                    add_attended(g, 2)
                if isinstance(g, int) and g == NG - 1:
                    for expert in range(E // 2, E):
                        scale_w1(expert)
                if has_e:
                    pool.tensor_tensor(grouped(at(x1_bv, (e % 4) * GS, GS)), grouped(x1[:, :]),
                                       spread(xbv_rows[:, :].rearrange("p (a n) -> p a n", a=1), [128, G, S]),
                                       ALU.add).then_inc(s["x1_bv_ready"], 1)
                if has_f:
                    wait_alone(pool, s["rstd2_ready"], f + 1)
                    pool.tensor_tensor(pay[:, :, 0:D], grouped(feats[:, :]),
                                       spread(rstd2[:, :].rearrange("p (g a) -> p g a", a=1), [128, G, S]),
                                       ALU.mult).then_inc(s["pay_ready"], 1)
                if not isinstance(g, int) or h + 1 < NG:
                    if has_e:
                        wait_alone(pool, s["xn2_ready"], e + 1)
                    first_norm(h + 1)
                if has_e:
                    split_rest(e, "xq", xq, rest, xq_parts)

            first_norm(0)
            pool.memset(q_stack[:, :].bitcast(F32), 0.0).then_inc(s["xq_zeroed"], 1)
            wait_alone(pool, s["attn_loaded"], N_ATTN)
            passes(pool, run)
            ffn_pool(pool)

        @block.vector
        def _(dve):
            def first_norm(h):
                norm_stats(dve, 0, x_in, (h % 4) * GS, h, "x_loaded", 16 * (h + 1))
                norm_moments(dve, 0, h)

            first_norm(0)
            dve.wait_ge(s["attn_loaded"], N_ATTN)
            dve.tensor_copy(bv_cols[:, :], spread(bv_col[:, 0:1], [128, 128])).then_inc(s["bv_made"], 1)
            dve.wait_ge(s["wvo_done"], 1)
            dve.tensor_copy(wvo_t[:, :], self_bank[:, 0:D]).then_inc(s["wvo_ready"], 1)
            dve.tensor_copy(bvo_rows[:, :], self_bank[:, D:2 * D]).then_inc(s["wvo_ready"], 1)

            def topk(g, r):
                for b in range(G):
                    src = scores if r == 0 else left
                    if r == 0 and b == 0:
                        wait_alone(dve, s["scores_ready"], g + 1)
                    elif r > 0:
                        wait_alone(dve, s["topk_step"], 32 * g + 8 * (r - 1) + 4 + b + 1)
                    dve.max(best8[:, b, r, :], at(src, b * S, S)).then_inc(s["topk_step"], 1)
                for b in range(G):
                    src = scores if r == 0 else left
                    wait_alone(dve, s["topk_step"], 32 * g + 8 * r + b + 1)
                    dve.match_replace(at(left, b * S, S), best8[:, b, r, :], at(src, b * S, S), TAKEN)\
                       .then_inc(s["topk_step"], 1)

            def head_max(g, j, u):
                n, q = G * g + j, 16 * g + 4 * j + u
                dve.wait_ge(s["s1_done"], q + 1)
                bank = s1_bank[:, (u % 2) * GS:(u % 2 + 1) * GS]
                dve.tensor_reduce(neg_hmax[:, (j % 2) * H + u * 4:(j % 2) * H + u * 4 + 4], bank.rearrange("p (h k) -> p h k", k=S),
                                  AX.X, ALU.max, negate=True).then_inc(s["s1_max"], 1)

            def hmax_split(g, j):
                n, i = G * g + j, j % 2
                dve.wait_ge(s["s1_max"], 4 * n + 4)
                if later(n, 2):
                    dve.wait_ge(s["hmax_transposed"], n - 1)
                parts = [hmax_parts[:, i * 128 + a * H:i * 128 + (a + 1) * H] for a in range(2)]
                maxima = neg_hmax[:, i * H:(i + 1) * H]
                dve.tensor_copy(parts[0], maxima).then_inc(s["hmax_step"], 1)
                dve.wait_ge(s["hmax_step"], n + 1)
                dve.tensor_tensor(parts[1], maxima, parts[0], ALU.subtract).then_inc(s["hmax_split"], 1)

            def normalise(g, j):
                n, i = G * g + j, j % 2
                pv = pv_bank[:, i * 512:i * 512 + H * HC].rearrange("p (h c) -> p h c", c=HC)
                dve.wait_ge(s["pv_done"], 4 * n + 4)
                dve.reciprocal(wsum_inv[:, :], pv[:, :, HD]).then_inc(s["wsum_inv_ready"], 1)
                dve.wait_ge(s["wsum_inv_ready"], n + 1)
                if later(n, 2):
                    dve.wait_ge(s["x2_ready"], n - 1)
                dve.tensor_tensor(attended[:, i * S:(i + 1) * S].rearrange("p (h d) -> p h d", d=HD), pv[:, :, 0:HD],
                                  spread(wsum_inv[:, :].rearrange("p (h a) -> p h a", a=1), [128, H, HD]),
                                  ALU.mult).then_inc(s["attended_ready"], 1)

            def next_maxima(g, j, u):
                g2, j2 = (g, j + 1) if j + 1 < G else (g + 1, 0)
                if isinstance(g2, int) and not 0 <= g2 < NG:
                    return
                head_max(g2, j2, u)
                head_max(g2, j2, u + 1)
                if u == 2:
                    hmax_split(g2, j2)

            def expert_bias(g, n):
                if isinstance(g, int) and NG - 2 <= g < NG:
                    expert = (g - (NG - 2)) * (E // 2) + n
                    place = b1_rows[:, expert * F:(expert + 1) * F]
                    if expert == 0:
                        dve.wait_ge(s["ffn_loaded"], N_FFN)
                    dve.wait_ge(s["b1_done"], expert + 1)
                    dve.tensor_tensor(place, self_bank[:, 0:F], place, ALU.add).then_inc(s["b1_ready"], 1)

            def run(g):
                has_f, has_c, has_e, has_s = stages(g)
                f, e, h = g - 1, g + 2, g + 3
                if isinstance(g, int) and g == NG - 2:
                    dve.wait_ge(s["attn_done"], NG)
                    dve.tensor_copy(beta_cols.rearrange("p (e n) -> p e n", e=E),
                                    spread(beta_t[:, :].rearrange("p (e a) -> p e a", a=1), [128, E, 128]))\
                       .then_inc(s["beta_made"], 1)
                if not isinstance(g, int) or h + 1 < NG:
                    first_norm(h + 1)
                if isinstance(g, int) and g == -3:
                    dve.memset(k_stack[:, :].bitcast(F32), 0.0).then_inc(s["xk_zeroed"], 1)
                if has_f:
                    normalise(f, 3)
                if has_e:
                    wait_alone(dve, s["topk_step"], 32 * e + 29)
                    if later(e, 1):
                        dve.wait_ge(s["self_exp"], G * e)
                    dve.tensor_scalar(neg_max[:, :], best8[:, :, 0, 0], -SELF_SCALE, None, ALU.mult)\
                       .then_inc(s["neg_max_ready"], 1)
                if has_c:
                    next_maxima(g, 0, 0)
                if has_c:
                    next_maxima(g, 0, 2)
                if has_e:
                    wait_alone(dve, s["topk_step"], 32 * e + 32)
                    if later(e, 1):
                        dve.wait_ge(s["probs_n_ready"], G * e)
                    for b in range(G):
                        dve.wait_ge(s["self_exp"], G * e + b + 1)
                        dve.scalar_tensor_tensor(at(probs, b * S, S), at(left, b * S, S), TAKEN, at(expd, b * S, S),
                                                 ALU.is_equal, ALU.mult, accum_out=prob_sum[:, b:b + 1])\
                           .then_inc(s["probs_ready"], 1)
                    dve.wait_ge(s["probs_ready"], G * e + G)
                    dve.reciprocal(prob_inv[:, :], prob_sum[:, :]).then_inc(s["inv_ready"], 1)
                    dve.wait_ge(s["inv_ready"], e + 1)
                    if later(e, 1):
                        dve.wait_ge(s["probs_transposed"], e)
                    for b in range(G):
                        dve.tensor_scalar(at(probs_n, b * S, S), at(probs, b * S, S), prob_inv[:, b:b + 1], 0.0,
                                          ALU.mult, ALU.max).then_inc(s["probs_n_ready"], 1)
                expert_bias(g, 0)
                if has_c:
                    normalise(g, 0)
                    next_maxima(g, 1, 0)
                if has_f:
                    norm_stats(dve, 2, x2, half(f) * GS, f, "x2_ready", G * g)
                    if later(f, 1):
                        dve.wait_ge(s["rstd2_ready"], f)
                    norm_moments(dve, 2, f)
                if has_c:
                    next_maxima(g, 1, 2)
                if has_e:
                    dve.wait_ge(s["attn_done"], e + 1)
                    dve.wait_ge(s["x_bo_ready"], e + 1)
                    if later(e, 1):
                        dve.wait_ge(s["x1_bv_ready"], e)
                    dve.tensor_tensor(x1[:, :], cross_bank[:, :], x_bo[:, :], ALU.add).then_inc(s["x1_ready"], 1)
                    norm_stats(dve, 1, x1, 0, e, "x1_ready", e + 1)
                    norm_moments(dve, 1, e)
                expert_bias(g, 1)
                if has_c:
                    normalise(g, 1)
                    next_maxima(g, 2, 0)
                if has_s:
                    topk(h, 0)
                if has_c:
                    next_maxima(g, 2, 2)
                if has_s:
                    topk(h, 1)
                    dve.wait_ge(s["v_done"], h + 1)
                    if later(h, 2):
                        dve.wait_ge(s["attn_done"], h - 1)
                    dve.tensor_tensor(grouped(at(v, half(h) * GS, GS)), grouped(self_bank[:, :]),
                                      spread(bvo_rows[:, :].rearrange("p (a n) -> p a n", a=1), [128, G, S]),
                                      ALU.add).then_inc(s["v_ready"], 1)
                if has_f:
                    dve.wait_ge(s["aff_done"], g)
                    dve.tensor_copy(aff[:, ds(f * G, G), :],
                                    pv_bank[:, AFF:AFF + G * E].rearrange("p (b e) -> p b e", e=E))\
                       .then_inc(s["aff_ready"], 1)
                expert_bias(g, 2)
                if has_c:
                    normalise(g, 2)
                    next_maxima(g, 3, 0)
                if has_f:
                    wait_alone(dve, s["aff_ready"], g)
                    if later(f, 1):
                        wait_alone(dve, s["aff_exp_ready"], f)
                    dve.tensor_reduce(aff_max[:, :], aff[:, ds(f * G, G), :], AX.X, ALU.max).then_inc(s["aff_max_ready"], 1)
                if has_s:
                    topk(h, 2)
                if has_c or isinstance(g, int) and g == -1:
                    if not has_c:
                        next_maxima(g, 3, 0)
                    next_maxima(g, 3, 2)
                if has_s:
                    topk(h, 3)
                if has_f:
                    dve.wait_ge(s["aff_exp_ready"], g)
                    dve.tensor_scalar(aff_den[:, :], aff_exp[:, :], 1.0, None, ALU.add).then_inc(s["aff_den_ready"], 1)
                expert_bias(g, 3)
                if has_f:
                    dve.wait_ge(s["aff_den_ready"], g)
                    if later(f, 1):
                        dve.wait_ge(s["pay_stored"], 16 * f)
                    dve.reciprocal(pay[:, :, 2 * D], aff_den[:, :]).then_inc(s["alpha_ready"], 1)

            passes(dve, run)
            route_vector(dve)

        @block.scalar
        def _(act):
            for dst, src in ((xwk_t, "xwk_t"), (xwv_t, "xwv_t"), (xwq_t, "xwq_t"), (cent_t, "cent_t"),
                             (gamma_t, "gamma_t"), (beta_t, "beta_t")):
                act.dma_start(dst[:, :], T[src]).then_inc(s["cross_loaded"], 16)
            for n, src in ((2, "xbq"), (3, "xbk")):
                act.dma_start(bias_cols[:, n:n + 1], T[src].rearrange("(p a) -> p a", a=1)).then_inc(s["cross_loaded"], 16)
            act.dma_start(xbv_rows[:, :], T["xbv"].partition_broadcast(128)).then_inc(s["cross_loaded"], 16)
            act.wait_ge(s["attn_loaded"], N_ATTN)

            def evacuate(dst, bank, done, count, ready, bias=None):
                act.wait_ge(s[done], count)
                if bias is None:
                    act.activation(dst, bank, ACT.Copy).then_inc(s[ready], 1)
                else:
                    act.activation(dst, bank, ACT.Identity, bias=bias_cols[:, bias:bias + 1]).then_inc(s[ready], 1)

            def exps(g, j, u):
                q = 16 * g + 4 * j + u
                act.wait_ge(s["s2_done"], q + 1)
                if later(g, 1) or q >= 4:
                    act.wait_ge(s["pv_done"], q - 3)
                act.activation(weights[:, u, :], s2_bank[:, (u % 2) * GS:(u % 2 + 1) * GS], ACT.Exp,
                               scale=HEAD_SCALE).then_inc(s["s2_exp"], 1)

            def hmax_out(g, j):
                n, i = G * g + j, j % 2
                if later(n, 2):
                    act.wait_ge(s["s2_done"], 4 * (n - 1))
                evacuate(hmax_t[:, i * 128:(i + 1) * 128], hmax_bank, "hmax_transposed", n + 1, "hmax_t_ready")

            def part0(g, name, parts, bias):
                act.activation(parts[:, 0, :], cross_bank[:, :], ACT.Identity, bias=bias_cols[:, bias:bias + 1])\
                   .then_inc(s[name + "_ready"], 1)

            def part1(g, name, rest, parts):
                act.wait_ge(s[name + "_rest_ready"], g + 1)
                act.activation(parts[:, 1, :], rest[:, :], ACT.Copy).then_inc(s[name + "_part1"], 1)

            def run(g):
                has_f, has_c, has_e, has_s = stages(g)
                e, h = g + 2, g + 3

                def step(n, before, after):
                    before()
                    if has_c:
                        exps(g, n // 2, n % 2 * 2)
                        exps(g, n // 2, n % 2 * 2 + 1)
                    after()
                    g2, j2 = (g, n // 2 + 1) if n // 2 + 1 < G else (g + 1, 0)
                    if n % 2 == 1 and (has_c or n == 7) and not (isinstance(g2, int) and not 0 <= g2 < NG):
                        hmax_out(g2, j2)

                def context():
                    if isinstance(g, int) and g == -2:
                        act.wait_ge(s["cross_loaded"], N_CROSS)
                    if has_e:
                        evacuate(ctx_t[:, :], cross_bank[:, :], "ctx_transposed", e + 1, "ctx_t_ready")

                def keys_and_weights():
                    if not isinstance(g, int) or 0 <= e - 1 < NG:
                        part1(e - 1, "xq", rest, xq_parts)
                    if has_e:
                        if later(e, 1):
                            act.wait_ge(s["xk_rest_ready"], e)
                            act.wait_ge(s["xk_stored"], 16 * NPART * e)
                        evacuate(xk[:, :], cross_bank[:, :], "xk_done", e + 1, "xk_ready", 3)
                        part0(e, "xk", xk_parts, 3)
                        act.wait_ge(s["neg_max_ready"], e + 1)
                        if later(e, 1):
                            act.wait_ge(s["probs_ready"], G * e)
                        for b in range(G):
                            act.activation(at(expd, b * S, S), at(scores, b * S, S), ACT.Exp, bias=neg_max[:, b:b + 1],
                                           scale=SELF_SCALE).then_inc(s["self_exp"], 1)

                def values():
                    if has_e:
                        if later(e, 4):
                            act.wait_ge(s["pv_done"], 16 * (e - 3))
                        act.wait_ge(s["xv_done"], e + 1)
                        act.activation(at(xv, (e % 4) * G * H * HC, G * H * HC)
                                       .rearrange("p (n c) -> p n c", c=HC)[:, :, 0:HD],
                                       cross_bank[:, :].rearrange("p (n c) -> p n c", c=HD), ACT.Copy)\
                           .then_inc(s["xv_ready"], 1)

                def xn_out():
                    if has_s:
                        evacuate(xn_t[:, :], self_bank[:, :], "xn_transposed", h + 1, "xn_t_ready")

                def queries():
                    if has_s:
                        evacuate(q_t[:, :], self_bank[:, :], "q_done", h + 1, "q_ready", 0)

                def probs_out():
                    if has_e:
                        evacuate(probs_t[:, :], cross_bank[:, :], "probs_transposed", e + 1, "probs_t_ready")
                        part1(e, "xk", rest, xk_parts)

                def self_keys():
                    if has_s:
                        evacuate(k_t[:, :], self_bank[:, :], "k_done", h + 1, "k_ready", 1)

                def scores_out():
                    if has_s:
                        if later(h, 1):
                            act.wait_ge(s["topk_step"], 32 * h)
                        evacuate(scores[:, :], self_bank[:, :], "scores_done", h + 1, "scores_ready")

                def feats_out():
                    if has_f:
                        evacuate(feats_t[:, :], cross_bank[:, :], "feats_transposed", g, "feats_t_ready")

                def xn2_out():
                    if has_e:
                        evacuate(xn2_t[:, :], cross_bank[:, :], "xn2_transposed", e + 1, "xn2_t_ready")

                def cross_queries():
                    if has_e:
                        if later(e, 1):
                            act.wait_ge(s["xq_rest_ready"], e)
                            act.wait_ge(s["xq_stored"], 16 * NPART * e)
                        evacuate(xq[:, :], cross_bank[:, :], "xq_done", e + 1, "xq_ready", 2)
                        part0(e, "xq", xq_parts, 2)

                def affinity_exp():
                    if has_f:
                        act.wait_ge(s["aff_max_ready"], g)
                        if later(g, 2):
                            act.wait_ge(s["aff_den_ready"], g - 1)
                        act.activation(aff_exp[:, :], aff_max[:, :], ACT.Exp, scale=-1.0).then_inc(s["aff_exp_ready"], 1)

                def nothing():
                    pass

                step(0, context, keys_and_weights)
                step(1, values, xn_out)
                step(2, queries, probs_out)
                step(3, nothing, self_keys)
                step(4, scores_out, feats_out)
                step(5, nothing, nothing)
                step(6, nothing, xn2_out)
                step(7, affinity_exp, cross_queries)

            passes(act, run)
            ffn_scalar(act)

        @block.tensor
        def _(pe):
            def transposed(src, bank, g, ready, count, done):
                pe.wait_ge(s[ready], count)
                for b in range(G):
                    m = pe.transpose(bank[:, b * S:(b + 1) * S], src(b), ident[:, :])
                m.then_inc(s[done], 1)

            def project(bank, w, src, ready, count, done):
                pe.wait_ge(s[ready], count)
                pe.matmul(bank[:, :], w[:, :], src[:, :], start=True, stop=True).then_inc(s[done], 1)

            def stack_at(g, j, h):
                return half(g) * H * GS + h * GS + j * S

            def s1(g, j, u):
                q = 16 * g + 4 * j + u
                if later(g, 1) or q >= 2:
                    pe.wait_ge(s["s1_max"], q - 1)
                if j == 0 and u == 0:
                    pe.wait_ge(s["xq_stacked"], 16 * len(Q_PIECES) * (g + 1))
                    pe.wait_ge(s["xk_stacked"], 16 * len(K_PIECES) * (g + 1))
                if u == 1 and later(G * g + j, 1):
                    pe.wait_ge(s["hmax_t_ready"], G * g + j)
                for i in range(4):
                    o = stack_at(g, j, 4 * u + i)
                    m = pe.matmul(s1_bank[:, (u % 2) * GS + i * S:(u % 2) * GS + (i + 1) * S], at(q_stack, o, S),
                                  at(k_stack, o, S), start=True, stop=True)
                m.then_inc(s["s1_done"], 1)

            def s2(g, j, u):
                q = 16 * g + 4 * j + u
                if later(g, 1) or q >= 2:
                    pe.wait_ge(s["s2_exp"], q - 1)
                if u == 0:
                    pe.wait_ge(s["hmax_t_ready"], G * g + j + 1)
                for i in range(4):
                    o = stack_at(g, j, 4 * u + i)
                    to = s2_bank[:, (u % 2) * GS + i * S:(u % 2) * GS + (i + 1) * S]
                    pe.matmul(to, at(k_stack, o, S), at(q_stack, o, S), start=True, stop=False)
                    m = pe.matmul(to, head_sel[:, u * 4 + i, :], hmax_t[:, (j % 2) * 128:(j % 2 + 1) * 128],
                                  start=False, stop=True)
                m.then_inc(s["s2_done"], 1)

            def hmax_rows(g, j):
                n = G * g + j
                pe.wait_ge(s["hmax_split"], n + 1)
                pe.transpose(hmax_bank, hmax_parts[:, (j % 2) * 128:(j % 2 + 1) * 128], ident_bf[:, :])\
                  .then_inc(s["hmax_transposed"], 1)

            def pv(g, j, u):
                n = G * g + j
                pe.wait_ge(s["s2_exp"], 4 * n + u + 1)
                if u == 0 and later(n, 2):
                    pe.wait_ge(s["attended_ready"], n - 1)
                if u == 0 and j == 0:
                    pe.wait_ge(s["xv_ready"], g + 1)
                if u == 0 and j == 3 and later(g, 1):
                    pe.wait_ge(s["aff_ready"], g)
                for i in range(4):
                    h = u * 4 + i
                    m = pe.matmul(pv_bank[:, (j % 2) * 512 + h * HC:(j % 2) * 512 + (h + 1) * HC],
                                  weights[:, u, i * S:(i + 1) * S],
                                  at(xv, (g % 4) * G * H * HC + (j * H + h) * HC, HC), start=True, stop=True)
                m.then_inc(s["pv_done"], 1)

            def run(g):
                has_f, has_c, has_e, has_s = stages(g)
                e, h, f = g + 2, g + 3, g - 1

                def step(n, before, after):
                    before()
                    j, u = n // 2, n % 2 * 2
                    g2, j2 = (g, j + 1) if j + 1 < G else (g + 1, 0)
                    ahead = not isinstance(g2, int) or 0 <= g2 < NG
                    if has_c and u == 0:
                        s2(g, j, u)
                        s2(g, j, u + 1)
                    if ahead and (has_c or n == 7):
                        for w in (u, u + 1) if has_c else range(4):
                            s1(g2, j2, w)
                    if has_c and u == 2:
                        s2(g, j, u)
                        s2(g, j, u + 1)
                    after()
                    if has_c:
                        pv(g, j, u)
                    if ahead and u == 2 and (has_c or n == 7):
                        hmax_rows(g2, j2)
                    if has_c:
                        pv(g, j, u + 1)

                def context():
                    if isinstance(g, int) and g == -2:
                        pe.wait_ge(s["cross_loaded"], N_CROSS)
                    if has_e:
                        pe.wait_ge(s["ctx_loaded"], 16 * (e + 1))
                        if later(e, 1):
                            pe.wait_ge(s["xq_ready"], 2 * e)
                        transposed(lambda b: ctx_in[:, b * S:(b + 1) * S], cross_bank, e, "consts_made", 10,
                                   "ctx_transposed")

                def cross_keys():
                    if has_e:
                        project(cross_bank, xwk_t, ctx_t, "ctx_t_ready", e + 1, "xk_done")

                def cross_values():
                    if has_e:
                        pe.wait_ge(s["xk_ready"], 2 * e + 2)
                        for b in range(G):
                            m = pe.matmul(cross_bank[:, b * D:(b + 1) * D], ctx_t[:, b * S:(b + 1) * S], xwv_t[:, :],
                                          start=True, stop=True)
                        m.then_inc(s["xv_done"], 1)

                def xn_rows():
                    if has_s:
                        if later(h, 1):
                            pe.wait_ge(s["v_ready"], h)
                        transposed(lambda b: xn[:, b * S:(b + 1) * S], self_bank, h, "xn_ready", h + 1, "xn_transposed")

                def queries():
                    if has_s:
                        project(self_bank, wq_t, xn_t, "xn_t_ready", h + 1, "q_done")

                def probs_rows():
                    if has_e:
                        pe.wait_ge(s["xv_ready"], e + 1)
                        transposed(lambda b: probs_n[:, b * S:(b + 1) * S], cross_bank, e, "probs_n_ready", G * e + G,
                                   "probs_transposed")

                def attention():
                    if has_e:
                        pe.wait_ge(s["probs_t_ready"], e + 1)
                        pe.wait_ge(s["v_ready"], e + 1)
                        for b in range(G):
                            m = pe.matmul(cross_bank[:, b * D:(b + 1) * D], probs_t[:, b * S:(b + 1) * S],
                                          at(v, half(e) * GS + b * D, D), start=True, stop=True)
                        m.then_inc(s["attn_done"], 1)

                def self_keys():
                    if has_s:
                        pe.wait_ge(s["q_ready"], h + 1)
                        project(self_bank, wk_t, xn_t, "xn_t_ready", h + 1, "k_done")

                def self_scores():
                    if has_s:
                        pe.wait_ge(s["k_ready"], h + 1)
                        for b in range(G):
                            m = pe.matmul(self_bank[:, b * S:(b + 1) * S], q_t[:, b * S:(b + 1) * S],
                                          k_t[:, b * S:(b + 1) * S], start=True, stop=True)
                        m.then_inc(s["scores_done"], 1)

                def feats_rows():
                    if has_f:
                        if has_e:
                            pe.wait_ge(s["x1_ready"], e + 1)
                        if isinstance(g, int) and g == NG - 1:
                            pe.wait_ge(s["xq_ready"], 2 * NG)
                        transposed(lambda b: feats[:, b * S:(b + 1) * S], cross_bank, f, "feats_ready", f + 1,
                                   "feats_transposed")

                def self_values():
                    if has_s:
                        pe.wait_ge(s["scores_ready"], h + 1)
                        if isinstance(h, int) and h == 0:
                            pe.wait_ge(s["wvo_ready"], 2)
                        for b in range(G):
                            m = pe.matmul(self_bank[:, b * D:(b + 1) * D], xn_t[:, b * S:(b + 1) * S], wvo_t[:, :],
                                          start=True, stop=True)
                        m.then_inc(s["v_done"], 1)

                def affinities():
                    if has_f:
                        pe.wait_ge(s["feats_t_ready"], f + 1)
                        if has_c:
                            pe.wait_ge(s["attended_ready"], G * g + 2)
                        for b in range(G):
                            m = pe.matmul(pv_bank[:, AFF + b * E:AFF + (b + 1) * E], feats_t[:, b * S:(b + 1) * S],
                                          cent_t[:, :], start=True, stop=True)
                        m.then_inc(s["aff_done"], 1)

                def xn2_rows():
                    if has_e:
                        pe.wait_ge(s["x1_ready"], e + 1)
                        if has_f:
                            pe.wait_ge(s["feats_t_ready"], f + 1)
                        transposed(lambda b: xn2[:, b * S:(b + 1) * S], cross_bank, e, "xn2_ready", e + 1,
                                   "xn2_transposed")

                def cross_queries():
                    if has_e:
                        project(cross_bank, xwq_t, xn2_t, "xn2_t_ready", e + 1, "xq_done")

                def expert_bias(n):
                    if isinstance(g, int) and NG - 2 <= g < NG:
                        expert = (g - (NG - 2)) * (E // 2) + n
                        if expert == 0:
                            pe.wait_ge(s["ffn_loaded"], N_FFN)
                            pe.wait_ge(s["beta_made"], 1)
                        else:
                            pe.wait_ge(s["b1_ready"], expert)
                        pe.matmul(self_bank[:, 0:F], beta_cols[:, expert * 128:(expert + 1) * 128],
                                  w1[:, expert * F:(expert + 1) * F], start=True, stop=True).then_inc(s["b1_done"], 1)

                def nothing():
                    pass

                step(0, context, cross_keys)
                step(1, cross_values, xn_rows)
                expert_bias(0)
                step(2, queries, probs_rows)
                step(3, attention, self_keys)
                expert_bias(1)
                step(4, self_scores, feats_rows)
                step(5, self_values, affinities)
                expert_bias(2)
                step(6, nothing, xn2_rows)
                step(7, nothing, cross_queries)
                expert_bias(3)

            pe.wait_ge(s["attn_loaded"], N_ATTN)
            pe.matmul(self_bank[:, 0:D], wv[:, :], wo_t[:, :], start=True, stop=True)
            pe.wait_ge(s["bv_made"], 1)
            pe.matmul(self_bank[:, D:2 * D], bv_cols[:, :], wo_t[:, :], start=True, stop=True).then_inc(s["wvo_done"], 1)
            pe.wait_ge(s["wvo_ready"], 2)
            pe.wait_ge(s["sel_made"], 2)
            pe.wait_ge(s["ones_made"], 2)
            passes(pe, run)
            ffn_tensor(pe)



_TRANSPOSED = {"wq_t": "L0_attn_Wq", "wk_t": "L0_attn_Wk", "wo_t": "L0_attn_Wo",
               "xwq_t": "L0_xattn_Wq", "xwk_t": "L0_xattn_Wk", "xwv_t": "L0_xattn_Wv",
               "cent_t": "L0_ffn_centroids", "gamma_t": "L0_ffn_gamma", "beta_t": "L0_ffn_beta"}
_PLAIN = {"x": "x", "ctx_1024": "ctx_1024", "wv": "L0_attn_Wv", "bq": "L0_attn_bq", "bk": "L0_attn_bk",
          "bv": "L0_attn_bv", "bo": "L0_attn_bo", "xbq": "L0_xattn_bq", "xbk": "L0_xattn_bk", "xbv": "L0_xattn_bv",
          "w1": "L0_ffn_w1", "b1": "L0_ffn_b1", "w2": "L0_ffn_w2", "b2": "L0_ffn_b2"}


def kernel(**inputs):
    import concourse.bacc as bacc
    from concourse.bass_utils import run_bass_kernel_spmd

    nc = bacc.Bacc("TRN2", target_bir_lowering=False, num_devices=1)
    arrays, tensors = {}, {}
    for name, source in list(_PLAIN.items()) + list(_TRANSPOSED.items()):
        a = np.asarray(inputs[source])
        a = np.ascontiguousarray(a.T if name in _TRANSPOSED else a)
        arrays[f"in_{name}"] = a
        tensors[name] = nc.dram_tensor(f"in_{name}", a.shape, mybir.dt.from_np(a.dtype), kind="ExternalInput").ap()
    out = nc.dram_tensor("out", tensors["x"].shape, mybir.dt.float32, kind="ExternalOutput").ap()
    preln_decoder_kernel(nc, tensors, out)
    result = run_bass_kernel_spmd(nc, [arrays], core_ids=[0])
    return result.results[0]["out"]
```

```python
import numpy as np
import concourse.bass as bass
from concourse import mybir
from contextlib import ExitStack


def preln_decoder_kernel(nc, T, out):
    F32 = mybir.dt.float32
    BF16 = mybir.dt.bfloat16
    I32 = mybir.dt.int32
    U32 = mybir.dt.uint32
    ALU = mybir.AluOpType
    ACT = mybir.ActivationFunctionType
    AX = mybir.AxisListType
    ds = bass.ds

    B, S, D = T["x"].shape
    E, _, F = T["w1"].shape
    H, HD = 16, 8
    G = 4
    NG = B // G
    GS = G * S
    TOPK = 32
    NPART = 3
    STK = NPART * NPART * HD
    HC = HD + 1
    FC = F // 128
    NTILE = B * S // 128 + E - 1
    NTC = NTILE + 1
    PAY = 2 * D + 4
    TAKEN = -3.0e38
    EPS = 1e-5
    SELF_SCALE = 1.0 / float(np.sqrt(D))
    HEAD_SCALE = 1.0 / float(np.sqrt(HD))
    Q_PIECES = ((0, 0, 3), (3, 0, 3), (6, 0, 3))
    K_PIECES = ((0, 0, 3), (3, 1, 2), (5, 0, 1), (6, 2, 1), (7, 0, 2))
    RING = 6

    q_scratch = nc.dram_tensor("q_parts", [H, NPART, HD, GS], BF16, kind="Internal").ap()
    k_scratch = nc.dram_tensor("k_parts", [H, NPART, HD, GS], BF16, kind="Internal").ap()
    rows = nc.dram_tensor("routed_rows", [B * S, PAY], F32, kind="Internal").ap()
    out_rows = out.rearrange("b s d -> (b s) d")

    with ExitStack() as stack:
        def sb(name, shape, dt=F32):
            return stack.enter_context(nc.sbuf_tensor(name, shape, dt))

        def ps(name, shape, dt=F32):
            return stack.enter_context(nc.psum_tensor(name, shape, dt))

        def sem(name):
            return stack.enter_context(nc.semaphore(name))

        ident = sb("ident", [128, 128])
        ident_bf = sb("ident_bf", [128, 128], BF16)
        head_sel = sb("head_sel", [128, H, 128], BF16)
        minus_half = sb("minus_half", [128, G])
        wq_t, wk_t, wv, wo_t, wvo_t = (sb(n, [128, D]) for n in ("wq_t", "wk_t", "wv", "wo_t", "wvo_t"))
        xwq_t, xwk_t, xwv_t = (sb(n, [128, D]) for n in ("xwq_t", "xwk_t", "xwv_t"))
        cent_t = sb("cent_t", [128, E])
        gamma_t = sb("gamma_t", [128, E])
        beta_t = sb("beta_t", [128, E])
        bias_cols = sb("bias_cols", [128, 4])
        bv_col = sb("bv_col", [128, 1])
        bv_cols = sb("bv_cols", [128, 128])
        bo_rows = sb("bo_rows", [128, D])
        xbv_rows = sb("xbv_rows", [128, D])
        bvo_rows = sb("bvo_rows", [128, D])
        b1_cols = sb("b1_cols", [128, E * FC])
        w1 = sb("w1", [128, E * F])
        w2 = sb("w2", [128, E * FC * D])
        x_in = sb("x_in", [128, 4 * GS])
        ctx_in = sb("ctx_in", [128, GS])
        stats = [sb(f"stats_{i}", [128, G, 6]) for i in range(3)]
        moments = [sb(f"moments_{i}", [128, G, 2]) for i in range(3)]
        var_eps = [sb(f"var_eps_{i}", [128, G]) for i in range(3)]
        rstd = [sb(f"rstd_{i}", [128, G]) for i in range(3)]
        centred = sb("centred", [128, GS])
        self_room = sb("self_room", [128, 10 * GS])
        xn, xn_t, q_t, k_t, scores, left, expd, probs, probs_n, probs_t = (
            self_room[:, n * GS:(n + 1) * GS] for n in range(10))
        v = sb("v", [128, 2 * GS])
        best8 = sb("best8", [128, G, TOPK // 8, 8])
        neg_max = sb("neg_max", [128, G])
        prob_sum = sb("prob_sum", [128, G])
        prob_inv = sb("prob_inv", [128, G])
        x_bo = sb("x_bo", [128, GS])
        x1 = sb("x1", [128, GS])
        x1_bv = sb("x1_bv", [128, 4 * GS])
        xn2 = sb("xn2", [128, GS])
        xq = sb("xq", [128, GS])
        xq_parts = sb("xq_parts", [128, NPART, GS], BF16)
        ctx_t = sb("ctx_t", [128, GS])
        xn2_t = ctx_t
        xk = sb("xk", [128, GS])
        rest = sb("rest", [128, GS])
        xk_parts = sb("xk_parts", [128, NPART, GS], BF16)
        xv = sb("xv", [128, 4 * G * H * HC])
        q_stack = sb("q_stack", [128, 2 * H * GS], BF16)
        k_stack = sb("k_stack", [128, 2 * H * GS], BF16)
        neg_hmax = sb("neg_hmax", [128, 2 * H])
        hmax_parts = sb("hmax_parts", [128, 2 * 128], BF16)
        hmax_t = sb("hmax_t", [128, 2 * 128], BF16)
        weights = sb("weights", [128, 4, GS])
        wsum_inv = sb("wsum_inv", [128, H])
        attended = sb("attended", [128, 2 * H * HD])
        x2 = sb("x2", [128, 2 * GS])
        feats = sb("feats", [128, GS])
        feats_t = sb("feats_t", [128, GS])
        var2 = sb("var2", [128, G])
        rstd2 = sb("rstd2", [128, G])
        pay = sb("pay", [128, G, PAY])
        aff = sb("aff", [128, B, E])
        aff_max = sb("aff_max", [128, G])
        aff_exp = sb("aff_exp", [128, G])
        aff_den = sb("aff_den", [128, G])

        iota_i = sb("iota_i", [128, 128], I32)
        iota_f = sb("iota_f", [128, 128])
        iota_bf = sb("iota_bf", [128, 128], BF16)
        place_i = sb("place_i", [128, 1], I32)
        place_f = sb("place_f", [128, 1])
        earlier = sb("earlier", [128, 128], BF16)
        all_ones = sb("all_ones", [128, 128], BF16)
        tile_expert = sb("tile_expert", [128, NTC], I32)
        gather_idx = sb("gather_idx", [128, NTC], I32)
        scatter_idx = sb("scatter_idx", [128, NTC], I32)

        room = {"q": [q_stack[:, :].bitcast(F32), 0], "k": [k_stack[:, :].bitcast(F32), 0]}

        def carve(which, n, dt=F32):
            words = n if dt == F32 or dt == I32 else n // 2
            ap, at0 = room[which]
            room[which][1] = at0 + words
            assert at0 + words <= H * GS
            piece = ap[:, at0:at0 + words]
            return piece if dt == F32 else piece.bitcast(dt)

        ffn_row = [carve("q", PAY) for _ in range(RING)]
        ffn_row_t = [carve("k", D) for _ in range(2)]
        ffn_hid = [carve("q", F) for _ in range(2)]
        ffn_relu = [carve("q", F) for _ in range(2)]
        ffn_y = [carve("q", D) for _ in range(2)]
        ffn_out = [x_in[:, (E + n) * D:(E + n + 1) * D] for n in range(RING)]
        beta_cols = self_room[:, 0:E * 128]
        ffn_w1 = [self_room[:, E * 128 + n * F:E * 128 + (n + 1) * F] for n in range(2)]
        b2_rows = x_in[:, 0:E * D]
        lo_hot = carve("k", B * 128, BF16)
        apart = self_room[:, 8 * GS:10 * GS]
        hi_hot = carve("k", B * 2 * NTC, BF16)
        onehot = carve("k", E * B, BF16)

        s1_bank = ps("s1_bank", [128, 1024])
        s2_bank = ps("s2_bank", [128, 1024])
        pv_bank = ps("pv_bank", [128, 1024])
        self_bank = ps("self_bank", [128, 512])
        cross_bank = ps("cross_bank", [128, 512])
        hmax_bank = s1_bank[:, 512:576].bitcast(BF16)
        AFF = 896

        names = """x_loaded ctx_loaded qk_loaded vo_loaded cross_loaded ffn_loaded consts_made sel_made
            ln0_stats ln0_moments ln0_var ln0_rstd ln0_centred xn_ready
            ln1_stats ln1_moments ln1_var ln1_rstd ln1_centred xn2_ready
            ln2_stats ln2_moments ln2_var ln2_rstd ln2_centred feats_ready
            xn_transposed xn_t_ready q_done q_ready k_done k_ready v_done v_ready scores_done scores_ready
            topk_step neg_max_ready self_exp probs_ready inv_ready probs_n_ready probs_transposed probs_t_ready
            attn_done x_bo_ready x1_ready x1_bv_ready
            xn2_transposed xn2_t_ready xq_done xq_ready xq_rest_ready xq_part1 xq_split xq_stored xq_stacked
            ctx_transposed ctx_t_ready xk_done xk_ready xk_rest_ready xk_part1 xk_split xk_stored xk_stacked xv_done xv_ready ones_made
            s1_done s1_max hmax_step hmax_split hmax_transposed hmax_t_ready s2_done s2_exp pv_done
            wsum_inv_ready attended_ready x2_ready
            feats_transposed feats_t_ready aff_done aff_ready aff_max_ready aff_exp_ready aff_den_ready alpha_ready
            rstd2_step rstd2_ready base_ready pay_ready pay_stored bv_made xk_zeroed xq_zeroed wvo_done wvo_ready
            beta_made b1_done b1_ready w1_scaled iota_made
            route_step onehot_ready counts_done slots_ready lo_ready apart_ready lo_hot_made tok_done tok_ready experts_ready
            row_transposed row_t_ready hid_done hid_ready w1_picked relu_ready
            y_done y_biased result_ready
            """.split()
        s = {n: sem(n) for n in names}
        row_gathered = [sem(f"row_gathered_{r}") for r in range(RING)]
        row_scattered = [sem(f"row_scattered_{r}") for r in range(RING)]
        block = stack.enter_context(nc.Block())

        N_QK = 16 * 4
        N_VO = 16 * 4
        N_CROSS = 16 * 9
        N_FFN = 16 * (2 * E + 2)

        def wait_alone(eng, semaphore, n):
            eng.wait_ge(semaphore, n)
            if not isinstance(n, int):
                eng.nop(nofuse=True)

        def at(t, start, n, p=128):
            return t[0:p, ds(start, n)]

        def grouped(ap):
            return ap.rearrange("p (g n) -> p g n", g=G)

        def spread(ap, shape):
            return ap.to_broadcast(shape)

        def passes(eng, run):
            for g in range(-3, 2):
                run(g)
            with eng.Fori(2, NG - 4) as g:
                run(g)
            for g in range(NG - 4, NG + 1):
                run(g)

        def stages(g):
            if not isinstance(g, int):
                return True, True, True, True
            return 0 <= g - 1, 0 <= g < NG, 0 <= g + 2 < NG, g + 3 < NG

        def half(g):
            return g % 2

        def before_cross(g):
            return isinstance(g, int) and -2 <= g < 0

        def last_group(g):
            return isinstance(g, int) and g == NG - 1

        def feats_count(f):
            return f + G if last_group(f) else f + 1

        def later(g, first):
            return not isinstance(g, int) or g >= first

        be = lambda ap: ap.rearrange("p (b e) -> p b e", e=E)
        eb = lambda ap: ap.rearrange("p (e b) -> p e b", b=B)
        chosen = carve("k", B * E)
        most = carve("k", B)
        counts = carve("k", 2 * E * B)
        running = carve("k", E * B)
        per_expert = carve("k", E)
        passed = carve("k", E * B)
        tiles_of = carve("k", E)
        tiles_end = carve("k", E)
        shift_of = carve("k", E)
        ones_f = carve("k", E * B)
        slot = carve("k", B)
        slot_i = carve("k", B, I32)
        hi_i = carve("k", B, I32)
        lo_i = carve("k", B, I32)
        hi_bf = carve("k", B, BF16)
        neg_lo = carve("k", B)
        lo_f = carve("k", B)
        hi_eq = carve("k", B * NTC, BF16)
        after = carve("k", NTC * E)
        expert_f = carve("k", NTC)
        token_f = carve("k", NTC)
        empty_f = carve("k", NTC)
        index_f = carve("k", NTC)

        LO_CHUNK = 8
        ACT_LO = B // 2

        col = lambda ap: ap.rearrange("p (b a) -> p b a", a=1)
        row = lambda ap: ap.rearrange("p (a n) -> p a n", a=1)

        def route_vector(dve):
            step = [0]

            def link(ins):
                step[0] += 1
                ins.then_inc(s["route_step"], 1)
                dve.wait_ge(s["route_step"], step[0])

            dve.wait_ge(s["aff_ready"], NG)
            dve.wait_ge(s["iota_made"], 5)
            dve.wait_ge(s["attended_ready"], B)
            dve.wait_ge(s["s2_done"], 4 * B)
            link(dve.tensor_reduce(most, aff[:, :, :], AX.X, ALU.max))
            link(dve.tensor_tensor(be(chosen), aff[:, :, :], spread(most.rearrange("p (b a) -> p b a", a=1), [128, B, E]),
                                   ALU.is_equal))
            link(dve.tensor_scalar(per_expert, iota_f[:, 0:E], -1.0, float(E), ALU.mult, ALU.add))
            link(dve.tensor_tensor(be(chosen), be(chosen), spread(per_expert.rearrange("p (a e) -> p a e", a=1), [128, B, E]),
                                   ALU.mult))
            link(dve.tensor_reduce(most, be(chosen), AX.X, ALU.max))
            link(dve.tensor_tensor(onehot.rearrange("p (e b) -> p b e", b=B), be(chosen),
                                   spread(most.rearrange("p (b a) -> p b a", a=1), [128, B, E]), ALU.is_equal))
            dve.memset(ones_f, 1.0).then_inc(s["onehot_ready"], 1)
            dve.wait_ge(s["counts_done"], 1)
            link(dve.tensor_copy(counts, s1_bank[:, 0:2 * E * B]))
            total = counts[:, E * B:2 * E * B]
            dve.wait_ge(s["onehot_ready"], 1)
            link(dve.tensor_tensor_scan(running, ones_f, total, 0.0, ALU.mult, ALU.add))
            link(dve.tensor_reduce(per_expert, eb(total), AX.X, ALU.add))
            link(dve.tensor_scalar(chosen[:, 0:B], iota_f[:, 0:B], 128.0, None, ALU.mult))
            link(dve.tensor_tensor(eb(passed), spread(per_expert.rearrange("p (e a) -> p e a", a=1), [128, E, B]),
                                   spread(chosen[:, 0:B].rearrange("p (a b) -> p a b", a=1), [128, E, B]), ALU.is_gt))
            link(dve.tensor_reduce(tiles_of, eb(passed), AX.X, ALU.add))
            link(dve.tensor_tensor_scan(tiles_end, ones_f[:, 0:E], tiles_of, 0.0, ALU.mult, ALU.add))
            link(dve.tensor_tensor(shift_of, tiles_end, tiles_of, ALU.subtract))
            link(dve.scalar_tensor_tensor(shift_of, shift_of, 128.0, per_expert, ALU.mult, ALU.add))
            link(dve.tensor_tensor(shift_of, shift_of, eb(running)[:, :, B - 1], ALU.subtract))
            link(dve.tensor_tensor(running, running, total, ALU.subtract))
            link(dve.tensor_tensor(running, running, counts[:, 0:E * B], ALU.add))
            link(dve.tensor_tensor(eb(running), eb(running), spread(shift_of.rearrange("p (e a) -> p e a", a=1), [128, E, B]),
                                   ALU.add))
            link(dve.tensor_tensor(running, running, onehot, ALU.mult))
            link(dve.tensor_reduce(slot, running.rearrange("p (e b) -> p b e", b=B), AX.X, ALU.add))
            link(dve.tensor_copy(slot_i, slot))
            link(dve.tensor_scalar(lo_i, slot_i, 127, None, ALU.bitwise_and))
            dve.tensor_scalar(neg_lo, lo_i, -1.0, None, ALU.mult).then_inc(s["lo_ready"], 1)
            dve.tensor_copy(lo_f, lo_i).then_inc(s["lo_ready"], 1)
            link(dve.tensor_scalar(hi_i, slot_i, 7, None, ALU.logical_shift_right))
            link(dve.tensor_copy(hi_bf, hi_i))
            link(dve.tensor_tensor(hi_eq.rearrange("p (b n) -> p b n", b=B), spread(row(iota_bf[:, 0:NTC]), [128, B, NTC]),
                                   spread(col(hi_bf), [128, B, NTC]), ALU.is_equal))
            parts = hi_hot.rearrange("p (b k n) -> p b k n", b=B, k=2)
            heq = hi_eq.rearrange("p (b n) -> p b n", b=B)
            dve.tensor_scalar(parts[:, :, 0, :], heq, place_f[:, 0:1], None, ALU.mult).then_inc(s["slots_ready"], 1)
            dve.tensor_tensor(parts[:, :, 1, :], heq, spread(col(iota_bf[:, 0:B]), [128, B, NTC]), ALU.mult)\
               .then_inc(s["slots_ready"], 1)
            dve.wait_ge(s["lo_ready"], 2)
            for b in range(ACT_LO, B, LO_CHUNK):
                dve.tensor_tensor(lo_hot[:, b * 128:(b + LO_CHUNK) * 128].rearrange("p (b n) -> p b n", b=LO_CHUNK),
                                  spread(row(iota_bf[:, :]), [128, LO_CHUNK, 128]),
                                  spread(col(lo_f[:, b:b + LO_CHUNK]), [128, LO_CHUNK, 128]),
                                  ALU.is_equal).then_inc(s["slots_ready"], 1)
            dve.wait_ge(s["tok_done"], 1)
            link(dve.tensor_copy(token_f, self_bank[:, 0:NTC]))
            link(dve.tensor_scalar(index_f, self_bank[:, NTC:2 * NTC], float(S), -1.0, ALU.mult, ALU.add))
            link(dve.tensor_tensor(index_f, token_f, index_f, ALU.add))
            dve.tensor_scalar(gather_idx[:, :], index_f, 0.0, None, ALU.max).then_inc(s["tok_ready"], 1)
            link(dve.tensor_scalar(empty_f, token_f, 0.5, float(2 * B * S), ALU.is_lt, ALU.mult))
            dve.tensor_tensor(scatter_idx[:, :], empty_f, index_f, ALU.add).then_inc(s["tok_ready"], 1)
            link(dve.tensor_tensor(after.rearrange("p (t e) -> p t e", e=E), spread(col(iota_f[:, 0:NTC]), [128, NTC, E]),
                                   spread(row(tiles_end), [128, NTC, E]), ALU.is_ge))
            link(dve.tensor_reduce(expert_f, after.rearrange("p (t e) -> p t e", e=E), AX.X, ALU.add))
            link(dve.tensor_scalar(expert_f, expert_f, float(E - 1), None, ALU.min))
            dve.tensor_copy(tile_expert[:, :], expert_f).then_inc(s["experts_ready"], 1)
            dve.wait_ge(s["experts_ready"], 1)
            ffn_vector(dve)

        def tiles(eng, step, first, last):
            for t in range(first, RING):
                step(t // RING, t % RING)
            with eng.Fori(1, NTILE // RING) as i:
                for r in range(RING):
                    step(i, r)
            for t in range(NTILE // RING * RING, last):
                step(t // RING, t % RING)

        def tile(i, r, ahead):
            t = RING * i + r + ahead
            return t, (r + ahead) % RING, not isinstance(i, int) or 0 <= t < NTILE

        def expert_of(eng, t):
            col = tile_expert[0:1, t:t + 1] if isinstance(t, int) else tile_expert[0:1, ds(t, 1)]
            return eng.value_load(col, min_val=0, max_val=E - 1)

        def ffn_tensor(pe):
            pe.wait_ge(s["onehot_ready"], 1)
            pe.wait_ge(s["iota_made"], 5)
            pe.matmul(s1_bank[:, 0:E * B], earlier[:, :], onehot, start=True, stop=True)
            pe.matmul(s1_bank[:, E * B:2 * E * B], all_ones[:, :], onehot, start=True, stop=True)\
              .then_inc(s["counts_done"], 1)
            pe.wait_ge(s["slots_ready"], 2)
            order = [*range(0, LO_CHUNK), *range(ACT_LO, B), *range(LO_CHUNK, ACT_LO)]
            for b in order:
                if b % LO_CHUNK == 0 and b < ACT_LO:
                    pe.wait_ge(s["lo_hot_made"], 1 + b // LO_CHUNK)
                elif b % LO_CHUNK == 0:
                    pe.wait_ge(s["slots_ready"], 3 + (b - ACT_LO) // LO_CHUNK)
                m = pe.matmul(self_bank[:, 0:2 * NTC], lo_hot[:, b * 128:(b + 1) * 128],
                              hi_hot[:, b * 2 * NTC:(b + 1) * 2 * NTC], start=b == order[0], stop=b == order[-1])
            m.then_inc(s["tok_done"], 1)
            pe.wait_ge(s["experts_ready"], 1)
            pe.wait_ge(s["b1_ready"], E)
            pe.wait_ge(s["w1_scaled"], E)

            def step(i, r):
                t, k, there = tile(i, r, 1)
                if there:
                    q = t // RING if isinstance(t, int) else (i + (1 if r + 1 >= RING else 0))
                    pe.wait_ge(row_gathered[k], 16 * (q + 1))
                    if not isinstance(i, int) or t >= 1:
                        pe.wait_ge(s["row_t_ready"], t)
                    pe.transpose(cross_bank[:, 0:128], ffn_row[k][:, 0:D], ident[:, :]).then_inc(s["row_transposed"], 1)
                t, k, there = tile(i, r, 0)
                if there:
                    pe.wait_ge(s["row_t_ready"], t + 1)
                    pe.wait_ge(s["w1_picked"], t + 1)
                    if not isinstance(i, int) or t >= 2:
                        pe.wait_ge(s["hid_ready"], t - 1)
                    for c in range(FC):
                        m = pe.matmul(s1_bank[:, (k % 2) * F + c * 128:(k % 2) * F + (c + 1) * 128],
                                      ffn_w1[k % 2][:, c * 128:(c + 1) * 128], ffn_row_t[k % 2], start=True, stop=True)
                    m.then_inc(s["hid_done"], 1)
                t, k, there = tile(i, r, -1)
                if there:
                    e = expert_of(pe, t)
                    pe.wait_ge(s["relu_ready"], t + 1)
                    if not isinstance(i, int) or t >= 2:
                        pe.wait_ge(s["y_biased"], t - 1)
                    bank = (pv_bank, self_bank)[k % 2]
                    for c in range(FC):
                        m = pe.matmul(bank[:, 0:D], ffn_relu[k % 2][:, c * 128:(c + 1) * 128],
                                      at(w2, e * (FC * D) + c * D, D), start=c == 0, stop=c == FC - 1)
                    m.then_inc(s["y_done"], 1)

            tiles(pe, step, -1, NTILE + 1)

        def ffn_vector(dve):
            def step(i, r):
                t, k, there = tile(i, r, 1)
                if there:
                    e = expert_of(dve, t)
                    dve.wait_ge(s["hid_done"], t + 1)
                    if not isinstance(i, int) or t >= 2:
                        dve.wait_ge(s["relu_ready"], t - 1)
                    by_chunk = lambda ap: ap.rearrange("p (c n) -> p c n", c=FC)
                    dve.tensor_tensor(by_chunk(ffn_hid[k % 2]), by_chunk(s1_bank[:, (k % 2) * F:(k % 2 + 1) * F]),
                                      spread(at(b1_cols, e * FC, FC).rearrange("p (c a) -> p c a", a=1), [128, FC, 128]),
                                      ALU.add).then_inc(s["hid_ready"], 1)
                t, k, there = tile(i, r, 0)
                if there:
                    e = expert_of(dve, t)
                    bank = (pv_bank, self_bank)[k % 2]
                    dve.wait_ge(s["y_done"], t + 1)
                    dve.tensor_tensor(ffn_y[k % 2], bank[:, 0:D], at(b2_rows, e * D, D), ALU.add).then_inc(s["y_biased"], 1)
                    dve.wait_ge(s["y_biased"], t + 1)
                    dve.wait_ge(row_gathered[k], 16 * (i + 1))
                    if not isinstance(i, int) or t >= RING:
                        dve.wait_ge(row_scattered[k], 16 * i)
                    dve.scalar_tensor_tensor(ffn_out[k], ffn_y[k % 2], ffn_row[k][:, 2 * D:2 * D + 1], ffn_row[k][:, D:2 * D],
                                             ALU.mult, ALU.add).then_inc(s["result_ready"], 1)

            tiles(dve, step, -1, NTILE)

        def ffn_scalar(act):
            def step(i, r):
                t, k, there = tile(i, r, 1)
                if there:
                    act.wait_ge(s["row_transposed"], t + 1)
                    if not isinstance(i, int) or t >= 2:
                        act.wait_ge(s["hid_done"], t - 1)
                    act.activation(ffn_row_t[k % 2], cross_bank[:, 0:128], ACT.Copy).then_inc(s["row_t_ready"], 1)
                t, k, there = tile(i, r, 2)
                if there:
                    e = expert_of(act, t)
                    if not isinstance(i, int) or t >= 2:
                        act.wait_ge(s["hid_done"], t - 1)
                    act.activation(ffn_w1[k % 2], at(w1, e * F, F), ACT.Copy).then_inc(s["w1_picked"], 1)
                t, k, there = tile(i, r, 0)
                if there:
                    act.wait_ge(s["hid_ready"], t + 1)
                    if not isinstance(i, int) or t >= 2:
                        act.wait_ge(s["y_done"], t - 1)
                    act.activation(ffn_relu[k % 2], ffn_hid[k % 2], ACT.Relu).then_inc(s["relu_ready"], 1)

            act.wait_ge(s["lo_ready"], 1)
            for b in range(ACT_LO):
                if b % LO_CHUNK == 0 and b > 0:
                    act.wait_ge(s["lo_hot_made"], b // LO_CHUNK)
                act.activation(apart[:, (b % LO_CHUNK) * 128:(b % LO_CHUNK + 1) * 128], iota_f[:, :], ACT.Square,
                               bias=neg_lo[:, b:b + 1]).then_inc(s["apart_ready"], 1)
                if (b + 1) % LO_CHUNK == 0:
                    act.wait_ge(s["apart_ready"], b + 1)
                    act.activation(lo_hot[:, (b + 1 - LO_CHUNK) * 128:(b + 1) * 128], apart, ACT.Relu,
                                   bias=1.0, scale=-1.0).then_inc(s["lo_hot_made"], 1)
            act.wait_ge(s["experts_ready"], 1)
            act.wait_ge(s["w1_scaled"], E)
            tiles(act, step, -2, NTILE)

        def ffn_pool(pool):
            wait_alone(pool, s["s2_done"], 4 * B)
            wait_alone(pool, s["pay_stored"], 16 * NG)
            wait_alone(pool, s["tok_ready"], 1)

            for t in range(NTILE + RING):
                k, old = t % RING, t - RING
                if old == 0:
                    wait_alone(pool, s["tok_ready"], 2)
                if old >= 0:
                    pool.wait_ge(s["result_ready"], old + 1)
                if t < NTILE:
                    pool.indirect_dma_start(out=ffn_row[k], out_offset=None, in_=rows,
                                            in_offset=bass.IndirectOffsetOnAxis(ap=gather_idx[:, t:t + 1].bitcast(U32), axis=0))\
                        .then_inc(row_gathered[k], 16)
                if old >= 0:
                    pool.indirect_dma_start(out=out_rows,
                                            out_offset=bass.IndirectOffsetOnAxis(ap=scatter_idx[:, old:old + 1].bitcast(U32), axis=0),
                                            in_=ffn_out[k], in_offset=None, bounds_check=B * S - 1,
                                            oob_is_err=False).then_inc(row_scattered[k], 16)
            for k in range(RING):
                n = len(range(k, NTILE, RING))
                wait_alone(pool, row_scattered[k], 16 * n)

        @block.sync
        def _(sp):
            def load_x(g):
                sp.dma_start(grouped(at(x_in, (g % 4) * GS, GS)),
                             T["x"][ds(g * G, G), :, :].rearrange("b s d -> s b d")).then_inc(s["x_loaded"], 16)

            def load_ctx(g):
                sp.dma_start(grouped(ctx_in[:, :]),
                             T["ctx_1024"][ds(g * G, G), :, :].rearrange("b s d -> s b d")).then_inc(s["ctx_loaded"], 16)

            load_x(0)
            column = lambda src: T[src].rearrange("(p a) -> p a", a=1)
            for dst, src in ((wq_t[:, :], T["wq_t"]), (wk_t[:, :], T["wk_t"]), (bias_cols[:, 0:1], column("bq")),
                             (bias_cols[:, 1:2], column("bk"))):
                sp.dma_start(dst, src).then_inc(s["qk_loaded"], 16)
            for dst, src in ((wv[:, :], T["wv"]), (wo_t[:, :], T["wo_t"]), (bv_col[:, :], column("bv")),
                             (bo_rows[:, :], T["bo"].partition_broadcast(128))):
                sp.dma_start(dst, src).then_inc(s["vo_loaded"], 16)
            wait_alone(sp, s["x_loaded"], 16)
            load_x(1)
            load_ctx(0)

            def store(g, name, parts, scratch, reads):
                for a in range(NPART):
                    if a == 0:
                        wait_alone(sp, s[name + "_split"], g + 1)
                        if later(g, 1):
                            wait_alone(sp, s[name + "_stacked"], 16 * reads * g)
                    sp.dma_start(scratch[:, a, :, :], parts[:, a, :]).then_inc(s[name + "_stored"], 16)

            def stack_parts(g, name, scratch, stacked, pieces):
                wait_alone(sp, s[name + "_stored"], 16 * NPART * (g + 1))
                if not later(g, 1):
                    sp.wait_ge(s[name + "_zeroed"], 1)
                if later(g, 2):
                    wait_alone(sp, s["s2_done"], 16 * (g - 1))
                for row, a, n in pieces:
                    src = scratch[:, a:a + n, :, :].rearrange("h c d t -> (c d) h t")
                    dst = stacked[row * HD:(row + n) * HD, ds(half(g) * H * GS, H * GS)]
                    sp.dma_start(dst.rearrange("p (h t) -> p h t", h=H), src).then_inc(s[name + "_stacked"], 16)

            def load_biases():
                wait_alone(sp, s["attn_done"], NG)
                wait_alone(sp, s["x_bo_ready"], NG)
                sp.dma_start(b1_cols[:, :], T["b1_t"]).then_inc(s["ffn_loaded"], 16)
                sp.dma_start(b2_rows, T["b2"].rearrange("e d -> (e d)").partition_broadcast(128)).then_inc(s["ffn_loaded"], 16)

            def load_later_x(g):
                if isinstance(g, int) and g + 5 < NG:
                    if later(g, -1):
                        wait_alone(sp, s["x_bo_ready"], g + 2)
                    wait_alone(sp, s["x_loaded"], 16 * (g + 5))
                    load_x(g + 5)

            def run(g):
                has_f, has_c, has_e, has_s = stages(g)
                if not before_cross(g):
                    load_later_x(g)
                if not isinstance(g, int) or 0 <= g + 1 < NG:
                    if not before_cross(g):
                        stack_parts(g + 1, "xk", k_scratch, k_stack, K_PIECES)
                    stack_parts(g + 1, "xq", q_scratch, q_stack, Q_PIECES)
                if before_cross(g):
                    load_later_x(g)
                if not isinstance(g, int) or 0 < g + 3 < NG:
                    wait_alone(sp, s["ctx_transposed"], g + 3)
                    wait_alone(sp, s["ctx_loaded"], 16 * (g + 3))
                    load_ctx(g + 3)
                if has_e:
                    store(g + 2, "xk", xk_parts, k_scratch, len(K_PIECES))
                    if isinstance(g, int) and g == -2:
                        stack_parts(0, "xk", k_scratch, k_stack, K_PIECES)
                if isinstance(g, int) and g == NG - 3:
                    load_biases()
                if has_f:
                    wait_alone(sp, s["pay_ready"], g)
                    wait_alone(sp, s["alpha_ready"], g)
                    sp.dma_start(rows[ds((g - 1) * GS, GS), :].rearrange("(b s) c -> s b c", s=S),
                                 pay[:, :, :]).then_inc(s["pay_stored"], 16)
                if has_e:
                    store(g + 2, "xq", xq_parts, q_scratch, len(Q_PIECES))

            def load_ffn():
                for e in range(E):
                    sp.dma_start(at(w1, e * F, F), T["w1"][e, :, :]).then_inc(s["ffn_loaded"], 16)
                    sp.dma_start(at(w2, e * FC * D, FC * D).rearrange("p (c d) -> p c d", c=FC),
                                 T["w2"][e, :, :].rearrange("(c p) d -> p c d", c=FC)).then_inc(s["ffn_loaded"], 16)

            for g in range(-3, NG - 5):
                if g == 1:
                    load_ffn()
                run(g)
            with sp.Fori(NG - 5, NG - 3) as g:
                run(g)
            for g in range(NG - 3, NG):
                run(g)
            run(NG)

        def norm_stats(dve, n, src, base, g, ready, count):
            dve.wait_ge(s[ready], count)
            if not isinstance(g, int) or g >= 1:
                dve.wait_ge(s[f"ln{n}_centred"], g)
            for b in range(G):
                dve.bn_stats(stats[n][:, b, :], at(src, base + b * S, S)).then_inc(s[f"ln{n}_stats"], 1)

        def norm_moments(dve, n, g):
            for b in range(G):
                wait_alone(dve, s[f"ln{n}_stats"], G * g + b + 1)
                dve.bn_aggr(moments[n][:, b, :], stats[n][:, b, :]).then_inc(s[f"ln{n}_moments"], 1)
            dve.wait_ge(s[f"ln{n}_moments"], G * g + G)
            dve.tensor_scalar(var_eps[n][:, :], moments[n][:, :, 1], EPS, None, ALU.add).then_inc(s[f"ln{n}_var"], 1)

        def norm_rstd(pool, n, g):
            wait_alone(pool, s[f"ln{n}_var"], g + 1)
            pool.tensor_tensor(rstd[n][:, :], var_eps[n][:, :], minus_half[:, :], ALU.pow).then_inc(s[f"ln{n}_rstd"], 1)

        def norm_apply(pool, n, g, src, centred_buf, dst, done):
            shape = [128, G, S]
            pool.tensor_tensor(grouped(centred_buf), grouped(src), spread(moments[n][:, :, 0:1], shape),
                               ALU.subtract).then_inc(s[f"ln{n}_centred"], 1)
            wait_alone(pool, s[f"ln{n}_centred"], g + 1)
            wait_alone(pool, s[f"ln{n}_rstd"], g + 1)
            pool.tensor_tensor(grouped(dst), grouped(centred_buf),
                               spread(rstd[n][:, :].rearrange("p (g a) -> p g a", a=1), shape),
                               ALU.mult).then_inc(s[done], 1)

        @block.gpsimd
        def _(pool):
            pool.memset(ident[:, :], 0.0).then_inc(s["consts_made"], 1)
            pool.memset(ident_bf[:, :], 0.0).then_inc(s["consts_made"], 1)
            pool.memset(minus_half[:, :], -0.5).then_inc(s["consts_made"], 1)
            wait_alone(pool, s["consts_made"], 3)
            for m in (ident, ident_bf):
                pool.affine_select(out=m[:, :], in_=m[:, :], compare_op=ALU.not_equal, fill=1.0, base=0,
                                   pattern=[[-1, 128]], channel_multiplier=1).then_inc(s["consts_made"], 1)

            def later_constants():
                pool.memset(head_sel[:, :, :], 0.0).then_inc(s["consts_made"], 1)
                pool.memset(xv[:, :], 1.0).then_inc(s["ones_made"], 1)
                pool.memset(hmax_parts[:, :], 0.0).then_inc(s["ones_made"], 1)
                pool.memset(earlier[:, :], 1.0).then_inc(s["consts_made"], 1)
                pool.memset(all_ones[:, :], 1.0).then_inc(s["consts_made"], 1)
                pool.iota(iota_i[:, :], pattern=[[1, 128]], base=0, channel_multiplier=0).then_inc(s["consts_made"], 1)
                pool.iota(place_i[:, :], pattern=[[0, 1]], base=1, channel_multiplier=1).then_inc(s["consts_made"], 1)
                wait_alone(pool, s["consts_made"], 10)
                pool.affine_select(out=earlier[:, :], in_=earlier[:, :], compare_op=ALU.is_gt, fill=0.0, base=0,
                                   pattern=[[1, 128]], channel_multiplier=-1).then_inc(s["iota_made"], 1)
                pool.tensor_copy(iota_f[:, :], iota_i[:, :]).then_inc(s["iota_made"], 1)
                pool.tensor_copy(iota_bf[:, :], iota_i[:, :]).then_inc(s["iota_made"], 1)
                pool.tensor_copy(place_f[:, :], place_i[:, :]).then_inc(s["iota_made"], 1)
                pool.memset(pay[:, :, 2 * D:PAY], 0.0).then_inc(s["iota_made"], 1)
                for i in range(2):
                    if i > 0:
                        wait_alone(pool, s["sel_made"], i)
                    pool.affine_select(out=head_sel[:, :, :], in_=head_sel[:, :, :], compare_op=ALU.not_equal, fill=1.0,
                                       base=-H * i, pattern=[[-1, H], [0, 128]], channel_multiplier=1)\
                        .then_inc(s["sel_made"], 1)

            def split_rest(g, name, full, rest, parts):
                wait_alone(pool, s[name + "_ready"], 2 * g + 2)
                if name == "xq":
                    wait_alone(pool, s["xk_split"], g + 1)
                elif later(g, 1):
                    wait_alone(pool, s["xq_split"], g)
                pool.tensor_tensor(rest[:, :], full[:, :], parts[:, 0, :], ALU.subtract).then_inc(s[name + "_rest_ready"], 1)

            def split_last(g, name, rest, parts):
                wait_alone(pool, s[name + "_part1"], g + 1)
                pool.tensor_tensor(parts[:, 2, :], rest[:, :], parts[:, 1, :], ALU.subtract).then_inc(s[name + "_split"], 1)

            def add_attended(g, j):
                n = G * g + j
                wait_alone(pool, s["attended_ready"], n + 1)
                pool.tensor_tensor(at(x2, half(g) * GS + j * S, S), at(x1_bv, (g % 4) * GS + j * S, S),
                                   attended[:, (j % 2) * S:(j % 2 + 1) * S], ALU.add).then_inc(s["x2_ready"], 1)

            def first_norm(h):
                if later(h, 1):
                    wait_alone(pool, s["xn_ready"], h)
                norm_rstd(pool, 0, h)
                if later(h, 1):
                    wait_alone(pool, s["xn_transposed"], h)
                norm_apply(pool, 0, h, at(x_in, (h % 4) * GS, GS), centred[:, :], xn[:, :], "xn_ready")

            def scale_w1(e):
                wait_alone(pool, s["b1_done"], e + 1)
                pool.tensor_scalar(w1[:, e * F:(e + 1) * F], w1[:, e * F:(e + 1) * F], gamma_t[:, e:e + 1], 1.0,
                                   ALU.mult, ALU.mult).then_inc(s["w1_scaled"], 1)

            def run(g):
                has_f, has_c, has_e, has_s = stages(g)
                f, e, h = g - 1, g + 2, g + 3
                if isinstance(g, int) and g == NG - 1:
                    for expert in range(E // 2):
                        scale_w1(expert)
                if isinstance(g, int) and g == -2:
                    pool.wait_ge(s["vo_loaded"], N_VO)
                    pool.wait_ge(s["cross_loaded"], N_CROSS)
                if has_f:
                    add_attended(f, 3)
                if not isinstance(g, int) or 0 <= e - 1 < NG:
                    split_last(e - 1, "xq", rest, xq_parts)
                if has_e:
                    if later(e, 1):
                        wait_alone(pool, s["x1_ready"], e)
                    pool.tensor_tensor(grouped(x_bo[:, :]), grouped(at(x_in, (e % 4) * GS, GS)),
                                       spread(bo_rows[:, :].rearrange("p (a n) -> p a n", a=1), [128, G, S]),
                                       ALU.add).then_inc(s["x_bo_ready"], 1)
                    split_rest(e, "xk", xk, rest, xk_parts)
                if before_cross(g):
                    if e > 0:
                        wait_alone(pool, s["xn2_ready"], e)
                    first_norm(h + 1)
                if has_c:
                    if later(g, 2):
                        wait_alone(pool, s["pay_ready"], g - 1)
                    add_attended(g, 0)
                if has_e:
                    split_last(e, "xk", rest, xk_parts)
                if has_f:
                    norm_rstd(pool, 2, f)
                    if later(f, 1):
                        wait_alone(pool, s["feats_transposed"], f)
                    if not last_group(f):
                        norm_apply(pool, 2, f, at(x2, half(f) * GS, GS), centred[:, :], feats[:, :], "feats_ready")
                if has_e:
                    norm_rstd(pool, 1, e)
                    if later(e, 1):
                        wait_alone(pool, s["xn2_transposed"], e)
                    if has_f:
                        wait_alone(pool, s["feats_ready"], feats_count(f))
                    elif before_cross(g):
                        wait_alone(pool, s["xn_ready"], h + 2)
                    norm_apply(pool, 1, e, x1[:, :], centred[:, :], xn2[:, :], "xn2_ready")
                if has_c:
                    add_attended(g, 1)
                if has_f:
                    wait_alone(pool, s["ln2_rstd"], f + 1)
                    pool.tensor_tensor(var2[:, :], rstd[2][:, :], rstd[2][:, :], ALU.mult).then_inc(s["rstd2_step"], 1)
                    wait_alone(pool, s["rstd2_step"], 3 * f + 1)
                    pool.tensor_tensor(rstd2[:, :], var2[:, :], moments[2][:, :, 1], ALU.mult).then_inc(s["rstd2_step"], 1)
                    wait_alone(pool, s["rstd2_step"], 3 * f + 2)
                    pool.tensor_scalar(var2[:, :], rstd2[:, :], 1.0, EPS, ALU.mult, ALU.add).then_inc(s["rstd2_step"], 1)
                    wait_alone(pool, s["rstd2_step"], 3 * f + 3)
                    pool.tensor_tensor(rstd2[:, :], var2[:, :], minus_half[:, :], ALU.pow).then_inc(s["rstd2_ready"], 1)
                    if later(f, 1):
                        wait_alone(pool, s["pay_stored"], 16 * f)
                    wait_alone(pool, s["feats_ready"], feats_count(f))
                    pool.tensor_tensor(pay[:, :, D:2 * D], grouped(at(x2, half(f) * GS, GS)), grouped(feats[:, :]),
                                       ALU.add).then_inc(s["base_ready"], 1)
                if has_c:
                    add_attended(g, 2)
                if isinstance(g, int) and g == NG - 1:
                    for expert in range(E // 2, E):
                        scale_w1(expert)
                if has_e:
                    pool.tensor_tensor(grouped(at(x1_bv, (e % 4) * GS, GS)), grouped(x1[:, :]),
                                       spread(xbv_rows[:, :].rearrange("p (a n) -> p a n", a=1), [128, G, S]),
                                       ALU.add).then_inc(s["x1_bv_ready"], 1)
                if has_f:
                    wait_alone(pool, s["rstd2_ready"], f + 1)
                    pool.tensor_tensor(pay[:, :, 0:D], grouped(feats[:, :]),
                                       spread(rstd2[:, :].rearrange("p (g a) -> p g a", a=1), [128, G, S]),
                                       ALU.mult).then_inc(s["pay_ready"], 1)
                if not isinstance(g, int) or h + 1 < NG and not before_cross(g):
                    if has_e:
                        wait_alone(pool, s["xn2_ready"], e + 1)
                    first_norm(h + 1)
                if isinstance(g, int) and g == -3:
                    pool.memset(q_stack[:, :].bitcast(F32), 0.0).then_inc(s["xq_zeroed"], 1)
                if has_e:
                    split_rest(e, "xq", xq, rest, xq_parts)

            first_norm(0)
            later_constants()
            passes(pool, run)
            ffn_pool(pool)

        @block.vector
        def _(dve):
            def first_norm(h):
                norm_stats(dve, 0, x_in, (h % 4) * GS, h, "x_loaded", 16 * (h + 1))
                norm_moments(dve, 0, h)

            first_norm(0)
            def topk(g, r):
                for b in range(G):
                    src = scores if r == 0 else left
                    if r == 0 and b == 0:
                        wait_alone(dve, s["scores_ready"], g + 1)
                    elif r > 0:
                        wait_alone(dve, s["topk_step"], 32 * g + 8 * (r - 1) + 4 + b + 1)
                    dve.max(best8[:, b, r, :], at(src, b * S, S)).then_inc(s["topk_step"], 1)
                for b in range(G):
                    src = scores if r == 0 else left
                    wait_alone(dve, s["topk_step"], 32 * g + 8 * r + b + 1)
                    dve.match_replace(at(left, b * S, S), best8[:, b, r, :], at(src, b * S, S), TAKEN)\
                       .then_inc(s["topk_step"], 1)

            def head_max(g, j, u):
                n, q = G * g + j, 16 * g + 4 * j + u
                dve.wait_ge(s["s1_done"], q + 1)
                bank = s1_bank[:, (u % 2) * GS:(u % 2 + 1) * GS]
                dve.tensor_reduce(neg_hmax[:, (j % 2) * H + u * 4:(j % 2) * H + u * 4 + 4], bank.rearrange("p (h k) -> p h k", k=S),
                                  AX.X, ALU.max, negate=True).then_inc(s["s1_max"], 1)

            def hmax_split(g, j):
                n, i = G * g + j, j % 2
                dve.wait_ge(s["s1_max"], 4 * n + 4)
                if later(n, 2):
                    dve.wait_ge(s["hmax_transposed"], n - 1)
                parts = [hmax_parts[:, i * 128 + a * H:i * 128 + (a + 1) * H] for a in range(2)]
                maxima = neg_hmax[:, i * H:(i + 1) * H]
                dve.tensor_copy(parts[0], maxima).then_inc(s["hmax_step"], 1)
                dve.wait_ge(s["hmax_step"], n + 1)
                dve.tensor_tensor(parts[1], maxima, parts[0], ALU.subtract).then_inc(s["hmax_split"], 1)

            def normalise(g, j):
                n, i = G * g + j, j % 2
                pv = pv_bank[:, i * 512:i * 512 + H * HC].rearrange("p (h c) -> p h c", c=HC)
                dve.wait_ge(s["pv_done"], 4 * n + 4)
                dve.reciprocal(wsum_inv[:, :], pv[:, :, HD]).then_inc(s["wsum_inv_ready"], 1)
                dve.wait_ge(s["wsum_inv_ready"], n + 1)
                if later(n, 2):
                    dve.wait_ge(s["x2_ready"], n - 1)
                dve.tensor_tensor(attended[:, i * S:(i + 1) * S].rearrange("p (h d) -> p h d", d=HD), pv[:, :, 0:HD],
                                  spread(wsum_inv[:, :].rearrange("p (h a) -> p h a", a=1), [128, H, HD]),
                                  ALU.mult).then_inc(s["attended_ready"], 1)

            def next_maxima(g, j, u):
                g2, j2 = (g, j + 1) if j + 1 < G else (g + 1, 0)
                if isinstance(g2, int) and not 0 <= g2 < NG:
                    return
                head_max(g2, j2, u)
                head_max(g2, j2, u + 1)
                if u == 2:
                    hmax_split(g2, j2)

            def expert_bias(g, n):
                if isinstance(g, int) and NG - 2 <= g < NG:
                    expert = (g - (NG - 2)) * (E // 2) + n
                    place = b1_cols[:, expert * FC:(expert + 1) * FC]
                    if expert == 0:
                        dve.wait_ge(s["ffn_loaded"], N_FFN)
                    dve.wait_ge(s["b1_done"], expert + 1)
                    dve.tensor_tensor(place, self_bank[:, 0:F].rearrange("p (c n) -> p c n", c=FC)[:, :, 0], place, ALU.add).then_inc(s["b1_ready"], 1)

            def run(g):
                has_f, has_c, has_e, has_s = stages(g)
                f, e, h = g - 1, g + 2, g + 3
                if isinstance(g, int) and g == NG - 2:
                    dve.wait_ge(s["attn_done"], NG)
                    dve.tensor_copy(beta_cols.rearrange("p (e n) -> p e n", e=E),
                                    spread(beta_t[:, :].rearrange("p (e a) -> p e a", a=1), [128, E, 128]))\
                       .then_inc(s["beta_made"], 1)
                if not isinstance(g, int) or h + 1 < NG:
                    first_norm(h + 1)
                if isinstance(g, int) and g == -3:
                    dve.wait_ge(s["vo_loaded"], N_VO)
                    dve.tensor_copy(bv_cols[:, :], spread(bv_col[:, 0:1], [128, 128])).then_inc(s["bv_made"], 1)
                    dve.wait_ge(s["wvo_done"], 1)
                    dve.tensor_copy(wvo_t[:, :], cross_bank[:, 0:D]).then_inc(s["wvo_ready"], 1)
                    dve.tensor_copy(bvo_rows[:, :], cross_bank[:, D:2 * D]).then_inc(s["wvo_ready"], 1)
                    dve.memset(k_stack[:, :].bitcast(F32), 0.0).then_inc(s["xk_zeroed"], 1)
                if isinstance(g, int) and g == -1:
                    dve.wait_ge(s["ones_made"], 2)
                if has_f:
                    normalise(f, 3)
                if has_e:
                    wait_alone(dve, s["topk_step"], 32 * e + 29)
                    if later(e, 1):
                        dve.wait_ge(s["self_exp"], G * e)
                    dve.tensor_scalar(neg_max[:, :], best8[:, :, 0, 0], -SELF_SCALE, None, ALU.mult)\
                       .then_inc(s["neg_max_ready"], 1)
                if has_c:
                    next_maxima(g, 0, 0)
                if has_c:
                    next_maxima(g, 0, 2)
                if has_e:
                    wait_alone(dve, s["topk_step"], 32 * e + 32)
                    if later(e, 1):
                        dve.wait_ge(s["probs_n_ready"], G * e)
                    for b in range(G):
                        dve.wait_ge(s["self_exp"], G * e + b + 1)
                        dve.scalar_tensor_tensor(at(probs, b * S, S), at(left, b * S, S), TAKEN, at(expd, b * S, S),
                                                 ALU.is_equal, ALU.mult, accum_out=prob_sum[:, b:b + 1])\
                           .then_inc(s["probs_ready"], 1)
                    dve.wait_ge(s["probs_ready"], G * e + G)
                    dve.reciprocal(prob_inv[:, :], prob_sum[:, :]).then_inc(s["inv_ready"], 1)
                    dve.wait_ge(s["inv_ready"], e + 1)
                    if later(e, 1):
                        dve.wait_ge(s["probs_transposed"], e)
                    for b in range(G):
                        dve.tensor_scalar(at(probs_n, b * S, S), at(probs, b * S, S), prob_inv[:, b:b + 1], 0.0,
                                          ALU.mult, ALU.max).then_inc(s["probs_n_ready"], 1)
                expert_bias(g, 0)
                if has_c:
                    normalise(g, 0)
                    next_maxima(g, 1, 0)
                if has_f:
                    norm_stats(dve, 2, x2, half(f) * GS, f, "x2_ready", G * g)
                    if later(f, 1):
                        dve.wait_ge(s["rstd2_ready"], f)
                    norm_moments(dve, 2, f)
                if has_f and last_group(f):
                    dve.wait_ge(s["feats_transposed"], f)
                    dve.wait_ge(s["base_ready"], f)
                    dve.wait_ge(s["pay_ready"], f)
                    dve.wait_ge(s["ln2_rstd"], f + 1)
                    for b in range(G):
                        dve.tensor_scalar(at(feats, b * S, S), at(x2, half(f) * GS + b * S, S), moments[2][:, b, 0:1],
                                          rstd[2][:, b:b + 1], ALU.subtract, ALU.mult).then_inc(s["feats_ready"], 1)
                if has_c:
                    next_maxima(g, 1, 2)
                if isinstance(g, int) and g == -1:
                    topk(h, 0)
                    topk(h, 1)
                if has_e:
                    dve.wait_ge(s["attn_done"], e + 1)
                    dve.wait_ge(s["x_bo_ready"], e + 1)
                    if later(e, 1):
                        dve.wait_ge(s["x1_bv_ready"], e)
                    dve.tensor_tensor(x1[:, :], cross_bank[:, :], x_bo[:, :], ALU.add).then_inc(s["x1_ready"], 1)
                    norm_stats(dve, 1, x1, 0, e, "x1_ready", e + 1)
                    norm_moments(dve, 1, e)
                expert_bias(g, 1)
                if has_c:
                    normalise(g, 1)
                    next_maxima(g, 2, 0)
                if has_s and not (isinstance(g, int) and g == -1):
                    topk(h, 0)
                if has_c:
                    next_maxima(g, 2, 2)
                if has_s:
                    if not (isinstance(g, int) and g == -1):
                        topk(h, 1)
                    dve.wait_ge(s["v_done"], h + 1)
                    if later(h, 2):
                        dve.wait_ge(s["attn_done"], h - 1)
                    dve.tensor_tensor(grouped(at(v, half(h) * GS, GS)), grouped(self_bank[:, :]),
                                      spread(bvo_rows[:, :].rearrange("p (a n) -> p a n", a=1), [128, G, S]),
                                      ALU.add).then_inc(s["v_ready"], 1)
                if has_f:
                    dve.wait_ge(s["aff_done"], g)
                    dve.tensor_copy(aff[:, ds(f * G, G), :],
                                    pv_bank[:, AFF:AFF + G * E].rearrange("p (b e) -> p b e", e=E))\
                       .then_inc(s["aff_ready"], 1)
                expert_bias(g, 2)
                if isinstance(g, int) and g == -1:
                    next_maxima(g, 3, 0)
                    next_maxima(g, 3, 2)
                if has_c:
                    normalise(g, 2)
                    next_maxima(g, 3, 0)
                if has_f:
                    wait_alone(dve, s["aff_ready"], g)
                    if later(f, 1):
                        wait_alone(dve, s["aff_exp_ready"], f)
                    dve.tensor_reduce(aff_max[:, :], aff[:, ds(f * G, G), :], AX.X, ALU.max).then_inc(s["aff_max_ready"], 1)
                if has_s:
                    topk(h, 2)
                if has_c:
                    next_maxima(g, 3, 2)
                if has_s:
                    topk(h, 3)
                if has_f:
                    dve.wait_ge(s["aff_exp_ready"], g)
                    dve.tensor_scalar(aff_den[:, :], aff_exp[:, :], 1.0, None, ALU.add).then_inc(s["aff_den_ready"], 1)
                expert_bias(g, 3)
                if has_f:
                    dve.wait_ge(s["aff_den_ready"], g)
                    if later(f, 1):
                        dve.wait_ge(s["pay_stored"], 16 * f)
                    dve.reciprocal(pay[:, :, 2 * D], aff_den[:, :]).then_inc(s["alpha_ready"], 1)

            passes(dve, run)
            route_vector(dve)

        @block.scalar
        def _(act):
            for dst, src in ((xwk_t, "xwk_t"), (xwv_t, "xwv_t"), (xwq_t, "xwq_t"), (cent_t, "cent_t"),
                             (gamma_t, "gamma_t"), (beta_t, "beta_t")):
                act.dma_start(dst[:, :], T[src]).then_inc(s["cross_loaded"], 16)
            for n, src in ((2, "xbq"), (3, "xbk")):
                act.dma_start(bias_cols[:, n:n + 1], T[src].rearrange("(p a) -> p a", a=1)).then_inc(s["cross_loaded"], 16)
            act.dma_start(xbv_rows[:, :], T["xbv"].partition_broadcast(128)).then_inc(s["cross_loaded"], 16)
            act.wait_ge(s["qk_loaded"], N_QK)

            def evacuate(dst, bank, done, count, ready, bias=None):
                act.wait_ge(s[done], count)
                if bias is None:
                    act.activation(dst, bank, ACT.Copy).then_inc(s[ready], 1)
                else:
                    act.activation(dst, bank, ACT.Identity, bias=bias_cols[:, bias:bias + 1]).then_inc(s[ready], 1)

            def exps(g, j, u):
                q = 16 * g + 4 * j + u
                act.wait_ge(s["s2_done"], q + 1)
                if later(g, 1) or q >= 4:
                    act.wait_ge(s["pv_done"], q - 3)
                act.activation(weights[:, u, :], s2_bank[:, (u % 2) * GS:(u % 2 + 1) * GS], ACT.Exp,
                               scale=HEAD_SCALE).then_inc(s["s2_exp"], 1)

            def hmax_out(g, j):
                n, i = G * g + j, j % 2
                if later(n, 2):
                    act.wait_ge(s["s2_done"], 4 * (n - 1))
                evacuate(hmax_t[:, i * 128:(i + 1) * 128], hmax_bank, "hmax_transposed", n + 1, "hmax_t_ready")

            def part0(g, name, parts, bias):
                act.activation(parts[:, 0, :], cross_bank[:, :], ACT.Identity, bias=bias_cols[:, bias:bias + 1])\
                   .then_inc(s[name + "_ready"], 1)

            def part1(g, name, rest, parts):
                act.wait_ge(s[name + "_rest_ready"], g + 1)
                act.activation(parts[:, 1, :], rest[:, :], ACT.Copy).then_inc(s[name + "_part1"], 1)

            def run(g):
                has_f, has_c, has_e, has_s = stages(g)
                e, h = g + 2, g + 3

                def step(n, before, after):
                    scores_first = isinstance(g, int) and g == 0 and n == 0
                    if not scores_first:
                        before()
                    if has_c:
                        exps(g, n // 2, n % 2 * 2)
                        exps(g, n // 2, n % 2 * 2 + 1)
                    if scores_first:
                        before()
                    after()
                    g2, j2 = (g, n // 2 + 1) if n // 2 + 1 < G else (g + 1, 0)
                    if n % 2 == 1 and has_c and not (isinstance(g2, int) and not 0 <= g2 < NG):
                        hmax_out(g2, j2)

                def context():
                    if isinstance(g, int) and g == -2:
                        act.wait_ge(s["cross_loaded"], N_CROSS)
                        act.wait_ge(s["ones_made"], 2)
                    if has_e:
                        evacuate(ctx_t[:, :], cross_bank[:, :], "ctx_transposed", e + 1, "ctx_t_ready")

                def queries_part1():
                    if not isinstance(g, int) or 0 <= e - 1 < NG:
                        part1(e - 1, "xq", rest, xq_parts)

                def keys_and_weights():
                    if not before_cross(g):
                        queries_part1()
                    if has_e:
                        if later(e, 1):
                            act.wait_ge(s["xk_rest_ready"], e)
                            act.wait_ge(s["xk_stored"], 16 * NPART * e)
                        evacuate(xk[:, :], cross_bank[:, :], "xk_done", e + 1, "xk_ready", 3)
                        part0(e, "xk", xk_parts, 3)
                    if not before_cross(g):
                        self_weights()

                def self_weights():
                    if has_e:
                        act.wait_ge(s["neg_max_ready"], e + 1)
                        if later(e, 1):
                            act.wait_ge(s["probs_ready"], G * e)
                        for b in range(G):
                            act.activation(at(expd, b * S, S), at(scores, b * S, S), ACT.Exp, bias=neg_max[:, b:b + 1],
                                           scale=SELF_SCALE).then_inc(s["self_exp"], 1)

                def values():
                    if has_e:
                        if later(e, 4):
                            act.wait_ge(s["pv_done"], 16 * (e - 3))
                        act.wait_ge(s["xv_done"], e + 1)
                        act.activation(at(xv, (e % 4) * G * H * HC, G * H * HC)
                                       .rearrange("p (n c) -> p n c", c=HC)[:, :, 0:HD],
                                       cross_bank[:, :].rearrange("p (n c) -> p n c", c=HD), ACT.Copy)\
                           .then_inc(s["xv_ready"], 1)

                def xn_out():
                    if has_s:
                        evacuate(xn_t[:, :], self_bank[:, :], "xn_transposed", h + 1, "xn_t_ready")

                def queries():
                    if has_s:
                        evacuate(q_t[:, :], self_bank[:, :], "q_done", h + 1, "q_ready", 0)

                def probs_out():
                    if has_e:
                        evacuate(probs_t[:, :], cross_bank[:, :], "probs_transposed", e + 1, "probs_t_ready")
                        part1(e, "xk", rest, xk_parts)

                def self_keys():
                    if has_s:
                        evacuate(k_t[:, :], self_bank[:, :], "k_done", h + 1, "k_ready", 1)

                def scores_out():
                    if has_s:
                        if later(h, 1):
                            act.wait_ge(s["topk_step"], 32 * h)
                            if before_cross(g):
                                act.wait_ge(s["self_exp"], G * h)
                        evacuate(scores[:, :], self_bank[:, :], "scores_done", h + 1, "scores_ready")

                def feats_out():
                    if has_f:
                        evacuate(feats_t[:, :], cross_bank[:, :], "feats_transposed", g, "feats_t_ready")

                def xn2_out():
                    if has_e:
                        evacuate(xn2_t[:, :], cross_bank[:, :], "xn2_transposed", e + 1, "xn2_t_ready")

                def cross_queries():
                    if has_e:
                        if later(e, 1):
                            act.wait_ge(s["xq_rest_ready"], e)
                            act.wait_ge(s["xq_stored"], 16 * NPART * e)
                        evacuate(xq[:, :], cross_bank[:, :], "xq_done", e + 1, "xq_ready", 2)
                        part0(e, "xq", xq_parts, 2)

                def affinity_exp():
                    if has_f:
                        act.wait_ge(s["aff_max_ready"], g)
                        if later(g, 2):
                            act.wait_ge(s["aff_den_ready"], g - 1)
                        act.activation(aff_exp[:, :], aff_max[:, :], ACT.Exp, scale=-1.0).then_inc(s["aff_exp_ready"], 1)

                def nothing():
                    pass

                if before_cross(g):
                    for part in ((context, keys_and_weights, xn_out, self_weights, values, queries, probs_out, self_keys,
                                  scores_out, xn2_out, cross_queries),
                                 (xn_out, context, queries_part1, queries, keys_and_weights, self_keys, self_weights, values, scores_out,
                                  probs_out, xn2_out))[g + 2]:
                        part()
                    if g == -1:
                        hmax_out(0, 0)
                        cross_queries()
                    return
                step(0, context, keys_and_weights)
                step(1, values, xn_out)
                step(2, queries, probs_out)
                step(3, nothing, self_keys)
                step(4, scores_out, feats_out)
                step(5, nothing, nothing)
                step(6, nothing, xn2_out)
                step(7, affinity_exp, cross_queries)

            passes(act, run)
            ffn_scalar(act)

        @block.tensor
        def _(pe):
            def transposed(src, bank, g, ready, count, done):
                pe.wait_ge(s[ready], count)
                for b in range(G):
                    m = pe.transpose(bank[:, b * S:(b + 1) * S], src(b), ident[:, :])
                m.then_inc(s[done], 1)

            def project(bank, w, src, ready, count, done):
                pe.wait_ge(s[ready], count)
                pe.matmul(bank[:, :], w[:, :], src[:, :], start=True, stop=True).then_inc(s[done], 1)

            def stack_at(g, j, h):
                return half(g) * H * GS + h * GS + j * S

            def s1(g, j, u):
                q = 16 * g + 4 * j + u
                if later(g, 1) or q >= 2:
                    pe.wait_ge(s["s1_max"], q - 1)
                if j == 0 and u == 0:
                    pe.wait_ge(s["xq_stacked"], 16 * len(Q_PIECES) * (g + 1))
                    pe.wait_ge(s["xk_stacked"], 16 * len(K_PIECES) * (g + 1))
                if u == 1 and later(G * g + j, 1):
                    pe.wait_ge(s["hmax_t_ready"], G * g + j)
                for i in range(4):
                    o = stack_at(g, j, 4 * u + i)
                    m = pe.matmul(s1_bank[:, (u % 2) * GS + i * S:(u % 2) * GS + (i + 1) * S], at(q_stack, o, S),
                                  at(k_stack, o, S), start=True, stop=True)
                m.then_inc(s["s1_done"], 1)

            def s2(g, j, u):
                q = 16 * g + 4 * j + u
                if later(g, 1) or q >= 2:
                    pe.wait_ge(s["s2_exp"], q - 1)
                if u == 0:
                    pe.wait_ge(s["hmax_t_ready"], G * g + j + 1)
                for i in range(4):
                    o = stack_at(g, j, 4 * u + i)
                    to = s2_bank[:, (u % 2) * GS + i * S:(u % 2) * GS + (i + 1) * S]
                    pe.matmul(to, at(k_stack, o, S), at(q_stack, o, S), start=True, stop=False)
                    m = pe.matmul(to, head_sel[:, u * 4 + i, :], hmax_t[:, (j % 2) * 128:(j % 2 + 1) * 128],
                                  start=False, stop=True)
                m.then_inc(s["s2_done"], 1)

            def hmax_rows(g, j):
                n = G * g + j
                pe.wait_ge(s["hmax_split"], n + 1)
                pe.transpose(hmax_bank, hmax_parts[:, (j % 2) * 128:(j % 2 + 1) * 128], ident_bf[:, :])\
                  .then_inc(s["hmax_transposed"], 1)

            def pv(g, j, u):
                n = G * g + j
                pe.wait_ge(s["s2_exp"], 4 * n + u + 1)
                if u == 0 and later(n, 2):
                    pe.wait_ge(s["attended_ready"], n - 1)
                if u == 0 and j == 0:
                    pe.wait_ge(s["xv_ready"], g + 1)
                if u == 0 and j == 3 and later(g, 1):
                    pe.wait_ge(s["aff_ready"], g)
                for i in range(4):
                    h = u * 4 + i
                    m = pe.matmul(pv_bank[:, (j % 2) * 512 + h * HC:(j % 2) * 512 + (h + 1) * HC],
                                  weights[:, u, i * S:(i + 1) * S],
                                  at(xv, (g % 4) * G * H * HC + (j * H + h) * HC, HC), start=True, stop=True)
                m.then_inc(s["pv_done"], 1)

            def run(g):
                has_f, has_c, has_e, has_s = stages(g)
                e, h, f = g + 2, g + 3, g - 1

                def step(n, before, after):
                    scores_first = isinstance(g, int) and g == 0 and n == 0
                    if not scores_first:
                        before()
                    j, u = n // 2, n % 2 * 2
                    g2, j2 = (g, j + 1) if j + 1 < G else (g + 1, 0)
                    ahead = not isinstance(g2, int) or 0 <= g2 < NG
                    if has_c and u == 0:
                        s2(g, j, u)
                        s2(g, j, u + 1)
                    if scores_first:
                        before()
                    if has_c and ahead:
                        for w in (u, u + 1):
                            s1(g2, j2, w)
                    if has_c and u == 2:
                        s2(g, j, u)
                        s2(g, j, u + 1)
                    after()
                    if has_c:
                        pv(g, j, u)
                    if has_c and ahead and u == 2:
                        hmax_rows(g2, j2)
                    if has_c:
                        pv(g, j, u + 1)

                def context():
                    if isinstance(g, int) and g == -2:
                        pe.wait_ge(s["cross_loaded"], N_CROSS)
                        pe.wait_ge(s["wvo_ready"], 2)
                    if has_e:
                        pe.wait_ge(s["ctx_loaded"], 16 * (e + 1))
                        if later(e, 1):
                            pe.wait_ge(s["xq_ready"], 2 * e)
                        transposed(lambda b: ctx_in[:, b * S:(b + 1) * S], cross_bank, e, "consts_made", 10,
                                   "ctx_transposed")

                def cross_keys():
                    if has_e:
                        project(cross_bank, xwk_t, ctx_t, "ctx_t_ready", e + 1, "xk_done")

                def cross_values():
                    if has_e:
                        pe.wait_ge(s["xk_ready"], 2 * e + 2)
                        for b in range(G):
                            m = pe.matmul(cross_bank[:, b * D:(b + 1) * D], ctx_t[:, b * S:(b + 1) * S], xwv_t[:, :],
                                          start=True, stop=True)
                        m.then_inc(s["xv_done"], 1)

                def xn_rows():
                    if has_s:
                        if later(h, 1):
                            pe.wait_ge(s["v_ready"], h)
                        transposed(lambda b: xn[:, b * S:(b + 1) * S], self_bank, h, "xn_ready", h + 1, "xn_transposed")

                def queries():
                    if has_s:
                        project(self_bank, wq_t, xn_t, "xn_t_ready", h + 1, "q_done")

                def probs_rows():
                    if has_e:
                        pe.wait_ge(s["xv_ready"], e + 1)
                        transposed(lambda b: probs_n[:, b * S:(b + 1) * S], cross_bank, e, "probs_n_ready", G * e + G,
                                   "probs_transposed")

                def attention():
                    if has_e:
                        pe.wait_ge(s["probs_t_ready"], e + 1)
                        pe.wait_ge(s["v_ready"], e + 1)
                        for b in range(G):
                            m = pe.matmul(cross_bank[:, b * D:(b + 1) * D], probs_t[:, b * S:(b + 1) * S],
                                          at(v, half(e) * GS + b * D, D), start=True, stop=True)
                        m.then_inc(s["attn_done"], 1)

                def self_keys():
                    if has_s:
                        pe.wait_ge(s["q_ready"], h + 1)
                        project(self_bank, wk_t, xn_t, "xn_t_ready", h + 1, "k_done")

                def self_scores():
                    if has_s:
                        pe.wait_ge(s["k_ready"], h + 1)
                        for b in range(G):
                            m = pe.matmul(self_bank[:, b * S:(b + 1) * S], q_t[:, b * S:(b + 1) * S],
                                          k_t[:, b * S:(b + 1) * S], start=True, stop=True)
                        m.then_inc(s["scores_done"], 1)

                def feats_rows():
                    if has_f:
                        if has_e:
                            pe.wait_ge(s["x1_ready"], e + 1)
                        if isinstance(g, int) and g == NG - 1:
                            pe.wait_ge(s["xq_ready"], 2 * NG)
                        transposed(lambda b: feats[:, b * S:(b + 1) * S], cross_bank, f, "feats_ready", feats_count(f),
                                   "feats_transposed")

                def self_values():
                    if has_s:
                        pe.wait_ge(s["scores_ready"], h + 1)
                        if isinstance(h, int) and h == 0:
                            pe.wait_ge(s["wvo_ready"], 2)
                        for b in range(G):
                            m = pe.matmul(self_bank[:, b * D:(b + 1) * D], xn_t[:, b * S:(b + 1) * S], wvo_t[:, :],
                                          start=True, stop=True)
                        m.then_inc(s["v_done"], 1)

                def affinities():
                    if has_f:
                        pe.wait_ge(s["feats_t_ready"], f + 1)
                        if has_c:
                            pe.wait_ge(s["attended_ready"], G * g + 2)
                        for b in range(G):
                            m = pe.matmul(pv_bank[:, AFF + b * E:AFF + (b + 1) * E], feats_t[:, b * S:(b + 1) * S],
                                          cent_t[:, :], start=True, stop=True)
                        m.then_inc(s["aff_done"], 1)

                def xn2_rows():
                    if has_e:
                        pe.wait_ge(s["x1_ready"], e + 1)
                        if has_f:
                            pe.wait_ge(s["feats_t_ready"], f + 1)
                        transposed(lambda b: xn2[:, b * S:(b + 1) * S], cross_bank, e, "xn2_ready", e + 1,
                                   "xn2_transposed")

                def cross_queries():
                    if has_e:
                        project(cross_bank, xwq_t, xn2_t, "xn2_t_ready", e + 1, "xq_done")

                def expert_bias(n):
                    if isinstance(g, int) and NG - 2 <= g < NG:
                        expert = (g - (NG - 2)) * (E // 2) + n
                        if expert == 0:
                            pe.wait_ge(s["ffn_loaded"], N_FFN)
                            pe.wait_ge(s["beta_made"], 1)
                        else:
                            pe.wait_ge(s["b1_ready"], expert)
                        for c in range(FC):
                            m = pe.matmul(self_bank[:, c * 128:(c + 1) * 128],
                                          w1[:, expert * F + c * 128:expert * F + (c + 1) * 128],
                                          beta_cols[:, expert * 128:(expert + 1) * 128], start=True, stop=True)
                        m.then_inc(s["b1_done"], 1)

                def nothing():
                    pass

                if before_cross(g):
                    for part in ((context, cross_keys, xn_rows, cross_values, queries, probs_rows, attention, self_keys,
                                  self_scores, xn2_rows, self_values, cross_queries),
                                 (xn_rows, context, queries, cross_keys, self_keys, cross_values, self_scores,
                                  self_values, probs_rows, attention))[g + 2]:
                        part()
                        if g == -2 and part == context:
                            pe.wait_ge(s["sel_made"], 2)
                            pe.wait_ge(s["ones_made"], 2)
                    if g == -1:
                        for u in range(4):
                            s1(0, 0, u)
                        xn2_rows()
                        hmax_rows(0, 0)
                        cross_queries()
                    return
                step(0, context, cross_keys)
                step(1, cross_values, xn_rows)
                if isinstance(g, int) and g == -3:
                    pe.wait_ge(s["vo_loaded"], N_VO)
                    pe.matmul(cross_bank[:, 0:D], wv[:, :], wo_t[:, :], start=True, stop=True)
                    pe.wait_ge(s["bv_made"], 1)
                    pe.matmul(cross_bank[:, D:2 * D], bv_cols[:, :], wo_t[:, :], start=True, stop=True)\
                      .then_inc(s["wvo_done"], 1)
                expert_bias(0)
                step(2, queries, probs_rows)
                step(3, attention, self_keys)
                expert_bias(1)
                step(4, self_scores, feats_rows)
                step(5, self_values, affinities)
                expert_bias(2)
                step(6, nothing, xn2_rows)
                step(7, nothing, cross_queries)
                expert_bias(3)

            pe.wait_ge(s["qk_loaded"], N_QK)
            passes(pe, run)
            ffn_tensor(pe)



_TRANSPOSED = {"wq_t": "L0_attn_Wq", "wk_t": "L0_attn_Wk", "wo_t": "L0_attn_Wo",
               "xwq_t": "L0_xattn_Wq", "xwk_t": "L0_xattn_Wk", "xwv_t": "L0_xattn_Wv",
               "cent_t": "L0_ffn_centroids", "gamma_t": "L0_ffn_gamma", "beta_t": "L0_ffn_beta", "b1_t": "L0_ffn_b1"}
_PLAIN = {"x": "x", "ctx_1024": "ctx_1024", "wv": "L0_attn_Wv", "bq": "L0_attn_bq", "bk": "L0_attn_bk",
          "bv": "L0_attn_bv", "bo": "L0_attn_bo", "xbq": "L0_xattn_bq", "xbk": "L0_xattn_bk", "xbv": "L0_xattn_bv",
          "w1": "L0_ffn_w1", "w2": "L0_ffn_w2", "b2": "L0_ffn_b2"}


def kernel(**inputs):
    import concourse.bacc as bacc
    from concourse.bass_utils import run_bass_kernel_spmd

    nc = bacc.Bacc("TRN2", target_bir_lowering=False, num_devices=1)
    arrays, tensors = {}, {}
    for name, source in list(_PLAIN.items()) + list(_TRANSPOSED.items()):
        a = np.asarray(inputs[source])
        if name == "b1_t":
            a = a.reshape(a.shape[0], -1, 128).reshape(-1, 128)
        a = np.ascontiguousarray(a.T if name in _TRANSPOSED else a)
        arrays[f"in_{name}"] = a
        tensors[name] = nc.dram_tensor(f"in_{name}", a.shape, mybir.dt.from_np(a.dtype), kind="ExternalInput").ap()
    out = nc.dram_tensor("out", tensors["x"].shape, mybir.dt.float32, kind="ExternalOutput").ap()
    preln_decoder_kernel(nc, tensors, out)
    result = run_bass_kernel_spmd(nc, [arrays], core_ids=[0])
    return result.results[0]["out"]
```
